# Optimizing a Trainium2 kernel written in Bass

```python
import numpy as np
import jax
import jax.numpy as jnp

def _softmax(x, axis=-1):
    return jax.nn.softmax(x, axis=axis)

def _gelu(x):
    return jax.nn.gelu(x, approximate=True)

def _silu(x):
    return jax.nn.silu(x)

def _sigmoid(x):
    return jax.nn.sigmoid(x)

def _layernorm(x, axis=-1, eps=1e-05):
    m = jnp.mean(x, axis=axis, keepdims=True)
    v = jnp.var(x, axis=axis, keepdims=True)
    return (x - m) / jnp.sqrt(v + eps)

def _scatter_add(tgt, idx, src, axis=0):
    return tgt.at[idx].add(src)

def _segment_sum(src, seg, n):
    return jax.ops.segment_sum(src, seg, n)
kernel_name = 'mk_gnn_preln_d4_gnn_r64_5db383'

def setup_inputs(seed: int=0):
    np.random.seed(seed)
    _w = jnp.asarray

    def _rec_inputs():
        import jax
        import jax.numpy as jnp
        _gk = jax.random.key(seed)
        x = -0.000202 + 1 * jax.random.normal(jax.random.fold_in(_gk, 1), (100000, 128), jnp.float32)
        src = jax.random.randint(jax.random.fold_in(_gk, 2), (50000,), 0, 100000, jnp.int32)
        dst = jax.random.randint(jax.random.fold_in(_gk, 3), (50000,), 0, 100000, jnp.int32)
        _o = jnp.argsort(dst, stable=True)
        src = src[_o]
        dst = dst[_o]
        edge_attr_4 = -0.000107899 + 1.00008 * jax.random.normal(jax.random.fold_in(_gk, 12), (50000, 4), jnp.float32)
        edge_attr_8 = jax.random.uniform(jax.random.fold_in(_gk, 13), (50000, 8), jnp.float32, 0.0, 1)
        edge_attr_9 = 0.000458729 + 1.00015 * jax.random.normal(jax.random.fold_in(_gk, 14), (50000, 9), jnp.float32)
        return (x, src, dst, edge_attr_4, edge_attr_8, edge_attr_9)
    x, src, dst, edge_attr_4, edge_attr_8, edge_attr_9 = _rec_inputs()

    def _L0_gnn_setup():
        import jax, jax.numpy as jnp
        import numpy as np
        MUL = 32
        N_NODES = 50000
        N_EDGES = 12500
        R3 = np.sqrt(3.0).astype(np.float32)
        key = jax.random.key(seed)
        ks = jax.random.split(key, 12)
        inp = {}
        inp['node_feats'] = jax.random.normal(ks[0], (N_NODES, 4 * MUL), dtype=jnp.float32)
        inp['edge_attrs'] = jax.random.normal(ks[1], (N_EDGES, 4), dtype=jnp.float32)
        inp['edge_feats'] = jax.random.uniform(ks[2], (N_EDGES, 8), dtype=jnp.float32)
        inp['edge_index'] = jax.random.randint(ks[3], (2, N_EDGES), 0, N_NODES)
        inp['W_up_s'] = jax.random.normal(ks[4], (MUL, MUL), dtype=jnp.float32)
        inp['W_up_v'] = jax.random.normal(ks[5], (MUL, MUL), dtype=jnp.float32)
        inp['A1'] = jax.random.normal(ks[6], (8, 64), dtype=jnp.float32) / np.sqrt(8.0)
        inp['b1'] = jnp.zeros((64,), dtype=jnp.float32)
        inp['A2'] = jax.random.normal(ks[7], (64, 64), dtype=jnp.float32) / np.sqrt(64.0)
        inp['b2'] = jnp.zeros((64,), dtype=jnp.float32)
        inp['A3'] = jax.random.normal(ks[8], (64, 4 * MUL), dtype=jnp.float32) * (10.0 * np.sqrt(6.0 / (64 + 4 * MUL)))
        inp['W_out_s'] = jax.random.normal(ks[9], (2 * MUL, MUL), dtype=jnp.float32)
        inp['W_out_v'] = jax.random.normal(ks[10], (2 * MUL, MUL), dtype=jnp.float32)
        return inp
    _L0_gnn_all = _L0_gnn_setup()
    _L0_gnn_in = {k: v for k, v in _L0_gnn_all.items() if k in ('W_up_s', 'W_up_v', 'A1', 'b1', 'A2', 'b2', 'A3', 'W_out_s', 'W_out_v')}
    del _L0_gnn_all

    def _L1_gnn_setup():
        import jax, jax.numpy as jnp
        import numpy as np
        N, E, DIM, H = (50000, 12500, 128, 8)
        HD = DIM // H
        EPS = 1e-05

        def _batch_norm(x, g, b):
            mean = jnp.mean(x, axis=0)
            var = jnp.mean((x - mean) ** 2, axis=0)
            return (x - mean) * jax.lax.rsqrt(var + EPS) * g + b
        key = jax.random.key(seed)
        ks = jax.random.split(key, 12)
        s = 1.0 / np.sqrt(DIM)
        inp = {'h': jax.random.normal(ks[0], (N, DIM), jnp.float32), 'src': jax.random.randint(ks[1], (E,), 0, N, jnp.int32), 'dst': jax.random.randint(ks[2], (E,), 0, N, jnp.int32), 'Wq': jax.random.normal(ks[3], (DIM, DIM), jnp.float32) * s, 'Wk': jax.random.normal(ks[4], (DIM, DIM), jnp.float32) * s, 'Wv': jax.random.normal(ks[5], (DIM, DIM), jnp.float32) * s, 'Wo': jax.random.normal(ks[6], (DIM, DIM), jnp.float32) * s, 'bo': jnp.zeros((DIM,), jnp.float32), 'bn1_g': jnp.ones((DIM,), jnp.float32), 'bn1_b': jnp.zeros((DIM,), jnp.float32), 'bn2_g': jnp.ones((DIM,), jnp.float32), 'bn2_b': jnp.zeros((DIM,), jnp.float32), 'W1': jax.random.normal(ks[7], (DIM, 2 * DIM), jnp.float32) * s, 'b1': jnp.zeros((2 * DIM,), jnp.float32), 'W2': jax.random.normal(ks[8], (2 * DIM, DIM), jnp.float32) * (1.0 / np.sqrt(2 * DIM)), 'b2': jnp.zeros((DIM,), jnp.float32)}
        return inp
    _L1_gnn_all = _L1_gnn_setup()
    _L1_gnn_in = {k: v for k, v in _L1_gnn_all.items() if k in ('Wq', 'Wk', 'Wv', 'Wo', 'bo', 'bn1_g', 'bn1_b', 'bn2_g', 'bn2_b', 'W1', 'b1', 'W2', 'b2')}
    del _L1_gnn_all

    def _L2_gnn_setup():
        import jax, jax.numpy as jnp
        import numpy as np
        from fractions import Fraction
        from math import factorial

        def _su2_cg_coeff(j1, m1, j2, m2, j3, m3):
            if m3 != m1 + m2:
                return 0.0
            vmin = int(max(-j1 + j2 + m3, -j1 + m1, 0))
            vmax = int(min(j2 + j3 + m1, j3 - j1 + j2, j3 + m3))
            f = lambda n: factorial(round(n))
            C = ((2.0 * j3 + 1.0) * Fraction(f(j3 + j1 - j2) * f(j3 - j1 + j2) * f(j1 + j2 - j3) * f(j3 + m3) * f(j3 - m3), f(j1 + j2 + j3 + 1) * f(j1 - m1) * f(j1 + m1) * f(j2 - m2) * f(j2 + m2))) ** 0.5
            S = 0
            for v in range(vmin, vmax + 1):
                S += (-1) ** (v + j2 + m2) * Fraction(f(j2 + j3 + m1 - v) * f(j1 - m1 + v), f(v) * f(j3 - j1 + j2 - v) * f(j3 + m3 - v) * f(v + j1 - j2 - m3))
            return float(C * S)

        def _change_basis_real_to_complex(l):
            q = np.zeros((2 * l + 1, 2 * l + 1), dtype=np.complex128)
            for m in range(-l, 0):
                q[l + m, l + abs(m)] = 1 / np.sqrt(2)
                q[l + m, l - abs(m)] = -1j / np.sqrt(2)
            q[l, l] = 1
            for m in range(1, l + 1):
                q[l + m, l + abs(m)] = (-1) ** m / np.sqrt(2)
                q[l + m, l - abs(m)] = 1j * (-1) ** m / np.sqrt(2)
            return (-1j) ** l * q

        def wigner_3j(l1, l2, l3):
            C = np.zeros((2 * l1 + 1, 2 * l2 + 1, 2 * l3 + 1))
            for m1 in range(-l1, l1 + 1):
                for m2 in range(-l2, l2 + 1):
                    m3 = m1 + m2
                    if abs(m3) <= l3:
                        C[l1 + m1, l2 + m2, l3 + m3] = _su2_cg_coeff(l1, m1, l2, m2, l3, m3)
            Q1 = _change_basis_real_to_complex(l1)
            Q2 = _change_basis_real_to_complex(l2)
            Q3 = _change_basis_real_to_complex(l3)
            Cc = np.einsum('ij,kl,mn,ikn->jlm', Q1, Q2, np.conj(Q3.T), C.astype(np.complex128))
            Cr = np.real(Cc)
            return Cr / np.linalg.norm(Cr)
        MUL = 32
        IRREPS_IN = [(MUL, 0, 1), (MUL, 1, -1)]
        IRREPS_SH = [(1, 0, 1), (1, 1, -1), (1, 2, 1)]
        IRREPS_OUT = [(MUL, 0, 1), (MUL, 1, -1)]
        NUM_NEIGHBORS = 10.0
        N_NODES, N_EDGES = (10000, 100000)

        def _dim(irreps):
            return sum((m * (2 * l + 1) for m, l, _ in irreps))

        def _slices(irreps):
            s, out = (0, [])
            for m, l, _ in irreps:
                d = m * (2 * l + 1)
                out.append((s, s + d))
                s += d
            return out

        def _instructions():
            ins = []
            for i1, (m1, l1, p1) in enumerate(IRREPS_IN):
                for i2, (m2, l2, p2) in enumerate(IRREPS_SH):
                    for io, (mo, lo, po) in enumerate(IRREPS_OUT):
                        if abs(l1 - l2) <= lo <= l1 + l2 and p1 * p2 == po:
                            ins.append((i1, i2, io))
            return ins
        _INSTR = _instructions()
        _SL_IN, _SL_SH, _SL_OUT = (_slices(IRREPS_IN), _slices(IRREPS_SH), _slices(IRREPS_OUT))
        _W3J = [jnp.asarray(wigner_3j(IRREPS_IN[i1][1], IRREPS_SH[i2][1], IRREPS_OUT[io][1]), dtype=jnp.float32) for i1, i2, io in _INSTR]
        _NORM = []
        for _i1, _i2, _io in _INSTR:
            _alpha = 2 * IRREPS_OUT[_io][1] + 1
            _x = sum((IRREPS_IN[j1][0] * IRREPS_SH[j2][0] for j1, j2, jo in _INSTR if jo == _io))
            _NORM.append(float(np.sqrt(_alpha / _x)))

        def _tensor_product(x1, x2, weights):
            E = x1.shape[0]
            out = jnp.zeros((E, _dim(IRREPS_OUT)), dtype=x1.dtype)
            for k, (i1, i2, io) in enumerate(_INSTR):
                m1, l1, _ = IRREPS_IN[i1]
                m2, l2, _ = IRREPS_SH[i2]
                mo, lo, _ = IRREPS_OUT[io]
                a, b = _SL_IN[i1]
                c, d = _SL_SH[i2]
                e, f = _SL_OUT[io]
                x1s = x1[:, a:b].reshape(E, m1, 2 * l1 + 1)
                x2s = x2[:, c:d].reshape(E, m2, 2 * l2 + 1)
                seg = jnp.einsum('uvw,ijk,eui,evj->ewk', weights[k], _W3J[k], x1s, x2s, optimize='optimal') * _NORM[k]
                out = out.at[:, e:f].add(seg.reshape(E, mo * (2 * lo + 1)))
            return out
        key = jax.random.key(seed)
        ks = jax.random.split(key, 8)
        x = jax.random.normal(ks[0], (N_NODES, _dim(IRREPS_IN)), dtype=jnp.float32)
        edge_index = jax.random.randint(ks[1], (2, N_EDGES), 0, N_NODES)
        edge_attr = jax.random.normal(ks[2], (N_EDGES, _dim(IRREPS_SH)), dtype=jnp.float32)
        ws = {f'w{k}': jax.random.normal(ks[3 + k], (MUL, 1, MUL), dtype=jnp.float32) for k in range(len(_INSTR))}
        return {'x': x, 'edge_index': edge_index, 'edge_attr': edge_attr, **ws}
    _L2_gnn_all = _L2_gnn_setup()
    _L2_gnn_in = {k: v for k, v in _L2_gnn_all.items() if k in ('w0', 'w1', 'w2', 'w3', 'w4')}
    del _L2_gnn_all

    def _L3_gnn_setup():
        import jax, jax.numpy as jnp
        import numpy as np
        N = 50000
        F_IN = 128
        H = 4
        C = 32
        NEG_SLOPE = 0.2

        def _gat_forward(x, W, att_src, att_dst, bias, edge_index):
            n = x.shape[0]
            xp = (x @ W.T).reshape(n, H, C)
            loop = jnp.arange(n, dtype=edge_index.dtype)
            src = jnp.concatenate([edge_index[0], loop])
            dst = jnp.concatenate([edge_index[1], loop])
            a_src = (xp * att_src).sum(-1)
            a_dst = (xp * att_dst).sum(-1)
            logits = jax.nn.leaky_relu(a_src[src] + a_dst[dst], negative_slope=NEG_SLOPE)
            seg_max = jax.ops.segment_max(logits, dst, num_segments=n)
            seg_max = jnp.where(jnp.isfinite(seg_max), seg_max, 0.0)
            e = jnp.exp(logits - seg_max[dst])
            denom = jax.ops.segment_sum(e, dst, num_segments=n)
            alpha = e / (denom[dst] + 1e-16)
            msg = xp[src] * alpha[:, :, None]
            out = jax.ops.segment_sum(msg, dst, num_segments=n)
            out = out.reshape(n, H * C) + bias
            return jax.nn.elu(out)
        key = jax.random.key(seed)
        k1, k2, k3, k4, k5, k6 = jax.random.split(key, 6)
        x = jax.random.normal(k1, (N, F_IN), dtype=jnp.float32)
        edge_index = jax.random.randint(k2, (2, 12500), 0, N, dtype=jnp.int32)
        W = jax.random.normal(k3, (H * C, F_IN), dtype=jnp.float32) * (1.0 / np.sqrt(F_IN))
        att_src = jax.random.normal(k4, (1, H, C), dtype=jnp.float32) * (1.0 / np.sqrt(C))
        att_dst = jax.random.normal(k5, (1, H, C), dtype=jnp.float32) * (1.0 / np.sqrt(C))
        bias = jax.random.normal(k6, (H * C,), dtype=jnp.float32) * 0.01
        return {'x': x, 'W': W, 'att_src': att_src, 'att_dst': att_dst, 'bias': bias, 'edge_index': edge_index}
    _L3_gnn_all = _L3_gnn_setup()
    _L3_gnn_in = {k: v for k, v in _L3_gnn_all.items() if k in ('W', 'att_src', 'att_dst', 'bias')}
    del _L3_gnn_all
    return {'x': x, 'src': src, 'dst': dst, 'edge_attr_4': edge_attr_4, 'edge_attr_8': edge_attr_8, 'edge_attr_9': edge_attr_9, 'L0_gnn_W_up_s': _L0_gnn_in['W_up_s'], 'L0_gnn_W_up_v': _L0_gnn_in['W_up_v'], 'L0_gnn_A1': _L0_gnn_in['A1'], 'L0_gnn_b1': _L0_gnn_in['b1'], 'L0_gnn_A2': _L0_gnn_in['A2'], 'L0_gnn_b2': _L0_gnn_in['b2'], 'L0_gnn_A3': _L0_gnn_in['A3'], 'L0_gnn_W_out_s': _L0_gnn_in['W_out_s'], 'L0_gnn_W_out_v': _L0_gnn_in['W_out_v'], 'L1_gnn_Wq': _L1_gnn_in['Wq'], 'L1_gnn_Wk': _L1_gnn_in['Wk'], 'L1_gnn_Wv': _L1_gnn_in['Wv'], 'L1_gnn_Wo': _L1_gnn_in['Wo'], 'L1_gnn_bo': _L1_gnn_in['bo'], 'L1_gnn_bn1_g': _L1_gnn_in['bn1_g'], 'L1_gnn_bn1_b': _L1_gnn_in['bn1_b'], 'L1_gnn_bn2_g': _L1_gnn_in['bn2_g'], 'L1_gnn_bn2_b': _L1_gnn_in['bn2_b'], 'L1_gnn_W1': _L1_gnn_in['W1'], 'L1_gnn_b1': _L1_gnn_in['b1'], 'L1_gnn_W2': _L1_gnn_in['W2'], 'L1_gnn_b2': _L1_gnn_in['b2'], 'L2_gnn_w0': _L2_gnn_in['w0'], 'L2_gnn_w1': _L2_gnn_in['w1'], 'L2_gnn_w2': _L2_gnn_in['w2'], 'L2_gnn_w3': _L2_gnn_in['w3'], 'L2_gnn_w4': _L2_gnn_in['w4'], 'L3_gnn_W': _L3_gnn_in['W'], 'L3_gnn_att_src': _L3_gnn_in['att_src'], 'L3_gnn_att_dst': _L3_gnn_in['att_dst'], 'L3_gnn_bias': _L3_gnn_in['bias']}

def reference(x, src, dst, edge_attr_4, edge_attr_8, edge_attr_9, L0_gnn_W_up_s, L0_gnn_W_up_v, L0_gnn_A1, L0_gnn_b1, L0_gnn_A2, L0_gnn_b2, L0_gnn_A3, L0_gnn_W_out_s, L0_gnn_W_out_v, L1_gnn_Wq, L1_gnn_Wk, L1_gnn_Wv, L1_gnn_Wo, L1_gnn_bo, L1_gnn_bn1_g, L1_gnn_bn1_b, L1_gnn_bn2_g, L1_gnn_bn2_b, L1_gnn_W1, L1_gnn_b1, L1_gnn_W2, L1_gnn_b2, L2_gnn_w0, L2_gnn_w1, L2_gnn_w2, L2_gnn_w3, L2_gnn_w4, L3_gnn_W, L3_gnn_att_src, L3_gnn_att_dst, L3_gnn_bias):
    import jax
    import jax.numpy as jnp

    def _L0_gnn_ref(node_feats, edge_attrs, edge_feats, W_up_s, W_up_v, A1, b1, A2, b2, A3, W_out_s, W_out_v, edge_index):
        import jax, jax.numpy as jnp
        import numpy as np
        MUL = 32
        N_NODES = 50000
        N_EDGES = 12500
        R3 = np.sqrt(3.0).astype(np.float32)
        num_nodes = node_feats.shape[0]
        sender, receiver = (edge_index[0], edge_index[1])
        s = node_feats[:, :MUL]
        v = node_feats[:, MUL:].reshape(num_nodes, MUL, 3)
        inv = 1.0 / np.sqrt(MUL).astype(np.float32)
        s = s @ W_up_s * inv
        v = jnp.einsum('nui,uw->nwi', v, W_up_v) * inv
        h = jax.nn.silu(edge_feats @ A1 + b1)
        h = jax.nn.silu(h @ A2 + b2)
        tpw = h @ A3
        w0, w1, w2, w3 = jnp.split(tpw, 4, axis=1)
        ss = s[sender]
        vs = v[sender]
        y_s = edge_attrs[:, :1]
        y_v = edge_attrs[:, 1:4]
        out_s0 = ss * y_s * w0
        out_s3 = jnp.einsum('eui,ei->eu', vs, y_v) / R3 * w3
        out_v1 = ss[:, :, None] * y_v[:, None, :] * w1[:, :, None]
        out_v2 = vs * y_s[:, :, None] * w2[:, :, None]
        E = ss.shape[0]
        mji = jnp.concatenate([out_s0, out_s3, out_v1.reshape(E, 3 * MUL), out_v2.reshape(E, 3 * MUL)], axis=1)
        message = jax.ops.segment_sum(mji, receiver, num_segments=num_nodes) / 10.0
        ms = message[:, :2 * MUL]
        mv = message[:, 2 * MUL:].reshape(num_nodes, 2 * MUL, 3)
        inv2 = 1.0 / np.sqrt(2 * MUL).astype(np.float32)
        out_s = ms @ W_out_s * inv2
        out_v = jnp.einsum('nui,uw->nwi', mv, W_out_v) * inv2
        return jnp.concatenate([out_s, out_v.reshape(num_nodes, 3 * MUL)], axis=1)

    def _L1_gnn_ref(h, src, dst, Wq, Wk, Wv, Wo, bo, bn1_g, bn1_b, bn2_g, bn2_b, W1, b1, W2, b2):
        import jax, jax.numpy as jnp
        import numpy as np
        N, E, DIM, H = (50000, 12500, 128, 8)
        HD = DIM // H
        EPS = 1e-05

        def _batch_norm(x, g, b):
            mean = jnp.mean(x, axis=0)
            var = jnp.mean((x - mean) ** 2, axis=0)
            return (x - mean) * jax.lax.rsqrt(var + EPS) * g + b
        n = h.shape[0]
        h_in1 = h
        hn = _batch_norm(h, bn1_g, bn1_b)
        Q = (hn @ Wq).reshape(n, H, HD)
        K = (hn @ Wk).reshape(n, H, HD)
        V = (hn @ Wv).reshape(n, H, HD)
        score = jnp.einsum('ehd,ehd->eh', K[src], Q[dst]) / np.sqrt(HD)
        score = jnp.clip(score, -5.0, 5.0)
        smax = jax.ops.segment_max(score, dst, num_segments=n)
        a = jnp.exp(score - smax[dst])
        asum = jax.ops.segment_sum(a, dst, num_segments=n)
        a = a / asum[dst]
        m = V[src] * a[:, :, None]
        wV = jax.ops.segment_sum(m, dst, num_segments=n).reshape(n, DIM)
        h2 = wV @ Wo + bo
        h2 = h_in1 + h2
        h_in2 = h2
        h3 = _batch_norm(h2, bn2_g, bn2_b)
        h3 = jax.nn.relu(h3 @ W1 + b1) @ W2 + b2
        return h_in2 + h3

    def _L2_gnn_ref(x, edge_index, edge_attr, w0, w1, w2, w3, w4):
        import jax, jax.numpy as jnp
        import numpy as np
        from fractions import Fraction
        from math import factorial

        def _su2_cg_coeff(j1, m1, j2, m2, j3, m3):
            if m3 != m1 + m2:
                return 0.0
            vmin = int(max(-j1 + j2 + m3, -j1 + m1, 0))
            vmax = int(min(j2 + j3 + m1, j3 - j1 + j2, j3 + m3))
            f = lambda n: factorial(round(n))
            C = ((2.0 * j3 + 1.0) * Fraction(f(j3 + j1 - j2) * f(j3 - j1 + j2) * f(j1 + j2 - j3) * f(j3 + m3) * f(j3 - m3), f(j1 + j2 + j3 + 1) * f(j1 - m1) * f(j1 + m1) * f(j2 - m2) * f(j2 + m2))) ** 0.5
            S = 0
            for v in range(vmin, vmax + 1):
                S += (-1) ** (v + j2 + m2) * Fraction(f(j2 + j3 + m1 - v) * f(j1 - m1 + v), f(v) * f(j3 - j1 + j2 - v) * f(j3 + m3 - v) * f(v + j1 - j2 - m3))
            return float(C * S)

        def _change_basis_real_to_complex(l):
            q = np.zeros((2 * l + 1, 2 * l + 1), dtype=np.complex128)
            for m in range(-l, 0):
                q[l + m, l + abs(m)] = 1 / np.sqrt(2)
                q[l + m, l - abs(m)] = -1j / np.sqrt(2)
            q[l, l] = 1
            for m in range(1, l + 1):
                q[l + m, l + abs(m)] = (-1) ** m / np.sqrt(2)
                q[l + m, l - abs(m)] = 1j * (-1) ** m / np.sqrt(2)
            return (-1j) ** l * q

        def wigner_3j(l1, l2, l3):
            C = np.zeros((2 * l1 + 1, 2 * l2 + 1, 2 * l3 + 1))
            for m1 in range(-l1, l1 + 1):
                for m2 in range(-l2, l2 + 1):
                    m3 = m1 + m2
                    if abs(m3) <= l3:
                        C[l1 + m1, l2 + m2, l3 + m3] = _su2_cg_coeff(l1, m1, l2, m2, l3, m3)
            Q1 = _change_basis_real_to_complex(l1)
            Q2 = _change_basis_real_to_complex(l2)
            Q3 = _change_basis_real_to_complex(l3)
            Cc = np.einsum('ij,kl,mn,ikn->jlm', Q1, Q2, np.conj(Q3.T), C.astype(np.complex128))
            Cr = np.real(Cc)
            return Cr / np.linalg.norm(Cr)
        MUL = 32
        IRREPS_IN = [(MUL, 0, 1), (MUL, 1, -1)]
        IRREPS_SH = [(1, 0, 1), (1, 1, -1), (1, 2, 1)]
        IRREPS_OUT = [(MUL, 0, 1), (MUL, 1, -1)]
        NUM_NEIGHBORS = 10.0
        N_NODES, N_EDGES = (10000, 100000)

        def _dim(irreps):
            return sum((m * (2 * l + 1) for m, l, _ in irreps))

        def _slices(irreps):
            s, out = (0, [])
            for m, l, _ in irreps:
                d = m * (2 * l + 1)
                out.append((s, s + d))
                s += d
            return out

        def _instructions():
            ins = []
            for i1, (m1, l1, p1) in enumerate(IRREPS_IN):
                for i2, (m2, l2, p2) in enumerate(IRREPS_SH):
                    for io, (mo, lo, po) in enumerate(IRREPS_OUT):
                        if abs(l1 - l2) <= lo <= l1 + l2 and p1 * p2 == po:
                            ins.append((i1, i2, io))
            return ins
        _INSTR = _instructions()
        _SL_IN, _SL_SH, _SL_OUT = (_slices(IRREPS_IN), _slices(IRREPS_SH), _slices(IRREPS_OUT))
        _W3J = [jnp.asarray(wigner_3j(IRREPS_IN[i1][1], IRREPS_SH[i2][1], IRREPS_OUT[io][1]), dtype=jnp.float32) for i1, i2, io in _INSTR]
        _NORM = []
        for _i1, _i2, _io in _INSTR:
            _alpha = 2 * IRREPS_OUT[_io][1] + 1
            _x = sum((IRREPS_IN[j1][0] * IRREPS_SH[j2][0] for j1, j2, jo in _INSTR if jo == _io))
            _NORM.append(float(np.sqrt(_alpha / _x)))

        def _tensor_product(x1, x2, weights):
            E = x1.shape[0]
            out = jnp.zeros((E, _dim(IRREPS_OUT)), dtype=x1.dtype)
            for k, (i1, i2, io) in enumerate(_INSTR):
                m1, l1, _ = IRREPS_IN[i1]
                m2, l2, _ = IRREPS_SH[i2]
                mo, lo, _ = IRREPS_OUT[io]
                a, b = _SL_IN[i1]
                c, d = _SL_SH[i2]
                e, f = _SL_OUT[io]
                x1s = x1[:, a:b].reshape(E, m1, 2 * l1 + 1)
                x2s = x2[:, c:d].reshape(E, m2, 2 * l2 + 1)
                seg = jnp.einsum('uvw,ijk,eui,evj->ewk', weights[k], _W3J[k], x1s, x2s, optimize='optimal') * _NORM[k]
                out = out.at[:, e:f].add(seg.reshape(E, mo * (2 * lo + 1)))
            return out
        i, j = (edge_index[0], edge_index[1])
        summand = _tensor_product(x[i], edge_attr, [w0, w1, w2, w3, w4])
        out = jax.ops.segment_sum(summand, j, num_segments=x.shape[0])
        return out / float(np.sqrt(NUM_NEIGHBORS))

    def _L3_gnn_ref(x, W, att_src, att_dst, bias, edge_index):
        import jax, jax.numpy as jnp
        import numpy as np
        N = 50000
        F_IN = 128
        H = 4
        C = 32
        NEG_SLOPE = 0.2

        def _gat_forward(x, W, att_src, att_dst, bias, edge_index):
            n = x.shape[0]
            xp = (x @ W.T).reshape(n, H, C)
            loop = jnp.arange(n, dtype=edge_index.dtype)
            src = jnp.concatenate([edge_index[0], loop])
            dst = jnp.concatenate([edge_index[1], loop])
            a_src = (xp * att_src).sum(-1)
            a_dst = (xp * att_dst).sum(-1)
            logits = jax.nn.leaky_relu(a_src[src] + a_dst[dst], negative_slope=NEG_SLOPE)
            seg_max = jax.ops.segment_max(logits, dst, num_segments=n)
            seg_max = jnp.where(jnp.isfinite(seg_max), seg_max, 0.0)
            e = jnp.exp(logits - seg_max[dst])
            denom = jax.ops.segment_sum(e, dst, num_segments=n)
            alpha = e / (denom[dst] + 1e-16)
            msg = xp[src] * alpha[:, :, None]
            out = jax.ops.segment_sum(msg, dst, num_segments=n)
            out = out.reshape(n, H * C) + bias
            return jax.nn.elu(out)
        return _gat_forward(x, W, att_src, att_dst, bias, edge_index)
    edge_index = jnp.stack([src, dst])
    h = jnp.maximum(_layernorm(x, axis=-1), 0.0)
    x = x + _L0_gnn_ref(h, edge_attr_4, edge_attr_8, L0_gnn_W_up_s, L0_gnn_W_up_v, L0_gnn_A1, L0_gnn_b1, L0_gnn_A2, L0_gnn_b2, L0_gnn_A3, L0_gnn_W_out_s, L0_gnn_W_out_v, edge_index)
    h = jnp.maximum(_layernorm(x, axis=-1), 0.0)
    x = x + _L1_gnn_ref(h, src, dst, L1_gnn_Wq, L1_gnn_Wk, L1_gnn_Wv, L1_gnn_Wo, L1_gnn_bo, L1_gnn_bn1_g, L1_gnn_bn1_b, L1_gnn_bn2_g, L1_gnn_bn2_b, L1_gnn_W1, L1_gnn_b1, L1_gnn_W2, L1_gnn_b2)
    h = jnp.maximum(_layernorm(x, axis=-1), 0.0)
    x = x + _L2_gnn_ref(h, edge_index, edge_attr_9, L2_gnn_w0, L2_gnn_w1, L2_gnn_w2, L2_gnn_w3, L2_gnn_w4)
    h = jnp.maximum(_layernorm(x, axis=-1), 0.0)
    x = x + _L3_gnn_ref(h, L3_gnn_W, L3_gnn_att_src, L3_gnn_att_dst, L3_gnn_bias, edge_index)
    return x

_drawn_inputs = setup_inputs


def setup_inputs(seed=0):
    import zlib

    import numpy as np

    out = dict(_drawn_inputs(seed))
    spreads = {'L0_gnn_b1': (0.0, 0.352),
     'L0_gnn_b2': (0.0, 0.1),
     'L1_gnn_bo': (0.0, 0.1),
     'L1_gnn_bn1_g': (1.0, 0.2),
     'L1_gnn_bn1_b': (0.0, 0.1),
     'L1_gnn_bn2_g': (1.0, 0.2),
     'L1_gnn_bn2_b': (0.0, 0.1),
     'L1_gnn_b1': (0.0, 0.1),
     'L1_gnn_b2': (0.0, 0.1)}
    factors = {'L3_gnn_att_dst': 4.928, 'L3_gnn_bias': 8.0}
    for name, (base, spread) in spreads.items():
        noise = np.random.default_rng([zlib.crc32(name.encode()), seed]).standard_normal(out[name].shape)
        drawn = base * np.exp(spread * noise) if base else spread * noise
        out[name] = jnp.asarray(drawn.astype(out[name].dtype))
    for name, factor in factors.items():
        out[name] = (out[name] * factor).astype(out[name].dtype)
    return out
```

```python
import math
from contextlib import ExitStack
from functools import partial

import numpy as np

import concourse.bass as bass
from concourse import mybir

F32, I32, U8 = mybir.dt.float32, mybir.dt.int32, mybir.dt.uint8
ALU = mybir.AluOpType
ACT = mybir.ActivationFunctionType

N = 100000
E = 50000
D = 128
P = 128
G = 4
BLK = P * G
EB = -(-E // BLK)
EP = EB * BLK
NB = -(-N // BLK)
RING = 4
NEW = N - (NB - 1) * BLK
SPARE = 4
TRASH = 1 + SPARE * BLK
NT = N + TRASH
MUL = 32
HEADS1, HEADS3 = 8, 4
EPS = 1e-5
NEG = 1e30
LN_EXP = "natural_log_exp_and_others"
COEF = 17


def wigner_3j(l1, l2, l3):

    def f(n):
        return math.factorial(round(n))

    def su2(m1, m2, m3):
        vmin = int(max(-l1 + l2 + m3, -l1 + m1, 0))
        vmax = int(min(l2 + l3 + m1, l3 - l1 + l2, l3 + m3))
        c = ((2.0 * l3 + 1.0) * (
            f(l3 + l1 - l2) * f(l3 - l1 + l2) * f(l1 + l2 - l3) * f(l3 + m3) * f(l3 - m3) / (
            f(l1 + l2 + l3 + 1) * f(l1 - m1) * f(l1 + m1) * f(l2 - m2) * f(l2 + m2)))) ** 0.5
        s = 0
        for v in range(vmin, vmax + 1):
            s += (-1) ** (v + l2 + m2) * f(l2 + l3 + m1 - v) * f(l1 - m1 + v) / (
                f(v) * f(l3 - l1 + l2 - v) * f(l3 + m3 - v) * f(v + l1 - l2 - m3))
        return float(c * s)

    def real(l):
        q = np.zeros((2 * l + 1, 2 * l + 1), np.complex128)
        for m in range(-l, 0):
            q[l + m, l + abs(m)] = 1 / np.sqrt(2)
            q[l + m, l - abs(m)] = -1j / np.sqrt(2)
        q[l, l] = 1
        for m in range(1, l + 1):
            q[l + m, l + abs(m)] = (-1) ** m / np.sqrt(2)
            q[l + m, l - abs(m)] = 1j * (-1) ** m / np.sqrt(2)
        return (-1j) ** l * q

    c = np.zeros((2 * l1 + 1, 2 * l2 + 1, 2 * l3 + 1))
    for m1 in range(-l1, l1 + 1):
        for m2 in range(-l2, l2 + 1):
            if abs(m1 + m2) <= l3:
                c[l1 + m1, l2 + m2, l3 + m1 + m2] = su2(m1, m2, m1 + m2)
    r = np.real(np.einsum("ij,kl,mn,ikn->jlm", real(l1), real(l2), np.conj(real(l3).T), c.astype(np.complex128)))
    return r / np.linalg.norm(r)


def coefficient_matrix():
    n0, n1 = np.sqrt(1.0 / (2 * MUL)), np.sqrt(3.0 / (3 * MUL))
    down = 1.0 / np.sqrt(10.0)
    c = np.zeros((9, COEF))
    c[0, 0] = wigner_3j(0, 0, 0)[0, 0, 0] * n0
    c[1:4, 1:4] = wigner_3j(1, 1, 0)[:, :, 0].T * n0
    c[1:4, 4:7] = wigner_3j(0, 1, 1)[0] * n1
    keep = wigner_3j(1, 0, 1)[:, 0, :]
    assert np.allclose(keep, keep[0, 0] * np.eye(3))
    c[0, 7] = keep[0, 0] * n1
    c[4:9, 8:17] = wigner_3j(1, 2, 1).transpose(1, 0, 2).reshape(5, 9) * n1
    return (c * down).astype(np.float32)


def shape_constants():
    p = np.arange(P)
    h16, h32 = D // HEADS1, D // HEADS3
    blocks16 = (p[:, None] // h16 == p[None] // h16) / np.sqrt(h16)
    blocks32 = p[:, None] // h32 == p[None] // h32
    return np.concatenate([np.eye(P), blocks16, blocks32], 1).astype(np.float32)


def trash_rows():
    b, p, g = np.ogrid[:EB, :P, :G]
    return (N + 1 + b % SPARE * BLK + p * G + g).transpose(1, 0, 2).reshape(P, EB * G).astype(np.float32)


class Blk:

    def __init__(self, turn, at):
        self.turn, self.at = turn, at
        self.num = at if turn is None else turn * RING + at

    def back(self, n):
        return Blk(self.turn, self.at - n)


class Ring(list):

    def __getitem__(self, b):
        return list.__getitem__(self, (b.at if isinstance(b, Blk) else b) % len(self))


def this(sem, b, per=1):
    if isinstance(sem, Ring):
        turns = b.at // RING + 1
        return sem[b], turns * per if b.turn is None else b.turn * per + turns * per
    return sem, (b.at + 1) * per if b.turn is None else b.turn * (RING * per) + (b.at + 1) * per


def before(sem, b, n, per=1):
    return this(sem, b.back(n), per)


def wait_freed(eng, sem, count):
    if isinstance(count, int) and count <= 0:
        return
    eng.wait_ge(sem, count)


def wait_all(eng, ring, blocks, per):
    for c in range(RING):
        eng.wait_ge(ring[c], len(range(c, blocks, RING)) * per)


def pipeline(eng, blocks, stages):
    ahead = min(lag for lag, _ in stages)
    deepest = max(lag for lag, _ in stages) - ahead

    def step(turn, n):
        for lag, work in stages:
            at = n - lag + ahead
            if turn is not None or 0 <= at < blocks:
                work(Blk(turn, at))

    first, end = -(-(deepest + RING) // RING), (blocks - 1) // RING
    for n in range(first * RING):
        step(None, n)
    with eng.Fori(first, end) as turn:
        for n in range(RING):
            step(turn, n)
    for n in range(end * RING, blocks + deepest):
        step(None, n)


class Phase:

    def __init__(self, nc, name):
        self.nc, self.name, self.ctx, self.sems = nc, name, ExitStack(), []

    def __enter__(self):
        return self

    def __exit__(self, *exc):
        if exc[0] is None:
            self.nc.clear_and_free_semaphores(self.sems)
            self.nc.all_engine_barrier()
            self.ctx.close()

    def sem(self, name):
        self.sems.append(self.nc.alloc_semaphore(f"{self.name}_{name}"))
        return self.sems[-1]

    def dma(self, name):
        return Ring(self.sem(f"{name}{c}") for c in range(RING))

    def sb(self, name, shape, dt=F32):
        return self.ctx.enter_context(self.nc.sbuf_tensor(f"{self.name}_{name}", shape, dt))

    def ring(self, name, shape, dt=F32, depth=4):
        return Ring(self.sb(f"{name}{c}", shape, dt) for c in range(depth))

    def ps(self, name):
        return self.ctx.enter_context(self.nc.psum_tensor(f"{self.name}_{name}", [P, BLK], F32))

    def ps_ring(self, name, depth=2):
        return Ring(self.ps(f"{name}{c}") for c in range(depth))

    def block(self):
        return self.nc.Block()


def edge_rows(table, b):
    return table[bass.ds(b.num * BLK, BLK), :].rearrange("(p g) c -> p g c", g=G)


def node_rows(table, b):
    at = b.num * BLK
    if isinstance(at, int) and at + BLK > N:
        at = N - BLK
    return table[bass.ds(at, BLK), :].rearrange("(p g) c -> p g c", g=G)


def is_last_node_block(b):
    return b.turn is None and b.at == NB - 1


def grouped(t):
    return t.rearrange("p (g c) -> p g c", g=G)


class Norm:

    def __init__(self, ph, k, name, raw, raw_ready, ready_per, eps, h_free, depth=RING):
        self.k, self.raw, self.raw_ready, self.per, self.eps, self.h_free, self.depth = k, raw, raw_ready, ready_per, eps, h_free, depth
        self.stats = ph.ring(f"{name}_stats", [P, G, 6])
        self.mv = ph.ring(f"{name}_mv", [P, G, 2])
        self.ln = ph.ring(f"{name}_ln", [P, G, 1])
        self.rstd = ph.ring(f"{name}_rstd", [P, G, 1])
        self.shift = ph.ring(f"{name}_shift", [P, G, 1])
        self.h = ph.ring(f"{name}_h", [P, G, D], depth=depth)
        self.s_turn = ph.sem(f"{name}_vector_goes_on")
        self.s_stats = ph.sem(f"{name}_stats_done")
        self.s_mv = ph.sem(f"{name}_mean_var_done")
        self.s_ln = ph.sem(f"{name}_log_done")
        self.s_rstd = ph.sem(f"{name}_rstd_done")
        self.s_shift = ph.sem(f"{name}_shift_done")
        self.s_h = ph.sem(f"{name}_h_done")

    def vector_stats(self, dve, b):
        if self.raw_ready is not None:
            dve.wait_ge(*this(self.raw_ready, b, self.per))
        for g in range(G):
            last = dve.bn_stats(self.stats[b][:, g, :], self.raw[b][:, g, :])
        last.then_inc(self.s_stats, 1)
        dve.wait_ge(*this(self.s_stats, b))
        wait_freed(dve, *before(self.s_h, b, RING))
        dve.sem_inc(self.s_turn, 1)
        for g in range(G):
            last = dve.bn_aggr(self.mv[b][:, g, :], self.stats[b][:, g, :])
        last.then_inc(self.s_mv, 1)

    def scalar_rstd(self, act, b):
        act.wait_ge(*this(self.s_mv, b))
        act.activation(self.ln[b][:, :, :], self.mv[b][:, :, 1:2], ACT.Ln, bias=self.eps).then_inc(self.s_ln, 1)
        act.wait_ge(*this(self.s_ln, b))
        act.activation(self.rstd[b][:, :, :], self.ln[b][:, :, :], ACT.Exp, scale=-0.5).then_inc(self.s_rstd, 1)

    def vector_shift(self, dve, b):
        dve.wait_ge(*this(self.s_rstd, b))
        dve.scalar_tensor_tensor(self.shift[b][:, :, 0], self.mv[b][:, :, 0], -1.0, self.rstd[b][:, :, 0],
                                 ALU.mult, ALU.mult).then_inc(self.s_shift, 1)

    def scalar_relu(self, act, b):
        act.wait_ge(*this(self.s_shift, b))
        wait_freed(act, *before(self.h_free, b, self.depth))
        for g in range(G):
            last = act.activation(self.h[b][:, g, :], self.raw[b][:, g, :], ACT.Relu,
                                  bias=self.shift[b][:, g, :], scale=self.rstd[b][:, g, :])
        last.then_inc(self.s_h, 1)


def transpose_rows(pe, out, rows, ident, in_order):
    for g in range(G):
        o = out[:, g:BLK:G] if in_order else out[:, g * P:(g + 1) * P]
        last = pe.transpose(o, rows[:, g, :], ident)
    return last


def transpose_back(pe, out, cols, ident):
    for g in range(G):
        last = pe.transpose(out[:, g * P:(g + 1) * P], cols[:, g:BLK:G], ident)
    return last


def indexed_gather(pool, out, table, index, landed, rows):
    for g in range(G):
        pool.indirect_dma_start(out[:, g, :], None, table, bass.IndirectOffsetOnAxis(ap=index[:, g:g + 1], axis=0),
                                bounds_check=rows - 1, oob_is_err=False).then_inc(landed, 16)


def indexed_add(pool, table, index, rows, landed):
    for g in range(G):
        pool.indirect_dma_start(table, bass.IndirectOffsetOnAxis(ap=index[:, g:g + 1], axis=0), rows[:, g, :], None,
                                compute_op=ALU.add).then_inc(landed, 16)


def indexed_write(pool, table, index, rows, landed, bound):
    for g in range(G):
        pool.indirect_dma_start(table, bass.IndirectOffsetOnAxis(ap=index[:, g:g + 1], axis=0), rows[:, g, :], None,
                                bounds_check=bound, oob_is_err=False).then_inc(landed, 16)


def bc(ap, axis, n):
    a = ap.unsqueeze(axis)
    shape = list(a.shape)
    shape[axis] = n
    return a.to_broadcast(shape)


def setup(nc, t, k):
    with Phase(nc, "setup") as ph:
        MB = 7 * BLK
        assert EP % MB == 0
        dst_all = ph.ring("dst_all", [P, MB + 1], I32, 2)
        rows = ph.sb("rows", [P, 3, EB, G], I32)
        inner = ph.sb("inner", [P, EB, G])
        away, trash = ph.sb("away", [P, EB, G]), ph.sb("trash", [P, EB, G])
        table = ph.sb("table", [P, EB, 3, G], I32)
        zeros = ph.sb("zeros", [P, SPARE * G * D])
        a1, a2, a3 = ph.sb("a1", [8, 64]), ph.sb("a2", [64, 64]), ph.sb("a3", [64, D])
        b1, b2 = ph.sb("b1", [64, 1]), ph.sb("b2", [64, 1])
        ef = ph.ring("ef", [8, BLK])
        m1 = ph.ring("m1", [64, BLK])
        m2 = ph.ring("m2", [64, BLK])
        tp = ph.ring("tp", [P, G, D])
        p1 = ph.ps_ring("p1")
        p2 = ph.ps_ring("p2")
        p3 = ph.ps_ring("p3")
        s_const, s_rows, s_w = ph.sem("constants_loaded"), ph.sem("rows_loaded"), ph.sem("mlp_weights_loaded")
        s_zero, s_z0, s_copy = ph.sem("zeros_made"), ph.sem("trash_cleared"), ph.sem("x_copied")
        s_inner, s_table, s_tabled = ph.sem("index_steps"), ph.sem("index_table_made"), ph.sem("index_table_stored")
        s_dst, s_mask = ph.dma("dst_loaded"), ph.sem("mask_made")
        s_ef, s_p1, s_m1 = ph.dma("edge_feats_loaded"), ph.sem("mlp1_done"), ph.sem("silu1_done")
        s_p2, s_m2, s_p3 = ph.sem("mlp2_done"), ph.sem("silu2_done"), ph.sem("mlp3_done")
        s_tp, s_tps = ph.sem("tpw_ready"), ph.dma("tpw_stored")
        s_turn = ph.sem("tensor_goes_on")
        COPIES = EP // MB

        with ph.block() as block:
            @block.sync
            def _(sp):
                for dst, src in ((a1[:, :], t["A1"]), (a2[:, :], t["A2"]), (a3[:, :], t["A3"]),
                                 (b1[:, :], t["b1_0"].rearrange("(p a) -> p a", a=1)),
                                 (b2[:, :], t["b2_0"].rearrange("(p a) -> p a", a=1))):
                    sp.dma_start(dst, src).then_inc(s_w, 16)
                for dst, src in ((k["const"][:, :], t["shape_constants"]), (k["coef"][:, :], t["coefficients"]),
                                 (trash[:, :, :], t["trash_rows"].rearrange("p (b g) -> p b g", g=G))):
                    sp.dma_start(dst, src).then_inc(s_const, 16)
                for n, name in enumerate(("src_rows", "dst_rows", "next_rows")):
                    sp.dma_start(rows[:, n, :, :], t[name].rearrange("p (b g) -> p b g", g=G)).then_inc(s_rows, 16)

                def load(b):
                    wait_freed(sp, *before(s_p1, b, RING))
                    sp.dma_start(ef[b][:, :], t["edge8T"][:, bass.ds(b.num * BLK, BLK)]).then_inc(s_ef[b], 16)

                def store(b):
                    sp.wait_ge(*this(s_tp, b))
                    sp.dma_start(edge_rows(t["TPW"], b), tp[b][:, :, :]).then_inc(s_tps[b], 16)

                pipeline(sp, EB, [(0, load), (5, store)])
                wait_all(sp, s_tps, EB, 16)
                sp.wait_ge(s_table, 1)
                sp.dma_start(t["INDEX"].rearrange("(b p) c -> p b c", p=P),
                             table[:, :, :, :].rearrange("p b n g -> p b (n g)")).then_inc(s_tabled, 16)
                sp.wait_ge(s_tabled, 16)

            @block.gpsimd
            def _(pool):
                pool.memset(zeros[:, :], 0.0).then_inc(s_zero, 1)
                pool.wait_ge(s_zero, 1)
                for name in ("X1", "X3", "H2"):
                    pool.dma_start(t[name][N:N + 1, :], zeros[0:1, 0:D]).then_inc(s_z0, 16)
                    pool.dma_start(t[name][N + 1:NT, :].rearrange("(p g) c -> p (g c)", p=P), zeros[:, :]).then_inc(s_z0, 16)
                step = -(-N // COPIES)
                for c in range(COPIES):
                    if c >= 2:
                        pool.wait_ge(s_mask, c - 1)
                    pool.dma_start(dst_all[c % 2][:, :], t["dst_ext"][c * MB:(c + 1) * MB + 1].partition_broadcast(P)
                                   ).then_inc(s_dst[c % 2], 16)
                    pool.dma_start(t["X1"][c * step:min(N, (c + 1) * step), :], t["x"][c * step:min(N, (c + 1) * step), :]
                                   ).then_inc(s_copy, 16)
                pool.wait_ge(s_z0, 96)
                pool.wait_ge(s_copy, COPIES * 16)

            @block.tensor
            def _(pe):
                pe.wait_ge(s_w, 80)

                def first(b):
                    pe.wait_ge(*this(s_ef, b, 16))
                    wait_freed(pe, *before(s_m1, b, 2))
                    pe.matmul(p1[b][0:64, :], lhsT=a1[:, :], rhs=ef[b][:, :], start=True, stop=True).then_inc(s_p1, 1)

                def second(b):
                    pe.wait_ge(*this(s_m1, b))
                    wait_freed(pe, *before(s_m2, b, 2))
                    pe.sem_inc(s_turn, 1)
                    pe.matmul(p2[b][0:64, :], lhsT=a2[:, :], rhs=m1[b][:, :], start=True, stop=True).then_inc(s_p2, 1)

                def third(b):
                    pe.wait_ge(*this(s_m2, b))
                    wait_freed(pe, *before(s_tp, b, 2))
                    for g in range(G):
                        last = pe.matmul(p3[b][:, g * P:(g + 1) * P], lhsT=m2[b][:, g:BLK:G], rhs=a3[:, :],
                                         start=True, stop=True)
                    last.then_inc(s_p3, 1)

                pipeline(pe, EB, [(0, first), (1, second), (2, third)])

            @block.scalar
            def _(act):
                act.preload_act_table(ACT.Silu)
                act.wait_ge(s_w, 80)

                def silu1(b):
                    act.wait_ge(*this(s_p1, b))
                    wait_freed(act, *before(s_p2, b, RING))
                    act.activation(m1[b][:, :], p1[b][0:64, :], ACT.Silu, bias=b1[:, :]).then_inc(s_m1, 1)

                def silu2(b):
                    act.wait_ge(*this(s_p2, b))
                    wait_freed(act, *before(s_p3, b, RING))
                    act.activation(m2[b][:, :], p2[b][0:64, :], ACT.Silu, bias=b2[:, :]).then_inc(s_m2, 1)

                def evacuate(b):
                    act.wait_ge(*this(s_p3, b))
                    wait_freed(act, *before(s_tps, b, RING, 16))
                    act.copy(tp[b][:, :, :], grouped(p3[b][:, :])).then_inc(s_tp, 1)

                pipeline(act, EB, [(0, silu1), (1, silu2), (2, evacuate)])

            @block.vector
            def _(dve):
                dve.memset(k["eps"][:, :], EPS)
                dve.memset(k["same"][:, EP:EP + 1], 1)
                dve.wait_ge(s_const, 48)
                dve.wait_ge(s_rows, 48)
                dve.tensor_copy(away[:, :, :], rows[:, 1, :, :]).then_inc(s_inner, 1)
                dve.tensor_tensor(inner[:, :, :], rows[:, 1, :, :], rows[:, 2, :, :], ALU.is_equal).then_inc(s_inner, 1)
                dve.tensor_copy(table[:, :, 0, :], rows[:, 0, :, :])
                dve.tensor_copy(table[:, :, 1, :], rows[:, 1, :, :])
                dve.wait_ge(s_inner, 2)
                dve.tensor_tensor(away[:, :, :], trash[:, :, :], away[:, :, :], ALU.subtract).then_inc(s_inner, 1)
                dve.wait_ge(s_inner, 3)
                dve.tensor_tensor(away[:, :, :], away[:, :, :], inner[:, :, :], ALU.mult).then_inc(s_inner, 1)
                dve.wait_ge(s_inner, 4)
                dve.tensor_tensor(table[:, :, 2, :], away[:, :, :], rows[:, 1, :, :], ALU.add).then_inc(s_table, 1)

                for m in range(EP // MB):
                    dve.wait_ge(s_dst[m % 2], (m // 2 + 1) * 16)
                    dve.tensor_tensor(k["same"][:, m * MB:(m + 1) * MB], dst_all[m % 2][:, 1:MB + 1],
                                      dst_all[m % 2][:, 0:MB], ALU.is_equal).then_inc(s_mask, 1)


def layer0(nc, t, k):
    ident, same = k["ident"], k["same"]
    with Phase(nc, "layer0") as ph:
        w_up = ph.sb("w_up", [D, D])
        w_out = ph.sb("w_out", [D, 2, D])
        src = ph.ring("src", [P, G], I32)
        end = ph.ring("end", [P, G], I32)
        attr = ph.ring("attr", [P, G, 4])
        tpw = ph.ring("tpw", [P, G, 4, MUL])
        raw = ph.ring("raw", [P, G, D])
        hT = ph.ring("hT", [P, BLK])
        w0y, w2y, q1, dot = (ph.sb(n, [P, G, MUL]) for n in ("w0y", "w2y", "q1", "dot"))
        vy = ph.sb("vy", [P, G, 3, MUL])
        feat = ph.ring("feat", [P, G, 8, MUL])
        featT = ph.ring("featT", [P, 2, BLK])
        total = ph.ring("total", [P, BLK])
        rows = ph.ring("rows", [P, G, D])
        p_h, p_f0, p_f1, p_back = (ph.ps(n) for n in ("p_h", "p_f0", "p_f1", "p_back"))
        p_up, p_out = ph.ps_ring("p_up"), ph.ps_ring("p_out")
        p_f = [p_f0, p_f1]

        s_w0, s_w, s_wr = ph.sem("weights_cleared"), ph.sem("weights_loaded"), ph.sem("weights_ready")
        s_src, s_end, s_edge = ph.dma("src_loaded"), ph.dma("end_loaded"), ph.dma("edge_data_loaded")
        s_raw, s_add, s_turn = ph.dma("x_gathered"), ph.dma("rows_added"), ph.sem("pool_goes_on")
        s_hT, s_hTc = ph.sem("h_transposed"), ph.sem("hT_ready")
        s_up, s_first, s_mid, s_part, s_dot, s_feat = (ph.sem(n) for n in (
            "up_done", "products1_done", "products2_done", "dot_part_done", "dot_done", "features_done"))
        s_fT, s_fTc, s_out, s_total = (ph.sem(n) for n in (
            "features_transposed", "featT_ready", "out_done", "totals_done"))
        s_back, s_rows = ph.sem("totals_transposed"), ph.sem("rows_ready")
        norm = Norm(ph, k, "norm", raw, s_raw, 64, k["eps"][:, :], s_hT)

        with ph.block() as block:
            @block.sync
            def _(sp):
                sp.wait_ge(s_w0, 1)
                with nc.allow_non_contiguous_dma(reason="weights laid out by component"):
                    sp.dma_start(w_up[0:MUL, 0:MUL], t["W_up_s"]).then_inc(s_w, 16)
                    for c in range(3):
                        sp.dma_start(w_up[MUL + c:D:3, MUL * (c + 1):MUL * (c + 2)], t["W_up_v"]).then_inc(s_w, 16)
                    sp.dma_start(w_out[0:64, 0, 0:MUL], t["W_out_s"]).then_inc(s_w, 16)
                    sp.dma_start(w_out[64:128, 0, MUL:D:3], t["W_out_v"]).then_inc(s_w, 16)
                    sp.dma_start(w_out[0:64, 1, MUL + 1:D:3], t["W_out_v"]).then_inc(s_w, 16)
                    sp.dma_start(w_out[64:128, 1, MUL + 2:D:3], t["W_out_v"]).then_inc(s_w, 16)

                def index(b):
                    wait_freed(sp, *before(s_raw, b, RING, 64))
                    sp.dma_start(src[b][:, :], block_index(t, b)[:, 0:G]).then_inc(s_src[b], 16)

                def edge(b):
                    wait_freed(sp, *before(s_feat, b, RING))
                    sp.dma_start(attr[b][:, :, :], edge_rows(t["edge4"], b)).then_inc(s_edge[b], 16)
                    sp.dma_start(tpw[b][:, :, :, :].rearrange("p g a b -> p g (a b)"), edge_rows(t["TPW"], b)
                                 ).then_inc(s_edge[b], 16)

                def ends(b):
                    wait_freed(sp, *before(s_add, b, RING, 64))
                    sp.dma_start(end[b][:, :], block_index(t, b)[:, 2 * G:3 * G]).then_inc(s_end[b], 16)

                pipeline(sp, EB, [(0, index), (2, edge), (7, ends)])

            @block.gpsimd
            def _(pool):
                def gather(b):
                    pool.wait_ge(*this(s_src, b, 16))
                    wait_freed(pool, *before(norm.s_h, b, RING))
                    pool.sem_inc(s_turn, 1)
                    indexed_gather(pool, raw[b], t["x"], src[b], s_raw[b], N)

                def scatter(b):
                    pool.wait_ge(*this(s_end, b, 16))
                    pool.wait_ge(*this(s_rows, b))
                    pool.sem_inc(s_turn, 1)
                    indexed_add(pool, t["X1"], end[b], rows[b], s_add[b])

                pipeline(pool, EB, [(0, gather), (8, scatter)])
                wait_all(pool, s_add, EB, 64)

            @block.tensor
            def _(pe):
                pe.wait_ge(s_wr, 2)

                def up(b):
                    pe.wait_ge(*this(s_hTc, b))
                    wait_freed(pe, *before(s_feat, b, 2))
                    for g in range(G):
                        last = pe.matmul(p_up[b][:, g * P:(g + 1) * P], lhsT=hT[b][:, g * P:(g + 1) * P], rhs=w_up[:, :],
                                         start=True, stop=True)
                    last.then_inc(s_up, 1)

                def features(b):
                    pe.wait_ge(*this(s_feat, b))
                    wait_freed(pe, *before(s_fTc, b, 1))
                    for c in range(2):
                        last = transpose_rows(pe, p_f[c], feat[b][:, :, 4 * c:4 * c + 4, :].rearrange("p g a b -> p g (a b)"),
                                              ident, True)
                    last.then_inc(s_fT, 1)

                def rows_T(b):
                    pe.wait_ge(*this(norm.s_h, b))
                    wait_freed(pe, *before(s_hTc, b, 1))
                    transpose_rows(pe, p_h, norm.h[b], ident, False).then_inc(s_hT, 1)

                def out(b):
                    pe.wait_ge(*this(s_fTc, b))
                    wait_freed(pe, *before(s_total, b, 2))
                    for c in range(2):
                        last = pe.matmul(p_out[b][:, :], lhsT=w_out[:, c, :], rhs=featT[b][:, c, :], start=(c == 0), stop=(c == 1))
                    last.then_inc(s_out, 1)

                def back(b):
                    pe.wait_ge(*this(s_total, b))
                    wait_freed(pe, *before(s_rows, b, 1))
                    transpose_back(pe, p_back, total[b], ident).then_inc(s_back, 1)

                pipeline(pe, EB, [(5, out), (3, up), (2, rows_T), (4, features), (6, back)])

            @block.scalar
            def _(act):
                act.preload_act_table_set(LN_EXP)
                def evac_h(b):
                    act.wait_ge(*this(s_hT, b))
                    wait_freed(act, *before(s_up, b, RING))
                    act.copy(hT[b][:, :], p_h[:, :]).then_inc(s_hTc, 1)

                def evac_features(b):
                    act.wait_ge(*this(s_fT, b))
                    wait_freed(act, *before(s_out, b, RING))
                    act.copy(featT[b][:, 0, :], p_f0[:, :])
                    act.copy(featT[b][:, 1, :], p_f1[:, :]).then_inc(s_fTc, 1)

                def evac_rows(b):
                    act.wait_ge(*this(s_back, b))
                    wait_freed(act, *before(s_add, b, RING, 64))
                    act.copy(rows[b][:, :, :], grouped(p_back[:, :])).then_inc(s_rows, 1)

                pipeline(act, EB, [(1, partial(norm.scalar_relu, act)), (0, partial(norm.scalar_rstd, act)), (2, evac_h), (4, evac_features),
                                   (6, evac_rows)])

            @block.vector
            def _(dve):
                s_z = s_w0
                dve.memset(w_up[:, :], 0.0)
                dve.memset(total[RING - 1][:, :], 0.0)
                dve.memset(w_out[:, :, :], 0.0).then_inc(s_z, 1)
                dve.wait_ge(s_w, 128)
                dve.tensor_scalar_mul(w_up[:, :], w_up[:, :], float(1.0 / np.sqrt(MUL))).then_inc(s_wr, 1)
                dve.tensor_scalar_mul(w_out[:, :, :], w_out[:, :, :], float(0.1 / np.sqrt(2 * MUL))).then_inc(s_z, 1)
                dve.wait_ge(s_z, 2)
                dve.tensor_scalar_mul(w_out[MUL:2 * MUL, 0, :], w_out[MUL:2 * MUL, 0, :], float(1.0 / np.sqrt(3.0))
                                      ).then_inc(s_wr, 1)

                def products(b):
                    dve.wait_ge(*this(s_edge, b, 32))
                    wait_freed(dve, *before(s_feat, b, 1))
                    y = attr[b]
                    up = grouped(p_up[b][:, :])
                    vec = up[:, :, MUL:D].rearrange("p g (i c) -> p g i c", i=3)
                    yv = bc(y[:, :, 1:4], 3, MUL)
                    dve.tensor_tensor(w0y[:, :, :], tpw[b][:, :, 0, :], y[:, :, 0:1].to_broadcast([P, G, MUL]), ALU.mult)
                    dve.tensor_tensor(w2y[:, :, :], tpw[b][:, :, 2, :], y[:, :, 0:1].to_broadcast([P, G, MUL]), ALU.mult)
                    dve.wait_ge(*this(s_up, b))
                    dve.tensor_tensor(q1[:, :, :], up[:, :, 0:MUL], tpw[b][:, :, 1, :], ALU.mult)
                    dve.tensor_tensor(vy[:, :, :, :], vec, yv, ALU.mult).then_inc(s_first, 1)
                    dve.wait_ge(*this(s_first, b))
                    wait_freed(dve, *before(s_fT, b, RING))
                    dve.tensor_tensor(dot[:, :, :], vy[:, :, 0, :], vy[:, :, 1, :], ALU.add).then_inc(s_part, 1)
                    dve.tensor_tensor(feat[b][:, :, 0, :], up[:, :, 0:MUL], w0y[:, :, :], ALU.mult)
                    dve.wait_ge(*this(s_part, b))
                    dve.tensor_tensor(dot[:, :, :], dot[:, :, :], vy[:, :, 2, :], ALU.add).then_inc(s_mid, 1)
                    dve.tensor_tensor(feat[b][:, :, 2:8:2, :], bc(q1[:, :, :], 2, 3), yv, ALU.mult)
                    dve.tensor_tensor(feat[b][:, :, 3:8:2, :], vec, bc(w2y[:, :, :], 2, 3), ALU.mult)
                    dve.wait_ge(*this(s_mid, b))
                    dve.tensor_tensor(feat[b][:, :, 1, :], dot[:, :, :], tpw[b][:, :, 3, :], ALU.mult).then_inc(s_feat, 1)

                def sums(b):
                    dve.wait_ge(*this(s_out, b))
                    wait_freed(dve, *before(s_total, b, 1))
                    wait_freed(dve, *before(s_back, b, RING))
                    dve.tensor_tensor_scan(total[b][:, :], edge_cols(same, b), p_out[b][:, :], total[b.back(1)][:, BLK - 1:BLK],
                                           ALU.mult, ALU.add).then_inc(s_total, 1)

                dve.wait_ge(s_z, 2)
                pipeline(dve, EB, [(1, partial(norm.vector_shift, dve)), (0, partial(norm.vector_stats, dve)), (5, sums), (3, products)])


def block_index(t, b):
    return t["INDEX"][bass.ds(b.num * P, P), :]


def edge_cols(cols, b):
    return cols[:, bass.ds(b.num * BLK, BLK)]


def stats(nc, t, k):
    with Phase(nc, "stats") as ph:
        raw = ph.ring("raw", [P, G, D])
        p_h = ph.ps_ring("p_h", 4)
        s_raw, s_hT, s_bn, s_store = ph.dma("x1_loaded"), ph.sem("h_transposed"), ph.sem("columns_counted"), ph.dma("h_stored")
        norm = Norm(ph, k, "norm", raw, s_raw, 16, k["eps"][:, :], s_hT)
        s_aggr = ph.sem("node_mv_done")

        with ph.block() as block:
            @block.sync
            def _(sp):
                def load(b):
                    wait_freed(sp, *before(norm.s_h, b, RING))
                    sp.dma_start(raw[b][:, :, :], node_rows(t["X1"], b)).then_inc(s_raw[b], 16)

                def store(b):
                    sp.wait_ge(*this(norm.s_h, b))
                    if is_last_node_block(b):
                        wait_freed(sp, *before(s_store, b, 1, 16))
                    sp.dma_start(node_rows(t["H2"], b), norm.h[b][:, :, :]).then_inc(s_store[b], 16)

                pipeline(sp, NB, [(0, load), (5, store)])
                wait_all(sp, s_store, NB, 16)

            @block.tensor
            def _(pe):
                def rows_T(b):
                    pe.wait_ge(*this(norm.s_h, b))
                    wait_freed(pe, *before(s_bn, b, RING))
                    transpose_rows(pe, p_h[b], norm.h[b], k["ident"], True).then_inc(s_hT, 1)

                pipeline(pe, NB, [(0, rows_T)])

            @block.scalar
            def _(act):
                act.preload_act_table_set(LN_EXP)
                def rows_relu(b):
                    wait_freed(act, *before(s_store, b, RING, 16))
                    norm.scalar_relu(act, b)

                pipeline(act, NB, [(0, partial(norm.scalar_rstd, act)), (1, rows_relu)])

            @block.vector
            def _(dve):
                def columns(b):
                    dve.wait_ge(*this(s_hT, b))
                    new = BLK - NEW if is_last_node_block(b) else 0
                    dve.bn_stats(k["node_stats"][:, bass.ds(b.num, 1), :].rearrange("p b c -> p (b c)"),
                                 p_h[b][:, new:BLK]).then_inc(s_bn, 1)

                pipeline(dve, NB, [(0, partial(norm.vector_stats, dve)), (4, columns), (1, partial(norm.vector_shift, dve))])
                dve.wait_ge(s_bn, NB)
                dve.bn_aggr(k["node_mv"][:, :], k["node_stats"][:, :, :].rearrange("p b c -> p (b c)")).then_inc(s_aggr, 1)


def column(vector):
    return vector.rearrange("(p a) -> p a", a=1)


class Affine:

    def __init__(self, ph, name):
        self.g, self.b = ph.sb(f"{name}_g", [P, 1]), ph.sb(f"{name}_b", [P, 1])
        self.ln, self.rstd = ph.sb(f"{name}_ln", [P, 1]), ph.sb(f"{name}_rstd", [P, 1])
        self.scale, self.off, self.shift = (ph.sb(f"{name}_{n}", [P, 1]) for n in ("scale", "off", "shift"))
        self.s_rstd, self.s_ln, self.s_done = (ph.sem(f"{name}_{n}") for n in ("rstd_done", "ln_done", "affine_steps"))

    def scalar(self, act, var, eps):
        act.activation(self.ln[:, :], var, ACT.Ln, bias=eps).then_inc(self.s_ln, 1)
        act.wait_ge(self.s_ln, 1)
        act.activation(self.rstd[:, :], self.ln[:, :], ACT.Exp, scale=-0.5).then_inc(self.s_rstd, 1)

    def vector(self, dve, mean):
        dve.wait_ge(self.s_rstd, 1)
        dve.tensor_tensor(self.scale[:, :], self.g[:, :], self.rstd[:, :], ALU.mult).then_inc(self.s_done, 1)
        dve.wait_ge(self.s_done, 1)
        dve.tensor_tensor(self.off[:, :], mean, self.scale[:, :], ALU.mult).then_inc(self.s_done, 1)
        dve.wait_ge(self.s_done, 2)
        dve.tensor_tensor(self.shift[:, :], self.b[:, :], self.off[:, :], ALU.subtract).then_inc(self.s_done, 1)
        dve.wait_ge(self.s_done, 3)


def layer1(nc, t, k):
    ident, same = k["ident"], k["same"]
    with Phase(nc, "layer1") as ph:
        w = ph.sb("w", [D, 4, D])
        wn = ph.sb("wn", [D, 3, D])
        bias = ph.sb("bias", [D, 3])
        bn = Affine(ph, "bn")
        idx = {n: ph.ring(n, [P, G], I32) for n in ("src", "dst", "end")}
        raw_s = ph.ring("raw_s", [P, G, D])
        raw_d = ph.ring("raw_d", [P, G, D])
        hsT = ph.ring("hsT", [P, BLK])
        hdT = ph.ring("hdT", [P, BLK])
        key, value = ph.sb("key", [P, BLK]), ph.sb("value", [P, BLK])
        prod, score, weight = (ph.ring(n, [P, BLK], depth=2) for n in ("prod", "score", "weight"))
        wsum = ph.ring("wsum", [P, BLK])
        vsum = ph.ring("vsum", [P, BLK])
        lsum, inv, mix, gone, twice, junk = (ph.sb(n, [P, BLK]) for n in ("lsum", "inv", "mix", "gone", "twice", "junk"))
        delta = ph.ring("delta", [P, BLK])
        rows = ph.ring("rows", [P, G, D])
        p_hs, p_hd, p_k, p_q, p_v, p_s, p_o, p_back = (ph.ps(n) for n in (
            "p_hs", "p_hd", "p_k", "p_q", "p_v", "p_s", "p_o", "p_back"))

        s_w, s_wn, s_pb, s_bias = ph.sem("weights_loaded"), ph.sem("weights_scaled"), ph.sem("bias_multiplied"), ph.sem("bias_ready")
        s_idx = {n: ph.dma(f"{n}_loaded") for n in ("src", "dst", "end")}
        s_raw, s_rawd, s_add, s_turn = ph.dma("src_gathered"), ph.dma("dst_gathered"), ph.dma("rows_added"), ph.sem("pool_goes_on")
        s_hsT, s_hdT, s_hsc, s_hdc = (ph.sem(n) for n in ("hs_transposed", "hd_transposed", "hsT_ready", "hdT_ready"))
        s_kq, s_v, s_key, s_prod, s_s, s_score = (ph.sem(n) for n in (
            "key_query_done", "values_done", "key_ready", "product_ready", "scores_summed", "scores_clipped"))
        s_exp, s_val, s_sums, s_inv, s_mix = (ph.sem(n) for n in (
            "weights_ready", "values_weighted", "sums_done", "reciprocal_done", "mix_ready"))
        s_o, s_delta, s_back, s_rows, s_gone, s_moved = (ph.sem(n) for n in (
            "out_done", "delta_ready", "delta_transposed", "rows_ready", "ends_picked", "moved_done"))
        s_wsum, s_lsum = ph.sem("weights_summed"), ph.sem("log_of_sums")
        norm_s = Norm(ph, k, "src", raw_s, s_raw, 64, k["eps"][:, :], s_hsT)
        norm_d = Norm(ph, k, "dst", raw_d, s_rawd, 64, k["eps"][:, :], s_hdT)

        with ph.block() as block:
            @block.sync
            def _(sp):
                for n, name in enumerate(("Wq", "Wk", "Wv", "Wo")):
                    sp.dma_start(w[:, n, :], t[name]).then_inc(s_w, 16)
                sp.dma_start(bn.g[:, :], column(t["g1"])).then_inc(s_w, 16)
                sp.dma_start(bn.b[:, :], column(t["b1"])).then_inc(s_w, 16)
                gathers, ends = edge_indices(sp, t, idx, s_idx, {"src": s_raw, "dst": s_rawd}, s_add)
                pipeline(sp, EB, [(0, gathers), (7, ends)])

            @block.gpsimd
            def _(pool):
                def gather(b):
                    pool.wait_ge(*this(s_idx["src"], b, 16))
                    wait_freed(pool, *before(norm_s.s_h, b, RING))
                    pool.sem_inc(s_turn, 1)
                    indexed_gather(pool, raw_s[b], t["X1"], idx["src"][b], s_raw[b], NT)
                    pool.wait_ge(*this(s_idx["dst"], b, 16))
                    wait_freed(pool, *before(norm_d.s_h, b, RING))
                    pool.sem_inc(s_turn, 1)
                    indexed_gather(pool, raw_d[b], t["X1"], idx["dst"][b], s_rawd[b], NT)

                def scatter(b):
                    pool.wait_ge(*this(s_idx["end"], b, 16))
                    pool.wait_ge(*this(s_rows, b))
                    pool.sem_inc(s_turn, 1)
                    indexed_add(pool, t["H2"], idx["end"][b], rows[b], s_add[b])

                pipeline(pool, EB, [(0, gather), (8, scatter)])
                wait_all(pool, s_add, EB, 64)

            @block.tensor
            def _(pe):
                pe.wait_ge(s_w, 96)
                pe.wait_ge(bn.s_done, 3)
                for n in range(3):
                    last = pe.matmul(p_k[:, n:n + 1], lhsT=w[:, n, :], rhs=bn.shift[:, :], start=True, stop=True)
                last.then_inc(s_pb, 1)
                pe.wait_ge(s_bias, 1)
                pe.wait_ge(s_wn, 1)

                def rows_T(b):
                    for norm, p_h, s_t, s_c in ((norm_s, p_hs, s_hsT, s_hsc), (norm_d, p_hd, s_hdT, s_hdc)):
                        pe.wait_ge(*this(norm.s_h, b))
                        wait_freed(pe, *before(s_c, b, 1))
                        transpose_rows(pe, p_h, norm.h[b], ident, True).then_inc(s_t, 1)

                def project(b):
                    pe.wait_ge(*this(s_hsc, b))
                    pe.wait_ge(*this(s_hdc, b))
                    wait_freed(pe, *before(s_prod, b, 1))
                    pe.matmul(p_k[:, :], lhsT=wn[:, 1, :], rhs=hsT[b][:, :], start=True, stop=True)
                    pe.matmul(p_q[:, :], lhsT=wn[:, 0, :], rhs=hdT[b][:, :], start=True, stop=True).then_inc(s_kq, 1)

                def project_values(b):
                    wait_freed(pe, *before(s_val, b, 1))
                    pe.matmul(p_v[:, :], lhsT=wn[:, 2, :], rhs=hsT[b][:, :], start=True, stop=True).then_inc(s_v, 1)

                def head_sums(b):
                    pe.wait_ge(*this(s_prod, b))
                    wait_freed(pe, *before(s_score, b, 1))
                    pe.matmul(p_s[:, :], lhsT=k["blocks16"], rhs=prod[b][:, :], start=True, stop=True).then_inc(s_s, 1)

                def out(b):
                    pe.wait_ge(*this(s_mix, b))
                    wait_freed(pe, *before(s_delta, b, 1))
                    pe.matmul(p_o[:, :], lhsT=w[:, 3, :], rhs=mix[:, :], start=True, stop=True).then_inc(s_o, 1)

                def back(b):
                    pe.wait_ge(*this(s_delta, b))
                    wait_freed(pe, *before(s_rows, b, 1))
                    transpose_back(pe, p_back, delta[b], ident).then_inc(s_back, 1)

                pipeline(pe, EB, [(4, head_sums), (6, back), (5, out), (4, project_values), (2, rows_T), (3, project)])

            @block.scalar
            def _(act):
                act.preload_act_table_set(LN_EXP)
                bn.scalar(act, k["node_mv"][:, 1:2], k["eps"][:, :])

                def evac_h(b):
                    wait_freed(act, *before(s_v, b, RING))
                    wait_freed(act, *before(s_moved, b, RING))
                    act.wait_ge(*this(s_hsT, b))
                    act.copy(hsT[b][:, :], p_hs[:, :]).then_inc(s_hsc, 1)
                    act.wait_ge(*this(s_hdT, b))
                    act.copy(hdT[b][:, :], p_hd[:, :]).then_inc(s_hdc, 1)

                def exps(b):
                    act.wait_ge(*this(s_score, b))
                    wait_freed(act, *before(s_sums, b, 2))
                    act.activation(weight[b][:, :], score[b][:, :], ACT.Exp).then_inc(s_exp, 1)

                def inverse(b):
                    act.wait_ge(*this(s_wsum, b))
                    wait_freed(act, *before(s_inv, b, 1))
                    act.activation(lsum[:, :], wsum[b][:, :], ACT.Ln).then_inc(s_lsum, 1)
                    act.wait_ge(*this(s_lsum, b))
                    wait_freed(act, *before(s_mix, b, 1))
                    act.activation(inv[:, :], lsum[:, :], ACT.Exp, scale=-1.0).then_inc(s_inv, 1)

                def evac_out(b):
                    act.wait_ge(*this(s_o, b))
                    wait_freed(act, *before(s_back, b, RING))
                    wait_freed(act, *before(s_moved, b, RING))
                    act.copy(delta[b][:, :], p_o[:, :]).then_inc(s_delta, 1)

                def evac_rows(b):
                    act.wait_ge(*this(s_back, b))
                    wait_freed(act, *before(s_add, b, RING, 64))
                    act.copy(rows[b][:, :, :], grouped(p_back[:, :])).then_inc(s_rows, 1)

                pipeline(act, EB, [(5, inverse), (4, exps), (1, partial(norm_s.scalar_relu, act)), (1, partial(norm_d.scalar_relu, act)),
                                   (5, evac_out), (6, evac_rows), (2, evac_h), (0, partial(norm_s.scalar_rstd, act)),
                                   (0, partial(norm_d.scalar_rstd, act))])

            @block.vector
            def _(dve):
                dve.memset(wsum[RING - 1][:, :], 0.0)
                dve.memset(vsum[RING - 1][:, :], 0.0)
                dve.wait_ge(s_w, 96)
                bn.vector(dve, k["node_mv"][:, 0:1])
                dve.tensor_scalar(wn[:, :, :], w[:, 0:3, :], bn.scale[:, :], None, ALU.mult).then_inc(s_wn, 1)
                dve.wait_ge(s_pb, 1)
                dve.tensor_copy(bias[:, :], p_k[:, 0:3]).then_inc(s_bias, 1)
                dve.wait_ge(s_bias, 1)

                def scores(b):
                    dve.wait_ge(*this(s_kq, b))
                    wait_freed(dve, *before(s_prod, b, 1))
                    dve.tensor_scalar(key[:, :], p_k[:, :], bias[:, 1:2], None, ALU.add).then_inc(s_key, 1)
                    dve.wait_ge(*this(s_key, b))
                    wait_freed(dve, *before(s_s, b, 2))
                    dve.scalar_tensor_tensor(prod[b][:, :], p_q[:, :], bias[:, 0:1], key[:, :], ALU.add, ALU.mult
                                             ).then_inc(s_prod, 1)

                def clip(b):
                    dve.wait_ge(*this(s_s, b))
                    wait_freed(dve, *before(s_exp, b, 2))
                    dve.tensor_scalar(score[b][:, :], p_s[:, :], 5.0, -5.0, ALU.min, ALU.max).then_inc(s_score, 1)

                def sums(b):
                    dve.wait_ge(*this(s_v, b))
                    dve.wait_ge(*this(s_exp, b))
                    wait_freed(dve, *before(s_sums, b, 1))
                    dve.scalar_tensor_tensor(value[:, :], p_v[:, :], bias[:, 2:3], weight[b][:, :], ALU.add, ALU.mult
                                             ).then_inc(s_val, 1)
                    dve.tensor_tensor_scan(wsum[b][:, :], edge_cols(same, b), weight[b][:, :], wsum[b.back(1)][:, BLK - 1:BLK],
                                           ALU.mult, ALU.add).then_inc(s_wsum, 1)
                    dve.wait_ge(*this(s_val, b))
                    dve.tensor_tensor_scan(vsum[b][:, :], edge_cols(same, b), value[:, :], vsum[b.back(1)][:, BLK - 1:BLK],
                                           ALU.mult, ALU.add).then_inc(s_sums, 1)

                def average(b):
                    dve.wait_ge(*this(s_inv, b))
                    dve.wait_ge(*this(s_sums, b))
                    wait_freed(dve, *before(s_o, b, 1))
                    dve.tensor_tensor(mix[:, :], vsum[b][:, :], inv[:, :], ALU.mult).then_inc(s_mix, 1)

                def moved(b):
                    dve.wait_ge(*this(s_delta, b))
                    wait_freed(dve, *before(s_moved, b, 1))
                    at = bass.ds(b.num, 1)
                    dve.scalar_tensor_tensor(gone[:, :], same[:, bass.ds(b.num * BLK + 1, BLK)], 1.0, delta[b][:, :],
                                             ALU.subtract, ALU.mult, accum_out=k["moved"][:, 0, at])
                    dve.scalar_tensor_tensor(twice[:, :], hdT[b][:, :], 2.0, delta[b][:, :], ALU.mult, ALU.add
                                             ).then_inc(s_gone, 1)
                    dve.wait_ge(*this(s_gone, b))
                    dve.scalar_tensor_tensor(junk[:, :], gone[:, :], 1.0, twice[:, :], ALU.mult, ALU.mult,
                                             accum_out=k["moved"][:, 1, at]).then_inc(s_moved, 1)

                pipeline(dve, EB, [(4, clip), (5, average), (1, partial(norm_s.vector_shift, dve)), (1, partial(norm_d.vector_shift, dve)),
                                   (4, sums), (0, partial(norm_s.vector_stats, dve)), (0, partial(norm_d.vector_stats, dve)), (3, scores),
                                   (5, moved)])


def edge_indices(sp, t, idx, s_idx, used, s_scattered):
    cols = {"src": 0, "dst": G, "end": 2 * G}

    def gathers(b):
        for n in used:
            wait_freed(sp, *before(used[n], b, RING, 64))
            sp.dma_start(idx[n][b][:, :], block_index(t, b)[:, cols[n]:cols[n] + G]).then_inc(s_idx[n][b], 16)

    def ends(b):
        wait_freed(sp, *before(s_scattered, b, RING, 64))
        sp.dma_start(idx["end"][b][:, :], block_index(t, b)[:, cols["end"]:]).then_inc(s_idx["end"][b], 16)

    return gathers, ends


def nodes(nc, t, k):
    ident = k["ident"]
    F = 2 * D
    with Phase(nc, "nodes") as ph:
        bn = Affine(ph, "bn")
        bo, bf1 = ph.sb("bo", [P, 1]), ph.sb("bf1", [P, 2])
        w1, w1n, w2, wg = ph.sb("w1", [D, F]), ph.sb("w1n", [D, F]), ph.sb("w2", [P, 2, D]), ph.sb("wg", [D, D])
        add_rows, bias_rows = ph.sb("add_rows", [P, 2, D]), ph.sb("bias_rows", [P, D])
        add_row = ph.sb("add_row", [P, D])
        dsum, dsq, e1, e2, e3, e4 = (ph.sb(n, [P, 1]) for n in ("dsum", "dsq", "e1", "e2", "e3", "e4"))
        mean, var, meanb, hbias = (ph.sb(n, [P, 1]) for n in ("mean", "var", "meanb", "hbias"))
        b1n = ph.sb("b1n", [P, 2])
        x1 = ph.ring("x1", [P, G, D])
        h2 = ph.ring("h2", [P, G, D])
        both, base = ph.sb("both", [P, G, D]), ph.ring("base", [P, G, D])
        hT = ph.ring("hT", [P, BLK])
        z = ph.ring("z", [P, 2, BLK])
        x2 = ph.ring("x2", [P, G, D])
        h3T = ph.ring("h3T", [P, BLK])
        pre, low, ex = (ph.ring(n, [P, G, D], depth=2) for n in ("pre", "low", "ex"))
        part = ph.sb("part", [P, G, D])
        res = ph.ring("res", [P, G, D])
        p_z0, p_z1, p_h3, p_g = (ph.ps(n) for n in ("p_z0", "p_z1", "p_h3", "p_g"))
        p_h, p_y = ph.ps_ring("p_h"), ph.ps_ring("p_y")
        p_z = [p_z0, p_z1]

        s_w, s_v, s_b1, s_b1n = ph.sem("weights_loaded"), ph.sem("preparation_steps"), ph.sem("bias_multiplied"), ph.sem("prepared")
        s_var, s_rows = ph.sem("var_ready"), ph.sem("rows_added_up")
        s_in, s_base, s_both = ph.dma("rows_loaded"), ph.sem("base_ready"), ph.sem("both_ready")
        s_hT, s_hTc, s_z, s_zc, s_y, s_x2 = (ph.sem(n) for n in (
            "h_transposed", "hT_ready", "hidden_done", "relu_done", "ffn_done", "x2_ready"))
        s_h3, s_h3c, s_g, s_pre, s_low, s_ex, s_part, s_res = (ph.sem(n) for n in (
            "h3_transposed", "h3T_ready", "gat_done", "pre_ready", "low_ready", "exp_ready", "part_ready", "out_ready"))
        s_st2, s_sto = ph.dma("x2_stored"), ph.dma("out_stored")
        norm = Norm(ph, k, "norm", x2, None, 0, k["eps"][:, :], s_h3)

        with ph.block() as block:
            @block.sync
            def _(sp):
                with nc.allow_non_contiguous_dma(reason="columns of vectors"):
                    for dst, src in ((bn.g[:, :], column(t["g2"])), (bn.b[:, :], column(t["b2"])), (bo[:, :], column(t["bo"])),
                                     (bf1[:, :], t["bf1"].rearrange("(c p) -> p c", p=P)), (w1[:, :], t["W1"]),
                                     (w2[:, :, :], t["W2"].rearrange("(c p) n -> p c n", p=P)), (wg[:, :], t["WgT"]),
                                     (add_rows[:, 0, :], t["bo"].partition_broadcast(P)),
                                     (add_rows[:, 1, :], t["bf2"].partition_broadcast(P)),
                                     (bias_rows[:, :], t["bias"].partition_broadcast(P))):
                        sp.dma_start(dst, src).then_inc(s_w, 16)

                def load(b):
                    wait_freed(sp, *before(s_hT, b, RING))
                    wait_freed(sp, *before(s_both, b, RING))
                    sp.dma_start(x1[b][:, :, :], node_rows(t["X1"], b)).then_inc(s_in[b], 16)
                    sp.dma_start(h2[b][:, :, :], node_rows(t["H2"], b)).then_inc(s_in[b], 16)

                def store_x2(b):
                    if is_last_node_block(b):
                        wait_freed(sp, *before(s_st2, b, 1, 32))
                    sp.wait_ge(*this(s_x2, b))
                    sp.dma_start(node_rows(t["X2"], b), x2[b][:, :, :]).then_inc(s_st2[b], 16)
                    sp.dma_start(node_rows(t["X3"], b), x2[b][:, :, :]).then_inc(s_st2[b], 16)

                def store_out(b):
                    if is_last_node_block(b):
                        wait_freed(sp, *before(s_sto, b, 1, 16))
                    sp.wait_ge(*this(s_res, b))
                    sp.dma_start(node_rows(t["out"], b), res[b][:, :, :]).then_inc(s_sto[b], 16)

                pipeline(sp, NB, [(0, load), (6, store_x2), (9, store_out)])
                wait_all(sp, s_st2, NB, 32)
                wait_all(sp, s_sto, NB, 16)

            @block.gpsimd
            def _(pool):
                pool.wait_ge(s_w, 160)
                pool.tensor_tensor(add_row[:, :], add_rows[:, 0, :], add_rows[:, 1, :], ALU.add).then_inc(s_rows, 1)
                pool.wait_ge(s_rows, 1)

                def add(b):
                    pool.wait_ge(*this(s_in, b, 32))
                    wait_freed(pool, *before(s_base, b, 1))
                    pool.tensor_tensor(both[:, :, :], x1[b][:, :, :], h2[b][:, :, :], ALU.add).then_inc(s_both, 1)
                    pool.wait_ge(*this(s_both, b))
                    wait_freed(pool, *before(s_x2, b, RING))
                    pool.tensor_tensor(base[b][:, :, :], both[:, :, :], bc(add_row[:, :], 1, G), ALU.add).then_inc(s_base, 1)

                pipeline(pool, NB, [(0, add)])

            @block.tensor
            def _(pe):
                pe.wait_ge(s_w, 160)
                pe.wait_ge(s_v, 10)
                for c in range(2):
                    last = pe.matmul(p_g[:, c:c + 1], lhsT=w1[:, c * P:(c + 1) * P], rhs=hbias[:, :], start=True, stop=True)
                last.then_inc(s_b1, 1)
                pe.wait_ge(s_b1n, 2)

                def rows_T(b):
                    pe.wait_ge(*this(s_in, b, 32))
                    wait_freed(pe, *before(s_hTc, b, 2))
                    transpose_rows(pe, p_h[b], h2[b], ident, False).then_inc(s_hT, 1)

                def hidden(b):
                    pe.wait_ge(*this(s_hTc, b))
                    wait_freed(pe, *before(s_zc, b, 1))
                    for c in range(2):
                        last = pe.matmul(p_z[c][:, :], lhsT=w1n[:, c * P:(c + 1) * P], rhs=hT[b][:, :], start=True, stop=True)
                    last.then_inc(s_z, 1)

                def ffn(b):
                    pe.wait_ge(*this(s_zc, b))
                    wait_freed(pe, *before(s_x2, b, 2))
                    for g in range(G):
                        for c in range(2):
                            last = pe.matmul(p_y[b][:, g * P:(g + 1) * P], lhsT=z[b][:, c, g * P:(g + 1) * P], rhs=w2[:, c, :],
                                             start=(c == 0), stop=(c == 1))
                    last.then_inc(s_y, 1)

                def rows3_T(b):
                    pe.wait_ge(*this(norm.s_h, b))
                    wait_freed(pe, *before(s_h3c, b, 1))
                    transpose_rows(pe, p_h3, norm.h[b], ident, False).then_inc(s_h3, 1)

                def gat(b):
                    pe.wait_ge(*this(s_h3c, b))
                    wait_freed(pe, *before(s_pre, b, 1))
                    for g in range(G):
                        last = pe.matmul(p_g[:, g * P:(g + 1) * P], lhsT=h3T[b][:, g * P:(g + 1) * P], rhs=wg[:, :],
                                         start=True, stop=True)
                    last.then_inc(s_g, 1)

                pipeline(pe, NB, [(2, ffn), (1, hidden), (5, gat), (4, rows3_T), (0, rows_T)])

            @block.scalar
            def _(act):
                act.preload_act_table_set(LN_EXP)
                act.wait_ge(s_var, 1)
                bn.scalar(act, var[:, :], k["eps"][:, :])
                act.wait_ge(s_b1n, 2)

                def relu_hidden(b):
                    act.wait_ge(*this(s_z, b))
                    wait_freed(act, *before(s_y, b, RING))
                    for c in range(2):
                        last = act.activation(z[b][:, c, :], p_z[c][:, :], ACT.Relu, bias=b1n[:, c:c + 1])
                    last.then_inc(s_zc, 1)

                def exps(b):
                    act.wait_ge(*this(s_pre, b))
                    wait_freed(act, *before(s_ex, b, 2))
                    act.activation(low[b][:, :, :], pre[b][:, :, :], ACT.Relu, scale=-1.0).then_inc(s_low, 1)
                    act.wait_ge(*this(s_low, b))
                    wait_freed(act, *before(s_part, b, 2))
                    act.activation(ex[b][:, :, :], low[b][:, :, :], ACT.Exp, scale=-1.0).then_inc(s_ex, 1)

                pipeline(act, NB, [(3, partial(norm.scalar_rstd, act)), (3, partial(norm.scalar_relu, act)), (1, relu_hidden), (5, exps)])

            @block.vector
            def _(dve):
                steps = [0]

                def link(ins):
                    steps[0] += 1
                    ins.then_inc(s_v, 1)
                    dve.wait_ge(s_v, steps[0])

                old_mean, old_var = k["node_mv"][:, 0:1], k["node_mv"][:, 1:2]
                dve.wait_ge(s_w, 160)
                link(dve.reduce_sum(dsum[:, :], k["moved"][:, 0, :], mybir.AxisListType.X))
                link(dve.reduce_sum(dsq[:, :], k["moved"][:, 1, :], mybir.AxisListType.X))
                link(dve.tensor_scalar(e1[:, :], dsum[:, :], -1.0 / N, None, ALU.mult))
                link(dve.tensor_tensor(mean[:, :], old_mean, e1[:, :], ALU.add))
                link(dve.scalar_tensor_tensor(e2[:, :], dsum[:, :], 2.0, old_mean, ALU.mult, ALU.mult))
                link(dve.tensor_tensor(e3[:, :], e2[:, :], dsq[:, :], ALU.subtract))
                link(dve.scalar_tensor_tensor(e4[:, :], e3[:, :], 1.0 / N, old_var, ALU.mult, ALU.add))
                link(dve.tensor_tensor(e2[:, :], e1[:, :], e1[:, :], ALU.mult))
                dve.tensor_tensor(var[:, :], e4[:, :], e2[:, :], ALU.subtract).then_inc(s_var, 1)
                bn.vector(dve, mean[:, :])
                link(dve.tensor_scalar(w1n[:, :], w1[:, :], bn.scale[:, :], None, ALU.mult))
                link(dve.tensor_copy(hbias[:, :], bn.shift[:, :]))
                dve.wait_ge(s_b1, 1)
                dve.tensor_tensor(b1n[:, :], p_g[:, 0:2], bf1[:, :], ALU.add).then_inc(s_b1n, 2)
                dve.wait_ge(s_b1n, 2)

                def evac_h(b):
                    dve.wait_ge(*this(s_hT, b))
                    wait_freed(dve, *before(s_z, b, RING))
                    dve.tensor_copy(hT[b][:, :], p_h[b][:, :]).then_inc(s_hTc, 1)

                def residual(b):
                    dve.wait_ge(*this(s_y, b))
                    dve.wait_ge(*this(s_base, b))
                    wait_freed(dve, *before(s_st2, b, RING, 32))
                    wait_freed(dve, *before(s_res, b, RING))
                    wait_freed(dve, *before(norm.s_h, b, RING))
                    dve.tensor_tensor(x2[b][:, :, :], grouped(p_y[b][:, :]), base[b][:, :, :], ALU.add).then_inc(s_x2, 1)
                    dve.wait_ge(*this(s_x2, b))
                    norm.vector_stats(dve, b)

                def evac_h3(b):
                    dve.wait_ge(*this(s_h3, b))
                    wait_freed(dve, *before(s_g, b, RING))
                    dve.tensor_copy(h3T[b][:, :], p_h3[:, :]).then_inc(s_h3c, 1)

                def before_elu(b):
                    dve.wait_ge(*this(s_g, b))
                    wait_freed(dve, *before(s_low, b, 2))
                    wait_freed(dve, *before(s_part, b, 2))
                    dve.tensor_tensor(pre[b][:, :, :], grouped(p_g[:, :]), bc(bias_rows[:, :], 1, G), ALU.add).then_inc(s_pre, 1)

                def elu(b):
                    dve.wait_ge(*this(s_ex, b))
                    wait_freed(dve, *before(s_res, b, 1))
                    dve.scalar_tensor_tensor(part[:, :, :], pre[b][:, :, :], 0.0, ex[b][:, :, :], ALU.max, ALU.add
                                             ).then_inc(s_part, 1)
                    dve.wait_ge(*this(s_part, b))
                    wait_freed(dve, *before(s_sto, b, RING, 16))
                    dve.scalar_tensor_tensor(res[b][:, :, :], part[:, :, :], -1.0, x2[b][:, :, :], ALU.add, ALU.add
                                             ).then_inc(s_res, 1)

                pipeline(dve, NB, [(1, evac_h), (5, evac_h3), (3, partial(norm.vector_shift, dve)), (6, elu), (2, residual),
                                   (5, before_elu)])


def layer2(nc, t, k):
    ident, same = k["ident"], k["same"]
    NF = 11
    CHUNKS = [(0, 4), (4, 8), (8, NF)]
    WEIGHT = {0: ("w0", None), 1: ("w3", None)}
    for c in range(3):
        for n, name in enumerate(("w1", "w2", "w4")):
            WEIGHT[2 + 3 * c + n] = (name, c)
    with Phase(nc, "layer2") as ph:
        w = ph.sb("w", [P, 3, D])
        idx = {n: ph.ring(n, [P, G], I32) for n in ("src", "end")}
        attrT = ph.ring("attrT", [9, BLK])
        raw = ph.ring("raw", [P, G, D])
        coef = ph.ring("coef", [P, G, COEF])
        vy = ph.sb("vy", [P, G, MUL, 3])
        m0, m1, m2, m01 = (ph.sb(n, [P, G, 3, MUL]) for n in ("m0", "m1", "m2", "m01"))
        feat = ph.ring("feat", [P, G, NF, MUL])
        featT = ph.ring("featT", [P, 3, BLK])
        total = ph.ring("total", [P, BLK])
        rows = ph.ring("rows", [P, G, D])
        p_f0, p_f1, p_f2, p_back = (ph.ps(n) for n in ("p_f0", "p_f1", "p_f2", "p_back"))
        p_c, p_out = ph.ps_ring("p_c"), ph.ps_ring("p_out")
        p_f = [p_f0, p_f1, p_f2]

        s_w0, s_w = ph.sem("weights_cleared"), ph.sem("weights_loaded")
        s_idx = {n: ph.dma(f"{n}_loaded") for n in ("src", "end")}
        s_attr, s_c, s_cc = ph.dma("attributes_loaded"), ph.sem("coefficients_done"), ph.sem("coefficients_ready")
        s_raw, s_add, s_turn = ph.dma("x2_gathered"), ph.dma("rows_added"), ph.sem("pool_goes_on")
        s_first, s_mid, s_feat, s_fT, s_fTc = (ph.sem(n) for n in (
            "products_done", "half_summed", "features_done", "features_transposed", "featT_ready"))
        s_out, s_total, s_back, s_rows = (ph.sem(n) for n in ("out_done", "totals_done", "totals_transposed", "rows_ready"))
        norm = Norm(ph, k, "norm", raw, s_raw, 64, k["eps"][:, :], s_feat)

        with ph.block() as block:
            @block.sync
            def _(sp):
                sp.wait_ge(s_w0, 1)
                with nc.allow_non_contiguous_dma(reason="weights laid out by component"):
                    for n, (lo, hi) in enumerate(CHUNKS):
                        for f in range(lo, hi):
                            name, c = WEIGHT[f]
                            cols = slice(0, MUL) if c is None else slice(MUL + c, D, 3)
                            sp.dma_start(w[(f - lo) * MUL:(f - lo + 1) * MUL, n, cols],
                                         t[name].rearrange("u a v -> u (a v)")).then_inc(s_w, 16)

                cols = {"src": 0, "end": 2 * G}

                def gathers(b):
                    wait_freed(sp, *before(s_raw, b, RING, 64))
                    sp.dma_start(idx["src"][b][:, :], block_index(t, b)[:, 0:G]).then_inc(s_idx["src"][b], 16)
                    wait_freed(sp, *before(s_c, b, RING))
                    sp.dma_start(attrT[b][:, :], t["edge9T"][:, bass.ds(b.num * BLK, BLK)]).then_inc(s_attr[b], 16)

                def ends(b):
                    wait_freed(sp, *before(s_add, b, RING, 64))
                    sp.dma_start(idx["end"][b][:, :], block_index(t, b)[:, cols["end"]:]).then_inc(s_idx["end"][b], 16)

                pipeline(sp, EB, [(0, gathers), (6, ends)])

            @block.gpsimd
            def _(pool):
                def gather(b):
                    pool.wait_ge(*this(s_idx["src"], b, 16))
                    wait_freed(pool, *before(norm.s_h, b, RING))
                    pool.sem_inc(s_turn, 1)
                    indexed_gather(pool, raw[b], t["X2"], idx["src"][b], s_raw[b], N)

                def scatter(b):
                    pool.wait_ge(*this(s_idx["end"], b, 16))
                    pool.wait_ge(*this(s_rows, b))
                    pool.sem_inc(s_turn, 1)
                    indexed_add(pool, t["X3"], idx["end"][b], rows[b], s_add[b])

                pipeline(pool, EB, [(0, gather), (7, scatter)])
                wait_all(pool, s_add, EB, 64)

            @block.tensor
            def _(pe):
                pe.wait_ge(s_w, NF * 16)

                def coefficients(b):
                    pe.wait_ge(*this(s_attr, b, 16))
                    wait_freed(pe, *before(s_cc, b, 2))
                    for g in range(G):
                        last = pe.matmul(p_c[b][:, g * COEF:(g + 1) * COEF], lhsT=attrT[b][:, g:BLK:G], rhs=k["coef"][:, :],
                                         start=True, stop=True)
                    last.then_inc(s_c, 1)

                def features(b):
                    pe.wait_ge(*this(s_feat, b))
                    wait_freed(pe, *before(s_fTc, b, 1))
                    for n, (lo, hi) in enumerate(CHUNKS):
                        rows_f = (hi - lo) * MUL
                        for g in range(G):
                            last = pe.transpose(p_f[n][0:rows_f, g:BLK:G],
                                                feat[b][:, g, lo:hi, :].rearrange("p a b -> p (a b)"), ident)
                    last.then_inc(s_fT, 1)

                def out(b):
                    pe.wait_ge(*this(s_fTc, b))
                    wait_freed(pe, *before(s_total, b, 2))
                    for n, (lo, hi) in enumerate(CHUNKS):
                        r = (hi - lo) * MUL
                        last = pe.matmul(p_out[b][:, :], lhsT=w[0:r, n, :], rhs=featT[b][0:r, n, :], start=(n == 0), stop=(n == 2))
                    last.then_inc(s_out, 1)

                def back(b):
                    pe.wait_ge(*this(s_total, b))
                    wait_freed(pe, *before(s_rows, b, 1))
                    transpose_back(pe, p_back, total[b], ident).then_inc(s_back, 1)

                pipeline(pe, EB, [(4, out), (5, back), (3, features), (1, coefficients)])

            @block.scalar
            def _(act):
                act.preload_act_table_set(LN_EXP)

                def evac_coefficients(b):
                    act.wait_ge(*this(s_c, b))
                    wait_freed(act, *before(s_feat, b, RING))
                    act.copy(coef[b][:, :, :], p_c[b][:, 0:G * COEF].rearrange("p (g c) -> p g c", g=G)).then_inc(s_cc, 1)

                def evac_features(b):
                    act.wait_ge(*this(s_fT, b))
                    wait_freed(act, *before(s_out, b, RING))
                    for n, (lo, hi) in enumerate(CHUNKS):
                        r = (hi - lo) * MUL
                        last = act.copy(featT[b][0:r, n, :], p_f[n][0:r, :])
                    last.then_inc(s_fTc, 1)

                def evac_rows(b):
                    act.wait_ge(*this(s_back, b))
                    wait_freed(act, *before(s_add, b, RING, 64))
                    act.copy(rows[b][:, :, :], grouped(p_back[:, :])).then_inc(s_rows, 1)

                pipeline(act, EB, [(1, partial(norm.scalar_relu, act)), (5, evac_rows), (3, evac_features), (0, partial(norm.scalar_rstd, act)),
                                   (1, evac_coefficients)])

            @block.vector
            def _(dve):
                dve.memset(total[RING - 1][:, :], 0.0)
                dve.memset(w[:, :, :], 0.0).then_inc(s_w0, 1)

                def products(b):
                    dve.wait_ge(*this(norm.s_h, b))
                    dve.wait_ge(*this(s_cc, b))
                    wait_freed(dve, *before(s_feat, b, 1))
                    wait_freed(dve, *before(s_fT, b, RING))
                    h, c, f = norm.h[b], coef[b], feat[b]
                    hs = h[:, :, 0:MUL]
                    hv = h[:, :, MUL:D].rearrange("p g (c i) -> p g c i", i=3)
                    hvk = h[:, :, MUL:D].rearrange("p g (c i) -> p g i c", i=3)
                    dve.tensor_tensor(vy[:, :, :, :], hv, bc(c[:, :, 1:4], 2, MUL), ALU.mult)
                    for n, m in enumerate((m0, m1, m2)):
                        last = dve.tensor_tensor(m[:, :, :, :], bc(hvk[:, :, n, :], 2, 3),
                                                 bc(c[:, :, 8 + 3 * n:11 + 3 * n], 3, MUL), ALU.mult)
                    last.then_inc(s_first, 1)
                    dve.tensor_tensor(f[:, :, 0, :], hs, c[:, :, 0:1].to_broadcast([P, G, MUL]), ALU.mult)
                    dve.tensor_tensor(f[:, :, 2:NF:3, :], bc(hs, 2, 3), bc(c[:, :, 4:7], 3, MUL), ALU.mult)
                    dve.tensor_tensor(f[:, :, 3:NF:3, :], hvk, bc(c[:, :, 7:8].to_broadcast([P, G, 3]), 3, MUL), ALU.mult)
                    dve.wait_ge(*this(s_first, b))
                    dve.tensor_tensor(m01[:, :, :, :], m0[:, :, :, :], m1[:, :, :, :], ALU.add).then_inc(s_mid, 1)
                    dve.tensor_reduce(f[:, :, 1, :], vy[:, :, :, :], mybir.AxisListType.X, ALU.add)
                    dve.wait_ge(*this(s_mid, b))
                    dve.tensor_tensor(f[:, :, 4:NF:3, :], m01[:, :, :, :], m2[:, :, :, :], ALU.add).then_inc(s_feat, 1)

                def sums(b):
                    dve.wait_ge(*this(s_out, b))
                    wait_freed(dve, *before(s_total, b, 1))
                    wait_freed(dve, *before(s_back, b, RING))
                    dve.tensor_tensor_scan(total[b][:, :], edge_cols(same, b), p_out[b][:, :], total[b.back(1)][:, BLK - 1:BLK],
                                           ALU.mult, ALU.add).then_inc(s_total, 1)

                pipeline(dve, EB, [(1, partial(norm.vector_shift, dve)), (2, products), (4, sums), (0, partial(norm.vector_stats, dve))])


def layer3(nc, t, k):
    ident, same = k["ident"], k["same"]
    with Phase(nc, "layer3") as ph:
        wg, wgT = ph.sb("wg", [D, D]), ph.sb("wgT", [D, D])
        att = ph.sb("att", [P, 2])
        spread = ph.sb("spread", [P, 2, D])
        wa = ph.sb("wa", [D, 2, D])
        bias, nbias = ph.sb("bias", [P, 1]), ph.sb("nbias", [P, 1])
        idx = {n: ph.ring(n, [P, G], I32) for n in ("src", "dst", "end")}
        raw_s = ph.ring("raw_s", [P, G, D])
        raw_d = ph.ring("raw_d", [P, G, D])
        hsT = ph.ring("hsT", [P, BLK])
        hdT = ph.ring("hdT", [P, BLK])
        slow_e, slow_l, log_e, log_l, both = (ph.sb(n, [P, BLK]) for n in ("slow_e", "slow_l", "log_e", "log_l", "both"))
        top = ph.ring("top", [P, BLK + 1], depth=2)
        neg, fall, d_e, d_l, keep, w_e, w_l, wsum, vsum, num, den, ex = (ph.ring(n, [P, BLK], depth=2) for n in (
            "neg", "fall", "d_e", "d_l", "keep", "w_e", "w_l", "wsum", "vsum", "num", "den", "ex"))
        value, own, lden, inv, mix, low, part, elu_T = (ph.sb(n, [P, BLK]) for n in (
            "value", "own", "lden", "inv", "mix", "low", "part", "elu_T"))
        kept_d = ph.ring("kept_d", [P, G, D])
        rows = ph.ring("rows", [P, G, D])
        p_hs, p_hd, p_xs, p_xd, p_e, p_l, p_back = (ph.ps(n) for n in ("p_hs", "p_hd", "p_xs", "p_xd", "p_e", "p_l", "p_back"))

        s_w, s_spread, s_wa, s_wac = ph.sem("weights_loaded"), ph.sem("attention_spread"), ph.sem("wa_done"), ph.sem("wa_ready")
        s_idx = {n: ph.dma(f"{n}_loaded") for n in ("src", "dst", "end")}
        s_aside, s_kept, s_sp_turn = ph.dma("dst_rows_set_aside"), ph.dma("dst_rows_back"), ph.sem("sync_goes_on")
        s_raw, s_rawd, s_put, s_turn = ph.dma("src_gathered"), ph.dma("dst_gathered"), ph.dma("rows_written"), ph.sem("pool_goes_on")
        s_hsT, s_hdT, s_hsc, s_hdc = (ph.sem(n) for n in ("hs_transposed", "hd_transposed", "hsT_ready", "hdT_ready"))
        s_logp, s_xp, s_slow, s_neg, s_log, s_both, s_top = (ph.sem(n) for n in (
            "logits_projected", "values_projected", "slopes_ready", "resets_ready", "logits_ready", "logits_joined", "maximum_done"))
        s_diff, s_fall, s_exp, s_val, s_sums, s_num, s_den = (ph.sem(n) for n in (
            "logits_lowered", "fall_ready", "exps_done", "values_weighted", "sums_done", "numerator_ready", "denominator_ready"))
        s_own, s_lden, s_inv, s_mix, s_low, s_ex, s_part, s_elu = (ph.sem(n) for n in (
            "own_ready", "log_denominator", "reciprocal_ready", "mix_ready", "low_ready", "ex_ready", "part_ready", "elu_ready"))
        s_back, s_rows = ph.sem("elu_transposed"), ph.sem("rows_ready")
        norm_s = Norm(ph, k, "src", raw_s, s_raw, 64, k["eps"][:, :], s_hsT, 2)
        norm_d = Norm(ph, k, "dst", raw_d, s_rawd, 64, k["eps"][:, :], s_hdT, 2)

        with ph.block() as block:
            @block.sync
            def _(sp):
                for dst, src in ((wg[:, :], t["Wg"]), (wgT[:, :], t["WgT"]),
                                 (att[:, 0:1], t["att_src"].rearrange("a h c -> (h c) a")),
                                 (att[:, 1:2], t["att_dst"].rearrange("a h c -> (h c) a")), (bias[:, :], column(t["bias"]))):
                    sp.dma_start(dst, src).then_inc(s_w, 16)
                gathers, ends = edge_indices(sp, t, idx, s_idx, {"src": s_raw, "dst": s_rawd}, s_put)

                def set_aside(b):
                    sp.wait_ge(*this(s_rawd, b, 64))
                    sp.sem_inc(s_sp_turn, 1)
                    sp.dma_start(edge_rows(t["KEPT"], b), raw_d[b][:, :, :]).then_inc(s_aside[b], 16)

                def bring_back(b):
                    sp.wait_ge(*this(s_aside, b, 16))
                    sp.sem_inc(s_sp_turn, 1)
                    wait_freed(sp, *before(s_rows, b, RING))
                    sp.sem_inc(s_sp_turn, 1)
                    sp.dma_start(kept_d[b][:, :, :], edge_rows(t["KEPT"], b)).then_inc(s_kept[b], 16)

                pipeline(sp, EB, [(0, gathers), (3, set_aside), (8, bring_back), (8, ends)])

            @block.gpsimd
            def _(pool):
                def gather_src(b):
                    pool.wait_ge(*this(s_idx["src"], b, 16))
                    wait_freed(pool, *before(norm_s.s_h, b, RING))
                    pool.sem_inc(s_turn, 1)
                    indexed_gather(pool, raw_s[b], t["X3"], idx["src"][b], s_raw[b], NT)

                def gather_dst(b):
                    pool.wait_ge(*this(s_idx["dst"], b, 16))
                    wait_freed(pool, *before(norm_d.s_h, b, RING))
                    wait_freed(pool, *before(s_aside, b, RING, 16))
                    pool.sem_inc(s_turn, 1)
                    indexed_gather(pool, raw_d[b], t["X3"], idx["dst"][b], s_rawd[b], NT)

                def scatter(b):
                    pool.wait_ge(*this(s_idx["end"], b, 16))
                    pool.wait_ge(*this(s_rows, b))
                    pool.sem_inc(s_turn, 1)
                    indexed_write(pool, t["out"], idx["end"][b], rows[b], s_put[b], N - 1)

                pipeline(pool, EB, [(0, gather_src), (9, scatter), (0, gather_dst)])
                wait_all(pool, s_put, EB, 64)

            @block.tensor
            def _(pe):
                pe.wait_ge(s_w, 80)
                pe.wait_ge(s_spread, 2)
                for n in range(2):
                    last = pe.matmul(p_e[:, n * D:(n + 1) * D], lhsT=wg[:, :], rhs=spread[:, n, :], start=True, stop=True)
                last.then_inc(s_wa, 1)
                pe.wait_ge(s_wac, 1)

                def rows_T(b):
                    for norm, p_h, s_t, s_c in ((norm_s, p_hs, s_hsT, s_hsc), (norm_d, p_hd, s_hdT, s_hdc)):
                        pe.wait_ge(*this(norm.s_h, b))
                        wait_freed(pe, *before(s_c, b, 1))
                        transpose_rows(pe, p_h, norm.h[b], ident, True).then_inc(s_t, 1)

                def project(b):
                    pe.wait_ge(*this(s_hsc, b))
                    pe.wait_ge(*this(s_hdc, b))
                    wait_freed(pe, *before(s_log, b, 1))
                    pe.matmul(p_e[:, :], lhsT=wa[:, 0, :], rhs=hsT[b][:, :], start=True, stop=False)
                    pe.matmul(p_e[:, :], lhsT=wa[:, 1, :], rhs=hdT[b][:, :], start=False, stop=True)
                    pe.matmul(p_l[:, :], lhsT=wa[:, 0, :], rhs=hdT[b][:, :], start=True, stop=False)
                    pe.matmul(p_l[:, :], lhsT=wa[:, 1, :], rhs=hdT[b][:, :], start=False, stop=True).then_inc(s_logp, 1)

                def project_values(b):
                    wait_freed(pe, *before(s_own, b, 1))
                    pe.matmul(p_xs[:, :], lhsT=wgT[:, :], rhs=hsT[b][:, :], start=True, stop=True)
                    pe.matmul(p_xd[:, :], lhsT=wgT[:, :], rhs=hdT[b][:, :], start=True, stop=True).then_inc(s_xp, 1)

                def back(b):
                    pe.wait_ge(*this(s_elu, b))
                    wait_freed(pe, *before(s_rows, b, 1))
                    transpose_back(pe, p_back, elu_T, ident).then_inc(s_back, 1)

                pipeline(pe, EB, [(5, project_values), (3, project), (2, rows_T), (7, back)])

            @block.scalar
            def _(act):
                act.preload_act_table_set(LN_EXP)

                def evac_h(b):
                    wait_freed(act, *before(s_xp, b, RING))
                    act.wait_ge(*this(s_hsT, b))
                    act.copy(hsT[b][:, :], p_hs[:, :]).then_inc(s_hsc, 1)
                    act.wait_ge(*this(s_hdT, b))
                    act.copy(hdT[b][:, :], p_hd[:, :]).then_inc(s_hdc, 1)

                def resets(b):
                    wait_freed(act, *before(s_fall, b, 2))
                    act.activation(neg[b][:, :], edge_cols(same, b), ACT.Copy, bias=-NEG, scale=NEG).then_inc(s_neg, 1)

                def slopes(b):
                    wait_freed(act, *before(s_log, b, 1))
                    act.wait_ge(*this(s_logp, b))
                    act.activation(slow_e[:, :], p_e[:, :], ACT.Copy, scale=0.2)
                    act.activation(slow_l[:, :], p_l[:, :], ACT.Copy, scale=0.2).then_inc(s_slow, 1)

                def exps(b):
                    act.wait_ge(*this(s_diff, b))
                    wait_freed(act, *before(s_num, b, 2))
                    act.activation(w_e[b][:, :], d_e[b][:, :], ACT.Exp).then_inc(s_exp, 1)
                    act.activation(w_l[b][:, :], d_l[b][:, :], ACT.Exp).then_inc(s_exp, 1)
                    act.wait_ge(*this(s_fall, b))
                    act.activation(keep[b][:, :], fall[b][:, :], ACT.Exp).then_inc(s_exp, 1)

                def inverse(b):
                    act.wait_ge(*this(s_den, b))
                    wait_freed(act, *before(s_inv, b, 1))
                    act.activation(lden[:, :], den[b][:, :], ACT.Ln).then_inc(s_lden, 1)
                    act.wait_ge(*this(s_lden, b))
                    wait_freed(act, *before(s_mix, b, 1))
                    act.activation(inv[:, :], lden[:, :], ACT.Exp, scale=-1.0).then_inc(s_inv, 1)

                def low_exp(b):
                    act.wait_ge(*this(s_mix, b))
                    wait_freed(act, *before(s_ex, b, 1))
                    act.activation(low[:, :], mix[:, :], ACT.Relu, bias=nbias[:, :], scale=-1.0).then_inc(s_low, 1)
                    act.wait_ge(*this(s_low, b))
                    wait_freed(act, *before(s_elu, b, 2))
                    act.activation(ex[b][:, :], low[:, :], ACT.Exp, scale=-1.0).then_inc(s_ex, 1)

                act.wait_ge(s_spread, 3)
                pipeline(act, EB, [(6, inverse), (4, exps), (2, resets), (1, partial(norm_s.scalar_relu, act)),
                                   (1, partial(norm_d.scalar_relu, act)), (6, low_exp), (3, slopes), (0, partial(norm_s.scalar_rstd, act)),
                                   (0, partial(norm_d.scalar_rstd, act)), (2, evac_h)])

            @block.vector
            def _(dve):
                for x in (wsum[1], vsum[1], top[0], top[1]):
                    dve.memset(x[:, :], 0.0)
                dve.wait_ge(s_w, 80)
                for n in range(2):
                    dve.tensor_scalar(spread[:, n, :], k["blocks32"], att[:, n:n + 1], None, ALU.mult).then_inc(s_spread, 1)
                dve.tensor_scalar(nbias[:, :], bias[:, :], -1.0, None, ALU.mult).then_inc(s_spread, 1)
                dve.wait_ge(s_wa, 1)
                dve.tensor_copy(wa[:, :, :], p_e[:, 0:2 * D].rearrange("p (n c) -> p n c", n=2)).then_inc(s_wac, 1)
                dve.wait_ge(s_spread, 3)

                def logits(b):
                    dve.wait_ge(*this(s_slow, b))
                    wait_freed(dve, *before(s_diff, b, 1))
                    dve.tensor_tensor(log_e[:, :], p_e[:, :], slow_e[:, :], ALU.max)
                    dve.tensor_tensor(log_l[:, :], p_l[:, :], slow_l[:, :], ALU.max).then_inc(s_log, 1)
                    dve.wait_ge(*this(s_log, b))
                    wait_freed(dve, *before(s_top, b, 1))
                    dve.tensor_tensor(both[:, :], log_e[:, :], log_l[:, :], ALU.max).then_inc(s_both, 1)
                    dve.wait_ge(*this(s_both, b))
                    dve.wait_ge(*this(s_neg, b))
                    dve.tensor_tensor_scan(top[b][:, 1:BLK + 1], neg[b][:, :], both[:, :], top[b.back(1)][:, BLK:BLK + 1],
                                           ALU.add, ALU.max)
                    dve.tensor_copy(top[b][:, 0:1], top[b.back(1)][:, BLK:BLK + 1]).then_inc(s_top, 1)
                    dve.wait_ge(*this(s_top, b))
                    wait_freed(dve, *before(s_exp, b, 2, 3))
                    dve.tensor_tensor(d_e[b][:, :], log_e[:, :], top[b][:, 1:BLK + 1], ALU.subtract)
                    dve.tensor_tensor(d_l[b][:, :], log_l[:, :], top[b][:, 1:BLK + 1], ALU.subtract)
                    dve.tensor_tensor(fall[b][:, :], top[b][:, 0:BLK], top[b][:, 1:BLK + 1], ALU.subtract).then_inc(s_diff, 1)
                    dve.wait_ge(*this(s_diff, b))
                    dve.tensor_tensor(fall[b][:, :], fall[b][:, :], neg[b][:, :], ALU.add).then_inc(s_fall, 1)

                def sums(b):
                    dve.wait_ge(*this(s_xp, b))
                    dve.wait_ge(*this(s_exp, b, 3))
                    wait_freed(dve, *before(s_sums, b, 1))
                    dve.tensor_tensor(value[:, :], p_xs[:, :], w_e[b][:, :], ALU.mult).then_inc(s_val, 1)
                    dve.tensor_tensor_scan(wsum[b][:, :], keep[b][:, :], w_e[b][:, :], wsum[b.back(1)][:, BLK - 1:BLK], ALU.mult, ALU.add)
                    dve.tensor_tensor(own[:, :], p_xd[:, :], w_l[b][:, :], ALU.mult).then_inc(s_own, 1)
                    dve.wait_ge(*this(s_val, b))
                    dve.tensor_tensor_scan(vsum[b][:, :], keep[b][:, :], value[:, :], vsum[b.back(1)][:, BLK - 1:BLK],
                                           ALU.mult, ALU.add).then_inc(s_sums, 1)
                    dve.wait_ge(*this(s_sums, b))
                    wait_freed(dve, *before(s_lden, b, 2))
                    dve.scalar_tensor_tensor(den[b][:, :], wsum[b][:, :], 1e-16, w_l[b][:, :], ALU.add, ALU.add).then_inc(s_den, 1)
                    wait_freed(dve, *before(s_mix, b, 2))
                    dve.tensor_tensor(num[b][:, :], vsum[b][:, :], own[:, :], ALU.add).then_inc(s_num, 1)

                def output(b):
                    dve.wait_ge(*this(s_inv, b))
                    dve.wait_ge(*this(s_num, b))
                    wait_freed(dve, *before(s_ex, b, 1))
                    wait_freed(dve, *before(s_elu, b, 1))
                    wait_freed(dve, *before(s_part, b, 1))
                    dve.tensor_tensor(mix[:, :], num[b][:, :], inv[:, :], ALU.mult).then_inc(s_mix, 1)
                    dve.wait_ge(*this(s_mix, b))
                    dve.tensor_scalar(part[:, :], mix[:, :], bias[:, :], 0.0, ALU.add, ALU.max).then_inc(s_part, 1)

                def elu(b):
                    dve.wait_ge(*this(s_part, b))
                    dve.wait_ge(*this(s_ex, b))
                    wait_freed(dve, *before(s_back, b, 1))
                    dve.scalar_tensor_tensor(elu_T[:, :], ex[b][:, :], -1.0, part[:, :], ALU.add, ALU.add).then_inc(s_elu, 1)

                def add_rows(b):
                    dve.wait_ge(*this(s_back, b))
                    dve.wait_ge(*this(s_kept, b, 16))
                    wait_freed(dve, *before(s_put, b, RING, 64))
                    dve.tensor_tensor(rows[b][:, :, :], grouped(p_back[:, :]), kept_d[b][:, :, :], ALU.add).then_inc(s_rows, 1)

                pipeline(dve, EB, [(7, elu), (1, partial(norm_s.vector_shift, dve)), (1, partial(norm_d.vector_shift, dve)),
                                   (0, partial(norm_s.vector_stats, dve)), (0, partial(norm_d.vector_stats, dve)), (5, sums), (6, output),
                                   (3, logits), (7, add_rows)])


INPUTS = {
    "x": ("x", (N, D)), "A1": ("L0_gnn_A1", (8, 64)), "b1_0": ("L0_gnn_b1", (64,)), "A2": ("L0_gnn_A2", (64, 64)),
    "b2_0": ("L0_gnn_b2", (64,)), "A3": ("L0_gnn_A3", (64, D)), "W_up_s": ("L0_gnn_W_up_s", (MUL, MUL)),
    "W_up_v": ("L0_gnn_W_up_v", (MUL, MUL)), "W_out_s": ("L0_gnn_W_out_s", (2 * MUL, MUL)),
    "W_out_v": ("L0_gnn_W_out_v", (2 * MUL, MUL)), "Wq": ("L1_gnn_Wq", (D, D)), "Wk": ("L1_gnn_Wk", (D, D)),
    "Wv": ("L1_gnn_Wv", (D, D)), "Wo": ("L1_gnn_Wo", (D, D)), "bo": ("L1_gnn_bo", (D,)), "g1": ("L1_gnn_bn1_g", (D,)),
    "b1": ("L1_gnn_bn1_b", (D,)), "g2": ("L1_gnn_bn2_g", (D,)), "b2": ("L1_gnn_bn2_b", (D,)), "W1": ("L1_gnn_W1", (D, 2 * D)),
    "bf1": ("L1_gnn_b1", (2 * D,)), "W2": ("L1_gnn_W2", (2 * D, D)), "bf2": ("L1_gnn_b2", (D,)),
    "w0": ("L2_gnn_w0", (MUL, 1, MUL)), "w1": ("L2_gnn_w1", (MUL, 1, MUL)), "w2": ("L2_gnn_w2", (MUL, 1, MUL)),
    "w3": ("L2_gnn_w3", (MUL, 1, MUL)), "w4": ("L2_gnn_w4", (MUL, 1, MUL)), "Wg": ("L3_gnn_W", (D, D)),
    "att_src": ("L3_gnn_att_src", (1, HEADS3, D // HEADS3)), "att_dst": ("L3_gnn_att_dst", (1, HEADS3, D // HEADS3)),
    "bias": ("L3_gnn_bias", (D,)),
}


def build(nc, t, phases=None):
    with ExitStack() as ctx:
        def sb(name, shape, dt=F32):
            return ctx.enter_context(nc.sbuf_tensor(name, shape, dt))

        const, coef, eps = sb("const", [P, 3 * P]), sb("coef", [9, COEF]), sb("eps", [P, 1])
        k = {"const": const, "coef": coef, "eps": eps, "same": sb("same", [P, EP + 4], U8),
             "ident": const[:, 0:P], "blocks16": const[:, P:2 * P], "blocks32": const[:, 2 * P:3 * P],
             "node_stats": sb("node_stats", [P, NB, 6]), "node_mv": sb("node_mv", [P, 2]),
             "moved": sb("moved", [P, 2, EB])}
        for phase in (setup, layer0, stats, layer1, nodes, layer2, layer3)[:phases]:
            phase(nc, t, k)


def laid_out(inputs):
    arrays = {name: np.ascontiguousarray(inputs[key]) for name, (key, _) in INPUTS.items()}
    src, dst = np.asarray(inputs["src"]), np.asarray(inputs["dst"])
    tail = EP - E

    def by_partition(a):
        return np.ascontiguousarray(a.reshape(EB, P, G).transpose(1, 0, 2).reshape(P, EB * G))

    ext = np.concatenate([np.full(1, -1, dst.dtype), dst, np.full(tail, N, dst.dtype), np.full(1, N + 1, dst.dtype)])
    arrays["dst_ext"] = ext
    arrays["src_rows"] = by_partition(np.concatenate([src, np.zeros(tail, src.dtype)]))
    arrays["dst_rows"] = by_partition(ext[1:EP + 1])
    arrays["next_rows"] = by_partition(ext[2:EP + 2])

    def padded(a):
        a = np.asarray(a)
        return np.concatenate([a, np.zeros((tail, a.shape[1]), a.dtype)])

    arrays["edge4"] = padded(inputs["edge_attr_4"])
    arrays["edge8T"] = np.ascontiguousarray(padded(inputs["edge_attr_8"]).T)
    arrays["edge9T"] = np.ascontiguousarray(padded(inputs["edge_attr_9"]).T)
    arrays["WgT"] = np.ascontiguousarray(np.asarray(inputs["L3_gnn_W"]).T)
    arrays["shape_constants"] = shape_constants()
    arrays["trash_rows"] = trash_rows()
    arrays["coefficients"] = coefficient_matrix()
    return arrays


def make(nc, arrays, phases=None, debug=False):
    t = {name: nc.dram_tensor(f"in_{name}", a.shape, mybir.dt.from_np(a.dtype), kind="ExternalInput").ap()
         for name, a in arrays.items()}
    kind = "ExternalOutput" if debug else "Internal"
    for name, rows, cols, dt in (("X1", NT, D, F32), ("H2", NT, D, F32), ("X2", N, D, F32), ("X3", NT, D, F32),
                                 ("TPW", EP, D, F32), ("KEPT", EP, D, F32),
                                 ("INDEX", EB * P, 3 * G, I32)):
        t[name] = nc.dram_tensor(name, (rows, cols), dt, kind=kind).ap()
    t["out"] = nc.dram_tensor("out_0", (N, D), F32, kind="ExternalOutput").ap()
    build(nc, t, phases)


def kernel(**inputs):
    import concourse.bacc as bacc
    from concourse.bass_utils import run_bass_kernel_spmd

    nc = bacc.Bacc("TRN2", target_bir_lowering=False, num_devices=1)
    arrays = laid_out(inputs)
    make(nc, arrays)
    result = run_bass_kernel_spmd(nc, [{f"in_{name}": a for name, a in arrays.items()}], core_ids=[0])
    return result.results[0]["out_0"]
```

```python
import math
from contextlib import ExitStack
from functools import partial

import numpy as np

import concourse.bass as bass
from concourse import mybir

F32, I32, U8 = mybir.dt.float32, mybir.dt.int32, mybir.dt.uint8
ALU = mybir.AluOpType
ACT = mybir.ActivationFunctionType

N = 100000
E = 50000
D = 128
P = 128
G = 4
BLK = P * G
EB = -(-E // BLK)
EP = EB * BLK
NB = -(-N // BLK)
RING = 4
NEW = N - (NB - 1) * BLK
SPARE = 4
TRASH = 1 + SPARE * BLK
NT = N + TRASH
MUL = 32
HEADS1, HEADS3 = 8, 4
EPS = 1e-5
NEG = 1e30
LN_EXP = "natural_log_exp_and_others"
COEF = 17


def wigner_3j(l1, l2, l3):

    def f(n):
        return math.factorial(round(n))

    def su2(m1, m2, m3):
        vmin = int(max(-l1 + l2 + m3, -l1 + m1, 0))
        vmax = int(min(l2 + l3 + m1, l3 - l1 + l2, l3 + m3))
        c = ((2.0 * l3 + 1.0) * (
            f(l3 + l1 - l2) * f(l3 - l1 + l2) * f(l1 + l2 - l3) * f(l3 + m3) * f(l3 - m3) / (
            f(l1 + l2 + l3 + 1) * f(l1 - m1) * f(l1 + m1) * f(l2 - m2) * f(l2 + m2)))) ** 0.5
        s = 0
        for v in range(vmin, vmax + 1):
            s += (-1) ** (v + l2 + m2) * f(l2 + l3 + m1 - v) * f(l1 - m1 + v) / (
                f(v) * f(l3 - l1 + l2 - v) * f(l3 + m3 - v) * f(v + l1 - l2 - m3))
        return float(c * s)

    def real(l):
        q = np.zeros((2 * l + 1, 2 * l + 1), np.complex128)
        for m in range(-l, 0):
            q[l + m, l + abs(m)] = 1 / np.sqrt(2)
            q[l + m, l - abs(m)] = -1j / np.sqrt(2)
        q[l, l] = 1
        for m in range(1, l + 1):
            q[l + m, l + abs(m)] = (-1) ** m / np.sqrt(2)
            q[l + m, l - abs(m)] = 1j * (-1) ** m / np.sqrt(2)
        return (-1j) ** l * q

    c = np.zeros((2 * l1 + 1, 2 * l2 + 1, 2 * l3 + 1))
    for m1 in range(-l1, l1 + 1):
        for m2 in range(-l2, l2 + 1):
            if abs(m1 + m2) <= l3:
                c[l1 + m1, l2 + m2, l3 + m1 + m2] = su2(m1, m2, m1 + m2)
    r = np.real(np.einsum("ij,kl,mn,ikn->jlm", real(l1), real(l2), np.conj(real(l3).T), c.astype(np.complex128)))
    return r / np.linalg.norm(r)


def coefficient_matrix():
    n0, n1 = np.sqrt(1.0 / (2 * MUL)), np.sqrt(3.0 / (3 * MUL))
    down = 1.0 / np.sqrt(10.0)
    c = np.zeros((9, COEF))
    c[0, 0] = wigner_3j(0, 0, 0)[0, 0, 0] * n0
    c[1:4, 1:4] = wigner_3j(1, 1, 0)[:, :, 0].T * n0
    c[1:4, 4:7] = wigner_3j(0, 1, 1)[0] * n1
    keep = wigner_3j(1, 0, 1)[:, 0, :]
    assert np.allclose(keep, keep[0, 0] * np.eye(3))
    c[0, 7] = keep[0, 0] * n1
    c[4:9, 8:17] = wigner_3j(1, 2, 1).transpose(1, 0, 2).reshape(5, 9) * n1
    return (c * down).astype(np.float32)


def shape_constants():
    p = np.arange(P)
    h16, h32 = D // HEADS1, D // HEADS3
    blocks16 = (p[:, None] // h16 == p[None] // h16) / np.sqrt(h16)
    blocks32 = p[:, None] // h32 == p[None] // h32
    return np.concatenate([np.eye(P), blocks16, blocks32], 1).astype(np.float32)


def trash_rows():
    b, p, g = np.ogrid[:EB, :P, :G]
    return (N + 1 + b % SPARE * BLK + p * G + g).transpose(1, 0, 2).reshape(P, EB * G).astype(np.float32)


class Blk:

    def __init__(self, turn, at):
        self.turn, self.at = turn, at
        self.num = at if turn is None else turn * RING + at

    def back(self, n):
        return Blk(self.turn, self.at - n)


class Ring(list):

    def __getitem__(self, b):
        return list.__getitem__(self, (b.at if isinstance(b, Blk) else b) % len(self))


def this(sem, b, per=1):
    if isinstance(sem, Ring):
        turns = b.at // RING + 1
        return sem[b], turns * per if b.turn is None else b.turn * per + turns * per
    return sem, (b.at + 1) * per if b.turn is None else b.turn * (RING * per) + (b.at + 1) * per


def before(sem, b, n, per=1):
    return this(sem, b.back(n), per)


def wait_freed(eng, sem, count):
    if isinstance(count, int) and count <= 0:
        return
    eng.wait_ge(sem, count)


def wait_all(eng, ring, blocks, per):
    for c in range(RING):
        eng.wait_ge(ring[c], len(range(c, blocks, RING)) * per)


def pipeline(eng, blocks, stages):
    ahead = min(lag for lag, _ in stages)
    deepest = max(lag for lag, _ in stages) - ahead

    def step(turn, n):
        for lag, work in stages:
            at = n - lag + ahead
            if turn is not None or 0 <= at < blocks:
                work(Blk(turn, at))

    first, end = -(-(deepest + RING) // RING), (blocks - 1) // RING
    for n in range(first * RING):
        step(None, n)
    with eng.Fori(first, end) as turn:
        for n in range(RING):
            step(turn, n)
    for n in range(end * RING, blocks + deepest):
        step(None, n)


class Phase:

    def __init__(self, nc, name):
        self.nc, self.name, self.ctx, self.sems = nc, name, ExitStack(), []

    def __enter__(self):
        return self

    def __exit__(self, *exc):
        if exc[0] is None:
            self.nc.clear_and_free_semaphores(self.sems)
            self.nc.all_engine_barrier()
            self.ctx.close()

    def sem(self, name):
        self.sems.append(self.nc.alloc_semaphore(f"{self.name}_{name}"))
        return self.sems[-1]

    def dma(self, name):
        return Ring(self.sem(f"{name}{c}") for c in range(RING))

    def sb(self, name, shape, dt=F32):
        return self.ctx.enter_context(self.nc.sbuf_tensor(f"{self.name}_{name}", shape, dt))

    def ring(self, name, shape, dt=F32, depth=4):
        return Ring(self.sb(f"{name}{c}", shape, dt) for c in range(depth))

    def ps(self, name):
        return self.ctx.enter_context(self.nc.psum_tensor(f"{self.name}_{name}", [P, BLK], F32))

    def ps_ring(self, name, depth=2):
        return Ring(self.ps(f"{name}{c}") for c in range(depth))

    def block(self):
        return self.nc.Block()


def edge_rows(table, b):
    return table[bass.ds(b.num * BLK, BLK), :].rearrange("(p g) c -> p g c", g=G)


def double_rows(table, b):
    return table[bass.ds(b.num * (2 * BLK), 2 * BLK), :].rearrange("(h p g) c -> p h g c", h=2, g=G)


def node_rows(table, b):
    at = b.num * BLK
    if isinstance(at, int) and at + BLK > N:
        at = N - BLK
    return table[bass.ds(at, BLK), :].rearrange("(p g) c -> p g c", g=G)


def is_last_node_block(b):
    return b.turn is None and b.at == NB - 1


def grouped(t):
    return t.rearrange("p (g c) -> p g c", g=G)


class Norm:

    def __init__(self, ph, k, name, raw, raw_ready, ready_per, eps, h_free, depth=RING):
        self.k, self.raw, self.raw_ready, self.per, self.eps, self.h_free, self.depth = k, raw, raw_ready, ready_per, eps, h_free, depth
        self.stats = ph.ring(f"{name}_stats", [P, G, 6])
        self.mv = ph.ring(f"{name}_mv", [P, G, 2])
        self.ln = ph.ring(f"{name}_ln", [P, G, 1])
        self.rstd = ph.ring(f"{name}_rstd", [P, G, 1])
        self.shift = ph.ring(f"{name}_shift", [P, G, 1])
        self.h = ph.ring(f"{name}_h", [P, G, D], depth=depth)
        self.s_turn = ph.sem(f"{name}_vector_goes_on")
        self.s_stats = ph.sem(f"{name}_stats_done")
        self.s_mv = ph.sem(f"{name}_mean_var_done")
        self.s_ln = ph.sem(f"{name}_log_done")
        self.s_rstd = ph.sem(f"{name}_rstd_done")
        self.s_shift = ph.sem(f"{name}_shift_done")
        self.s_h = ph.sem(f"{name}_h_done")

    def vector_stats(self, dve, b):
        if self.raw_ready is not None:
            dve.wait_ge(*this(self.raw_ready, b, self.per))
        for g in range(G):
            last = dve.bn_stats(self.stats[b][:, g, :], self.raw[b][:, g, :])
        last.then_inc(self.s_stats, 1)

    def vector_aggregate(self, dve, b):
        dve.wait_ge(*this(self.s_stats, b))
        wait_freed(dve, *before(self.s_h, b, RING))
        dve.sem_inc(self.s_turn, 1)
        for g in range(G):
            last = dve.bn_aggr(self.mv[b][:, g, :], self.stats[b][:, g, :])
        last.then_inc(self.s_mv, 1)

    def scalar_log(self, act, b):
        act.wait_ge(*this(self.s_mv, b))
        act.activation(self.ln[b][:, :, :], self.mv[b][:, :, 1:2], ACT.Ln, bias=self.eps).then_inc(self.s_ln, 1)

    def scalar_rstd(self, act, b):
        act.wait_ge(*this(self.s_ln, b))
        act.activation(self.rstd[b][:, :, :], self.ln[b][:, :, :], ACT.Exp, scale=-0.5).then_inc(self.s_rstd, 1)

    def vector_shift(self, dve, b):
        dve.wait_ge(*this(self.s_rstd, b))
        dve.scalar_tensor_tensor(self.shift[b][:, :, 0], self.mv[b][:, :, 0], -1.0, self.rstd[b][:, :, 0],
                                 ALU.mult, ALU.mult).then_inc(self.s_shift, 1)

    def scalar_relu(self, act, b):
        act.wait_ge(*this(self.s_shift, b))
        wait_freed(act, *before(self.h_free, b, self.depth))
        for g in range(G):
            last = act.activation(self.h[b][:, g, :], self.raw[b][:, g, :], ACT.Relu,
                                  bias=self.shift[b][:, g, :], scale=self.rstd[b][:, g, :])
        last.then_inc(self.s_h, 1)


def transpose_rows(pe, out, rows, ident, in_order):
    for g in range(G):
        o = out[:, g:BLK:G] if in_order else out[:, g * P:(g + 1) * P]
        last = pe.transpose(o, rows[:, g, :], ident)
    return last


def transpose_back(pe, out, cols, ident):
    for g in range(G):
        last = pe.transpose(out[:, g * P:(g + 1) * P], cols[:, g:BLK:G], ident)
    return last


def indexed_gather(pool, out, table, index, landed, rows):
    for g in range(G):
        pool.indirect_dma_start(out[:, g, :], None, table, bass.IndirectOffsetOnAxis(ap=index[:, g:g + 1], axis=0),
                                bounds_check=rows - 1, oob_is_err=False).then_inc(landed, 16)


def indexed_add(pool, table, index, rows, landed):
    for g in range(G):
        pool.indirect_dma_start(table, bass.IndirectOffsetOnAxis(ap=index[:, g:g + 1], axis=0), rows[:, g, :], None,
                                compute_op=ALU.add).then_inc(landed, 16)


def indexed_write(pool, table, index, rows, landed, bound):
    for g in range(G):
        pool.indirect_dma_start(table, bass.IndirectOffsetOnAxis(ap=index[:, g:g + 1], axis=0), rows[:, g, :], None,
                                bounds_check=bound, oob_is_err=False).then_inc(landed, 16)


def bc(ap, axis, n):
    a = ap.unsqueeze(axis)
    shape = list(a.shape)
    shape[axis] = n
    return a.to_broadcast(shape)


def setup(nc, t, k):
    with Phase(nc, "setup") as ph:
        dst_all = ph.ring("dst_all", [P, 2 * BLK + 1], I32)
        idx = ph.ring("idx", [P, 2, G], I32)
        xs = ph.ring("xs", [P, 2, G, D])
        rows = ph.sb("rows", [P, 3, EB, G], I32)
        inner = ph.sb("inner", [P, EB, G])
        away, trash = ph.sb("away", [P, EB, G]), ph.sb("trash", [P, EB, G])
        table = ph.sb("table", [P, EB, 3, G], I32)
        zeros = ph.sb("zeros", [P, SPARE * G * D])
        a1, a2, a3 = ph.sb("a1", [16, P]), ph.sb("a2", [P, P]), ph.sb("a3", [P, D])
        b1, b2 = ph.sb("b1", [P, 1]), ph.sb("b2", [P, 1])
        ef = ph.ring("ef", [16, BLK])
        m1 = ph.ring("m1", [P, BLK])
        m2 = ph.ring("m2", [P, BLK])
        tp = ph.ring("tp", [P, 2, G, D])
        p1 = ph.ps_ring("p1")
        p2 = ph.ps_ring("p2")
        p3 = Ring([ph.ps(f"p3{c}{half}") for half in range(2)] for c in range(2))
        s_const, s_rows, s_w = ph.sem("constants_loaded"), ph.sem("rows_loaded"), ph.sem("mlp_weights_loaded")
        s_zero, s_z0, s_copy = ph.sem("zeros_made"), ph.sem("trash_cleared"), ph.dma("x_copied")
        s_inner, s_table, s_tabled = ph.sem("index_steps"), ph.sem("index_table_made"), ph.sem("index_table_stored")
        s_idx, s_xs, s_xss = ph.dma("src_loaded"), ph.dma("x_gathered"), ph.dma("x_rows_stored")
        s_dst, s_mask = ph.dma("dst_loaded"), ph.sem("mask_made")
        s_ef, s_p1, s_m1 = ph.dma("edge_feats_loaded"), ph.sem("mlp1_done"), ph.sem("silu1_done")
        s_p2, s_m2, s_p3 = ph.sem("mlp2_done"), ph.sem("silu2_done"), ph.sem("mlp3_done")
        s_tp, s_tps = ph.sem("tpw_ready"), ph.dma("tpw_stored")
        s_pool_turn, s_turn, s_w0 = ph.sem("pool_goes_on"), ph.sem("tensor_goes_on"), ph.sem("mlp_weights_cleared")
        DB = EB // 2
        assert EB % 2 == 0

        with ph.block() as block:
            @block.sync
            def _(sp):
                sp.wait_ge(s_w0, 2)
                for h in range(2):
                    half = slice(h * 64, (h + 1) * 64)
                    for dst, src in ((a1[8 * h:8 * (h + 1), half], t["A1"]), (a2[half, half], t["A2"]),
                                     (a3[half, :], t["A3"]), (b1[half, :], column(t["b1_0"])),
                                     (b2[half, :], column(t["b2_0"]))):
                        sp.dma_start(dst, src).then_inc(s_w, 16)
                for dst, src in ((k["const"][:, :], t["shape_constants"]), (k["coef"][:, :], t["coefficients"]),
                                 (trash[:, :, :], t["trash_rows"].rearrange("p (b g) -> p b g", g=G))):
                    sp.dma_start(dst, src).then_inc(s_const, 16)
                for n, name in enumerate(("src_rows", "dst_rows", "next_rows")):
                    sp.dma_start(rows[:, n, :, :], t[name].rearrange("p (b g) -> p b g", g=G)).then_inc(s_rows, 16)

                def load(b):
                    wait_freed(sp, *before(s_p1, b, RING))
                    sp.dma_start(ef[b][:, :], t["edge8T"][:, bass.ds(b.num * BLK, BLK)]).then_inc(s_ef[b], 16)

                def store(b):
                    sp.wait_ge(*this(s_tp, b))
                    sp.dma_start(double_rows(t["TPW"], b), tp[b][:, :, :, :]).then_inc(s_tps[b], 16)

                def load_dst(b):
                    wait_freed(sp, *before(s_mask, b, RING))
                    sp.dma_start(dst_all[b][:, :], t["dst_ext"][bass.ds(b.num * (2 * BLK), 2 * BLK + 1)].partition_broadcast(P)
                                 ).then_inc(s_dst[b], 16)

                def load_index(b):
                    wait_freed(sp, *before(s_xs, b, RING, 2 * G * 16))
                    sp.dma_start(idx[b][:, :, :].rearrange("p h g -> p (h g)"), t["src_rows"][:, bass.ds(b.num * (2 * G), 2 * G)]
                                 ).then_inc(s_idx[b], 16)

                def copy_x(b):
                    at = b.num * (2 * 2 * BLK)
                    rows_here = min(2 * 2 * BLK, N - at) if isinstance(at, int) else 2 * 2 * BLK
                    sp.dma_start(t["X1"][bass.ds(at, rows_here), :], t["x"][bass.ds(at, rows_here), :]).then_inc(s_copy[b], 16)

                def store_gathered(b):
                    sp.wait_ge(*this(s_xs, b, 2 * G * 16))
                    sp.dma_start(double_rows(t["XS"], b), xs[b][:, :, :, :]).then_inc(s_xss[b], 16)

                assert (DB - 1) * 2 * 2 * BLK < N <= DB * 2 * 2 * BLK
                pipeline(sp, DB, [(0, load_index), (0, load), (0, load_dst), (0, copy_x), (3, store_gathered),
                                  (5, store)])
                wait_all(sp, s_copy, DB, 16)
                wait_all(sp, s_xss, DB, 16)
                wait_all(sp, s_tps, DB, 16)
                sp.wait_ge(s_table, 1)
                sp.dma_start(t["INDEX"].rearrange("(b p) c -> p b c", p=P),
                             table[:, :, :, :].rearrange("p b n g -> p b (n g)")).then_inc(s_tabled, 16)
                sp.wait_ge(s_tabled, 16)

            @block.gpsimd
            def _(pool):
                pool.memset(zeros[:, :], 0.0).then_inc(s_zero, 1)
                pool.wait_ge(s_zero, 1)
                for name in ("X1", "X3", "H2"):
                    pool.dma_start(t[name][N:N + 1, :], zeros[0:1, 0:D]).then_inc(s_z0, 16)
                    pool.dma_start(t[name][N + 1:NT, :].rearrange("(p g) c -> p (g c)", p=P), zeros[:, :]).then_inc(s_z0, 16)

                def gather(b):
                    pool.wait_ge(*this(s_idx, b, 16))
                    wait_freed(pool, *before(s_xss, b, RING, 16))
                    pool.sem_inc(s_pool_turn, 1)
                    for h in range(2):
                        indexed_gather(pool, xs[b][:, h, :, :], t["x"], idx[b][:, h, :], s_xs[b], N)

                pipeline(pool, DB, [(0, gather)])
                pool.wait_ge(s_z0, 96)

            @block.tensor
            def _(pe):
                pe.wait_ge(s_w, 160)

                def first(b):
                    pe.wait_ge(*this(s_ef, b, 16))
                    wait_freed(pe, *before(s_m1, b, 2))
                    pe.matmul(p1[b][:, :], lhsT=a1[:, :], rhs=ef[b][:, :], start=True, stop=True).then_inc(s_p1, 1)

                def second(b):
                    pe.wait_ge(*this(s_m1, b))
                    wait_freed(pe, *before(s_m2, b, 2))
                    pe.sem_inc(s_turn, 1)
                    pe.matmul(p2[b][:, :], lhsT=a2[:, :], rhs=m1[b][:, :], start=True, stop=True).then_inc(s_p2, 1)

                def third(b):
                    pe.wait_ge(*this(s_m2, b))
                    wait_freed(pe, *before(s_tp, b, 2))
                    for h in range(2):
                        for g in range(G):
                            last = pe.matmul(p3[b][h][:, g * P:(g + 1) * P], lhsT=m2[b][h * 64:(h + 1) * 64, g:BLK:G],
                                             rhs=a3[h * 64:(h + 1) * 64, :], start=True, stop=True)
                    last.then_inc(s_p3, 1)

                pipeline(pe, DB, [(0, first), (1, second), (2, third)])

            @block.scalar
            def _(act):
                act.preload_act_table(ACT.Silu)
                act.wait_ge(s_w, 160)

                def silu1(b):
                    act.wait_ge(*this(s_p1, b))
                    wait_freed(act, *before(s_p2, b, RING))
                    act.activation(m1[b][:, :], p1[b][:, :], ACT.Silu, bias=b1[:, :]).then_inc(s_m1, 1)

                def silu2(b):
                    act.wait_ge(*this(s_p2, b))
                    wait_freed(act, *before(s_p3, b, RING))
                    act.activation(m2[b][:, :], p2[b][:, :], ACT.Silu, bias=b2[:, :]).then_inc(s_m2, 1)

                def evacuate(b):
                    act.wait_ge(*this(s_p3, b))
                    wait_freed(act, *before(s_tps, b, RING, 16))
                    for h in range(2):
                        last = act.copy(tp[b][:, h, :, :], grouped(p3[b][h][:, :]))
                    last.then_inc(s_tp, 1)

                pipeline(act, DB, [(0, silu1), (1, silu2), (2, evacuate)])

            @block.vector
            def _(dve):
                dve.memset(a1[:, :], 0.0).then_inc(s_w0, 1)
                dve.memset(a2[:, :], 0.0).then_inc(s_w0, 1)
                dve.memset(k["eps"][:, :], EPS)
                dve.memset(k["same"][:, EP:EP + 1], 1)
                dve.wait_ge(s_const, 48)
                dve.wait_ge(s_rows, 48)
                dve.tensor_copy(away[:, :, :], rows[:, 1, :, :]).then_inc(s_inner, 1)
                dve.tensor_tensor(inner[:, :, :], rows[:, 1, :, :], rows[:, 2, :, :], ALU.is_equal).then_inc(s_inner, 1)
                dve.tensor_copy(table[:, :, 0, :], rows[:, 0, :, :])
                dve.tensor_copy(table[:, :, 1, :], rows[:, 1, :, :])
                dve.wait_ge(s_inner, 2)
                dve.tensor_tensor(away[:, :, :], trash[:, :, :], away[:, :, :], ALU.subtract).then_inc(s_inner, 1)
                dve.wait_ge(s_inner, 3)
                dve.tensor_tensor(away[:, :, :], away[:, :, :], inner[:, :, :], ALU.mult).then_inc(s_inner, 1)
                dve.wait_ge(s_inner, 4)
                dve.tensor_tensor(table[:, :, 2, :], away[:, :, :], rows[:, 1, :, :], ALU.add).then_inc(s_table, 1)

                def mask(b):
                    dve.wait_ge(*this(s_dst, b, 16))
                    dve.tensor_tensor(k["same"][:, bass.ds(b.num * (2 * BLK), 2 * BLK)], dst_all[b][:, 1:2 * BLK + 1],
                                      dst_all[b][:, 0:2 * BLK], ALU.is_equal).then_inc(s_mask, 1)

                pipeline(dve, DB, [(0, mask)])


def layer0(nc, t, k):
    ident, same = k["ident"], k["same"]
    with Phase(nc, "layer0") as ph:
        w_up = ph.sb("w_up", [D, D])
        w_out = ph.sb("w_out", [D, 2, D])
        end = ph.ring("end", [P, G], I32)
        attr = ph.ring("attr", [P, G, 4])
        tpw = ph.ring("tpw", [P, G, 4, MUL])
        raw = ph.ring("raw", [P, G, D])
        hT = ph.ring("hT", [P, BLK])
        w0y, w2y, q1, dot = (ph.sb(n, [P, G, MUL]) for n in ("w0y", "w2y", "q1", "dot"))
        vy = ph.sb("vy", [P, G, 3, MUL])
        feat = ph.ring("feat", [P, G, 8, MUL])
        featT = ph.ring("featT", [P, 2, BLK])
        total = ph.ring("total", [P, BLK])
        rows = ph.ring("rows", [P, G, D])
        p_h, p_f0, p_f1, p_back = (ph.ps(n) for n in ("p_h", "p_f0", "p_f1", "p_back"))
        p_up, p_out = ph.ps_ring("p_up"), ph.ps_ring("p_out")
        p_f = [p_f0, p_f1]

        s_w0, s_w, s_wr = ph.sem("weights_cleared"), ph.sem("weights_loaded"), ph.sem("weights_ready")
        s_end, s_edge = ph.dma("end_loaded"), ph.dma("edge_data_loaded")
        s_raw, s_add, s_turn = ph.dma("x_rows_loaded"), ph.dma("rows_added"), ph.sem("pool_goes_on")
        s_hT, s_hTc = ph.sem("h_transposed"), ph.sem("hT_ready")
        s_up, s_first, s_mid, s_part, s_dot, s_feat = (ph.sem(n) for n in (
            "up_done", "products1_done", "products2_done", "dot_part_done", "dot_done", "features_done"))
        s_fT, s_fTc, s_out, s_total = (ph.sem(n) for n in (
            "features_transposed", "featT_ready", "out_done", "totals_done"))
        s_back, s_rows = ph.sem("totals_transposed"), ph.sem("rows_ready")
        norm = Norm(ph, k, "norm", raw, s_raw, 16, k["eps"][:, :], s_hT)

        with ph.block() as block:
            @block.sync
            def _(sp):
                sp.wait_ge(s_w0, 1)
                with nc.allow_non_contiguous_dma(reason="weights laid out by component"):
                    sp.dma_start(w_up[0:MUL, 0:MUL], t["W_up_s"]).then_inc(s_w, 16)
                    for c in range(3):
                        sp.dma_start(w_up[MUL + c:D:3, MUL * (c + 1):MUL * (c + 2)], t["W_up_v"]).then_inc(s_w, 16)
                    sp.dma_start(w_out[0:64, 0, 0:MUL], t["W_out_s"]).then_inc(s_w, 16)
                    sp.dma_start(w_out[64:128, 0, MUL:D:3], t["W_out_v"]).then_inc(s_w, 16)
                    sp.dma_start(w_out[0:64, 1, MUL + 1:D:3], t["W_out_v"]).then_inc(s_w, 16)
                    sp.dma_start(w_out[64:128, 1, MUL + 2:D:3], t["W_out_v"]).then_inc(s_w, 16)

                def load(b):
                    wait_freed(sp, *before(norm.s_h, b, RING))
                    sp.dma_start(raw[b][:, :, :], edge_rows(t["XS"], b)).then_inc(s_raw[b], 16)

                def edge(b):
                    wait_freed(sp, *before(s_feat, b, RING))
                    sp.dma_start(attr[b][:, :, :], edge_rows(t["edge4"], b)).then_inc(s_edge[b], 16)
                    sp.dma_start(tpw[b][:, :, :, :].rearrange("p g a b -> p g (a b)"), edge_rows(t["TPW"], b)
                                 ).then_inc(s_edge[b], 16)

                def ends(b):
                    wait_freed(sp, *before(s_add, b, RING, 64))
                    sp.dma_start(end[b][:, :], block_index(t, b)[:, 2 * G:3 * G]).then_inc(s_end[b], 16)

                pipeline(sp, EB, [(0, load), (2, edge), (7, ends)])

            @block.gpsimd
            def _(pool):
                def scatter(b):
                    pool.wait_ge(*this(s_end, b, 16))
                    pool.wait_ge(*this(s_rows, b))
                    pool.sem_inc(s_turn, 1)
                    indexed_add(pool, t["X1"], end[b], rows[b], s_add[b])

                pipeline(pool, EB, [(0, scatter)])
                wait_all(pool, s_add, EB, 64)

            @block.tensor
            def _(pe):
                pe.wait_ge(s_wr, 2)

                def up(b):
                    pe.wait_ge(*this(s_hTc, b))
                    wait_freed(pe, *before(s_feat, b, 2))
                    for g in range(G):
                        last = pe.matmul(p_up[b][:, g * P:(g + 1) * P], lhsT=hT[b][:, g * P:(g + 1) * P], rhs=w_up[:, :],
                                         start=True, stop=True)
                    last.then_inc(s_up, 1)

                def features(b):
                    pe.wait_ge(*this(s_feat, b))
                    wait_freed(pe, *before(s_fTc, b, 1))
                    for c in range(2):
                        last = transpose_rows(pe, p_f[c], feat[b][:, :, 4 * c:4 * c + 4, :].rearrange("p g a b -> p g (a b)"),
                                              ident, True)
                    last.then_inc(s_fT, 1)

                def rows_T(b):
                    pe.wait_ge(*this(norm.s_h, b))
                    wait_freed(pe, *before(s_hTc, b, 1))
                    transpose_rows(pe, p_h, norm.h[b], ident, False).then_inc(s_hT, 1)

                def out(b):
                    pe.wait_ge(*this(s_fTc, b))
                    wait_freed(pe, *before(s_total, b, 2))
                    for c in range(2):
                        last = pe.matmul(p_out[b][:, :], lhsT=w_out[:, c, :], rhs=featT[b][:, c, :], start=(c == 0), stop=(c == 1))
                    last.then_inc(s_out, 1)

                def back(b):
                    pe.wait_ge(*this(s_total, b))
                    wait_freed(pe, *before(s_rows, b, 1))
                    transpose_back(pe, p_back, total[b], ident).then_inc(s_back, 1)

                pipeline(pe, EB, [(3, up), (5, out), (2, rows_T), (4, features), (6, back)])

            @block.scalar
            def _(act):
                act.preload_act_table_set(LN_EXP)

                def evac_h(b):
                    act.wait_ge(*this(s_hT, b))
                    wait_freed(act, *before(s_up, b, RING))
                    act.copy(hT[b][:, :], p_h[:, :]).then_inc(s_hTc, 1)

                def evac_features(b):
                    act.wait_ge(*this(s_fT, b))
                    wait_freed(act, *before(s_out, b, RING))
                    act.copy(featT[b][:, 0, :], p_f0[:, :])
                    act.copy(featT[b][:, 1, :], p_f1[:, :]).then_inc(s_fTc, 1)

                def evac_rows(b):
                    act.wait_ge(*this(s_back, b))
                    wait_freed(act, *before(s_add, b, RING, 64))
                    act.copy(rows[b][:, :, :], grouped(p_back[:, :])).then_inc(s_rows, 1)

                pipeline(act, EB, [(0, partial(norm.scalar_log, act)), (1, partial(norm.scalar_relu, act)),
                                   (0, partial(norm.scalar_rstd, act)), (2, evac_h), (4, evac_features),
                                   (6, evac_rows)])

            @block.vector
            def _(dve):
                s_z = s_w0
                dve.memset(w_up[:, :], 0.0)
                dve.memset(total[RING - 1][:, :], 0.0)
                dve.memset(w_out[:, :, :], 0.0).then_inc(s_z, 1)
                dve.wait_ge(s_w, 128)
                dve.tensor_scalar_mul(w_up[:, :], w_up[:, :], float(1.0 / np.sqrt(MUL))).then_inc(s_wr, 1)
                dve.tensor_scalar_mul(w_out[:, :, :], w_out[:, :, :], float(0.1 / np.sqrt(2 * MUL))).then_inc(s_z, 1)
                dve.wait_ge(s_z, 2)
                dve.tensor_scalar_mul(w_out[MUL:2 * MUL, 0, :], w_out[MUL:2 * MUL, 0, :], float(1.0 / np.sqrt(3.0))
                                      ).then_inc(s_wr, 1)

                def products(b):
                    dve.wait_ge(*this(s_edge, b, 32))
                    wait_freed(dve, *before(s_feat, b, 1))
                    y = attr[b]
                    up = grouped(p_up[b][:, :])
                    vec = up[:, :, MUL:D].rearrange("p g (i c) -> p g i c", i=3)
                    yv = bc(y[:, :, 1:4], 3, MUL)
                    dve.tensor_tensor(w0y[:, :, :], tpw[b][:, :, 0, :], y[:, :, 0:1].to_broadcast([P, G, MUL]), ALU.mult)
                    dve.tensor_tensor(w2y[:, :, :], tpw[b][:, :, 2, :], y[:, :, 0:1].to_broadcast([P, G, MUL]), ALU.mult)
                    dve.wait_ge(*this(s_up, b))
                    dve.tensor_tensor(q1[:, :, :], up[:, :, 0:MUL], tpw[b][:, :, 1, :], ALU.mult)
                    dve.tensor_tensor(vy[:, :, :, :], vec, yv, ALU.mult).then_inc(s_first, 1)
                    dve.wait_ge(*this(s_first, b))
                    wait_freed(dve, *before(s_fT, b, RING))
                    dve.tensor_tensor(dot[:, :, :], vy[:, :, 0, :], vy[:, :, 1, :], ALU.add).then_inc(s_part, 1)
                    dve.tensor_tensor(feat[b][:, :, 0, :], up[:, :, 0:MUL], w0y[:, :, :], ALU.mult)
                    dve.wait_ge(*this(s_part, b))
                    dve.tensor_tensor(dot[:, :, :], dot[:, :, :], vy[:, :, 2, :], ALU.add).then_inc(s_mid, 1)
                    dve.tensor_tensor(feat[b][:, :, 2:8:2, :], bc(q1[:, :, :], 2, 3), yv, ALU.mult)
                    dve.tensor_tensor(feat[b][:, :, 3:8:2, :], vec, bc(w2y[:, :, :], 2, 3), ALU.mult)
                    dve.wait_ge(*this(s_mid, b))
                    dve.tensor_tensor(feat[b][:, :, 1, :], dot[:, :, :], tpw[b][:, :, 3, :], ALU.mult).then_inc(s_feat, 1)

                def sums(b):
                    dve.wait_ge(*this(s_out, b))
                    wait_freed(dve, *before(s_total, b, 1))
                    wait_freed(dve, *before(s_back, b, RING))
                    dve.tensor_tensor_scan(total[b][:, :], edge_cols(same, b), p_out[b][:, :], total[b.back(1)][:, BLK - 1:BLK],
                                           ALU.mult, ALU.add).then_inc(s_total, 1)

                dve.wait_ge(s_z, 2)
                pipeline(dve, EB, [(0, partial(norm.vector_stats, dve)), (1, partial(norm.vector_shift, dve)),
                                   (0, partial(norm.vector_aggregate, dve)), (3, products), (5, sums)])


def block_index(t, b):
    return t["INDEX"][bass.ds(b.num * P, P), :]


def edge_cols(cols, b):
    return cols[:, bass.ds(b.num * BLK, BLK)]


def stats(nc, t, k):
    with Phase(nc, "stats") as ph:
        raw = ph.ring("raw", [P, G, D])
        p_h = ph.ps_ring("p_h", 4)
        s_raw, s_hT, s_bn, s_store = ph.dma("x1_loaded"), ph.sem("h_transposed"), ph.sem("columns_counted"), ph.dma("h_stored")
        norm = Norm(ph, k, "norm", raw, s_raw, 16, k["eps"][:, :], s_hT)
        s_aggr = ph.sem("node_mv_done")
        HG = G // 2
        EDGES = P * HG
        assert NB * EDGES == EP
        idx, xd = ph.ring("idx", [P, HG], I32), ph.ring("xd", [P, HG, D])
        s_idx, s_xd, s_xds, s_turn = ph.dma("dst_loaded"), ph.dma("x1_gathered"), ph.dma("x1_rows_stored"), ph.sem("pool_goes_on")

        with ph.block() as block:
            @block.sync
            def _(sp):
                def load(b):
                    wait_freed(sp, *before(norm.s_h, b, RING))
                    sp.dma_start(raw[b][:, :, :], node_rows(t["X1"], b)).then_inc(s_raw[b], 16)

                def store(b):
                    sp.wait_ge(*this(norm.s_h, b))
                    if is_last_node_block(b):
                        wait_freed(sp, *before(s_store, b, 1, 16))
                    sp.dma_start(node_rows(t["H2"], b), norm.h[b][:, :, :]).then_inc(s_store[b], 16)

                def load_index(b):
                    wait_freed(sp, *before(s_xd, b, RING, HG * 16))
                    sp.dma_start(idx[b][:, :], t["dst_ext"][bass.ds(b.num * EDGES + 1, EDGES)].rearrange("(p g) -> p g", g=HG)
                                 ).then_inc(s_idx[b], 16)

                def store_gathered(b):
                    sp.wait_ge(*this(s_xd, b, HG * 16))
                    sp.dma_start(t["XD"][bass.ds(b.num * EDGES, EDGES), :].rearrange("(p g) c -> p g c", g=HG), xd[b][:, :, :]
                                 ).then_inc(s_xds[b], 16)

                pipeline(sp, NB, [(0, load_index), (0, load), (3, store_gathered), (5, store)])
                wait_all(sp, s_xds, NB, 16)
                wait_all(sp, s_store, NB, 16)

            @block.gpsimd
            def _(pool):
                def gather(b):
                    pool.wait_ge(*this(s_idx, b, 16))
                    wait_freed(pool, *before(s_xds, b, RING, 16))
                    pool.sem_inc(s_turn, 1)
                    for g in range(HG):
                        pool.indirect_dma_start(xd[b][:, g, :], None, t["X1"],
                                                bass.IndirectOffsetOnAxis(ap=idx[b][:, g:g + 1], axis=0),
                                                bounds_check=NT - 1, oob_is_err=False).then_inc(s_xd[b], 16)

                pipeline(pool, NB, [(0, gather)])

            @block.tensor
            def _(pe):
                def rows_T(b):
                    pe.wait_ge(*this(norm.s_h, b))
                    wait_freed(pe, *before(s_bn, b, RING))
                    transpose_rows(pe, p_h[b], norm.h[b], k["ident"], True).then_inc(s_hT, 1)

                pipeline(pe, NB, [(0, rows_T)])

            @block.scalar
            def _(act):
                act.preload_act_table_set(LN_EXP)

                def rows_relu(b):
                    wait_freed(act, *before(s_store, b, RING, 16))
                    norm.scalar_relu(act, b)

                pipeline(act, NB, [(0, partial(norm.scalar_log, act)), (1, rows_relu),
                                   (0, partial(norm.scalar_rstd, act))])

            @block.vector
            def _(dve):
                def columns(b):
                    dve.wait_ge(*this(s_hT, b))
                    new = BLK - NEW if is_last_node_block(b) else 0
                    dve.bn_stats(k["node_stats"][:, bass.ds(b.num, 1), :].rearrange("p b c -> p (b c)"),
                                 p_h[b][:, new:BLK]).then_inc(s_bn, 1)

                pipeline(dve, NB, [(0, partial(norm.vector_stats, dve)), (0, partial(norm.vector_aggregate, dve)),
                                   (4, columns), (1, partial(norm.vector_shift, dve))])
                dve.wait_ge(s_bn, NB)
                dve.bn_aggr(k["node_mv"][:, :], k["node_stats"][:, :, :].rearrange("p b c -> p (b c)")).then_inc(s_aggr, 1)


def column(vector):
    return vector.rearrange("(p a) -> p a", a=1)


class Affine:

    def __init__(self, ph, name):
        self.g, self.b = ph.sb(f"{name}_g", [P, 1]), ph.sb(f"{name}_b", [P, 1])
        self.ln, self.rstd = ph.sb(f"{name}_ln", [P, 1]), ph.sb(f"{name}_rstd", [P, 1])
        self.scale, self.off, self.shift = (ph.sb(f"{name}_{n}", [P, 1]) for n in ("scale", "off", "shift"))
        self.s_rstd, self.s_ln, self.s_done = (ph.sem(f"{name}_{n}") for n in ("rstd_done", "ln_done", "affine_steps"))

    def scalar(self, act, var, eps):
        act.activation(self.ln[:, :], var, ACT.Ln, bias=eps).then_inc(self.s_ln, 1)
        act.wait_ge(self.s_ln, 1)
        act.activation(self.rstd[:, :], self.ln[:, :], ACT.Exp, scale=-0.5).then_inc(self.s_rstd, 1)

    def vector(self, dve, mean):
        dve.wait_ge(self.s_rstd, 1)
        dve.tensor_tensor(self.scale[:, :], self.g[:, :], self.rstd[:, :], ALU.mult).then_inc(self.s_done, 1)
        dve.wait_ge(self.s_done, 1)
        dve.tensor_tensor(self.off[:, :], mean, self.scale[:, :], ALU.mult).then_inc(self.s_done, 1)
        dve.wait_ge(self.s_done, 2)
        dve.tensor_tensor(self.shift[:, :], self.b[:, :], self.off[:, :], ALU.subtract).then_inc(self.s_done, 1)
        dve.wait_ge(self.s_done, 3)


def layer1(nc, t, k):
    ident, same = k["ident"], k["same"]
    with Phase(nc, "layer1") as ph:
        w = ph.sb("w", [D, 4, D])
        wn = ph.sb("wn", [D, 3, D])
        bias = ph.sb("bias", [D, 3])
        bn = Affine(ph, "bn")
        idx = {n: ph.ring(n, [P, G], I32) for n in ("src", "end")}
        raw_s = ph.ring("raw_s", [P, G, D])
        raw_d = ph.ring("raw_d", [P, G, D])
        hsT = ph.ring("hsT", [P, BLK])
        hdT = ph.ring("hdT", [P, BLK])
        key, value = ph.sb("key", [P, BLK]), ph.sb("value", [P, BLK])
        prod, score, weight = (ph.ring(n, [P, BLK], depth=2) for n in ("prod", "score", "weight"))
        wsum = ph.ring("wsum", [P, BLK])
        vsum = ph.ring("vsum", [P, BLK])
        lsum, inv, mix, gone, twice, junk = (ph.sb(n, [P, BLK]) for n in ("lsum", "inv", "mix", "gone", "twice", "junk"))
        delta = ph.ring("delta", [P, BLK])
        rows = ph.ring("rows", [P, G, D])
        p_hs, p_hd, p_k, p_q, p_v, p_s, p_o, p_back = (ph.ps(n) for n in (
            "p_hs", "p_hd", "p_k", "p_q", "p_v", "p_s", "p_o", "p_back"))

        s_w, s_wn, s_pb, s_bias = ph.sem("weights_loaded"), ph.sem("weights_scaled"), ph.sem("bias_multiplied"), ph.sem("bias_ready")
        s_idx = {n: ph.dma(f"{n}_loaded") for n in ("src", "end")}
        s_raw, s_rawd, s_add, s_turn = ph.dma("src_gathered"), ph.dma("dst_rows_loaded"), ph.dma("rows_added"), ph.sem("pool_goes_on")
        s_hsT, s_hdT, s_hsc, s_hdc = (ph.sem(n) for n in ("hs_transposed", "hd_transposed", "hsT_ready", "hdT_ready"))
        s_kq, s_v, s_key, s_prod, s_s, s_score = (ph.sem(n) for n in (
            "key_query_done", "values_done", "key_ready", "product_ready", "scores_summed", "scores_clipped"))
        s_exp, s_val, s_sums, s_inv, s_mix = (ph.sem(n) for n in (
            "weights_ready", "values_weighted", "sums_done", "reciprocal_done", "mix_ready"))
        s_o, s_delta, s_back, s_rows, s_gone, s_moved = (ph.sem(n) for n in (
            "out_done", "delta_ready", "delta_transposed", "rows_ready", "ends_picked", "moved_done"))
        s_wsum, s_lsum = ph.sem("weights_summed"), ph.sem("log_of_sums")
        norm_s = Norm(ph, k, "src", raw_s, s_raw, 64, k["eps"][:, :], s_hsT)
        norm_d = Norm(ph, k, "dst", raw_d, s_rawd, 16, k["eps"][:, :], s_hdT)

        with ph.block() as block:
            @block.sync
            def _(sp):
                for n, name in enumerate(("Wq", "Wk", "Wv", "Wo")):
                    sp.dma_start(w[:, n, :], t[name]).then_inc(s_w, 16)
                sp.dma_start(bn.g[:, :], column(t["g1"])).then_inc(s_w, 16)
                sp.dma_start(bn.b[:, :], column(t["b1"])).then_inc(s_w, 16)
                gathers, ends = edge_indices(sp, t, idx, s_idx, {"src": s_raw}, s_add)

                def load_dst_rows(b):
                    wait_freed(sp, *before(norm_d.s_h, b, RING))
                    sp.dma_start(raw_d[b][:, :, :], edge_rows(t["XD"], b)).then_inc(s_rawd[b], 16)

                pipeline(sp, EB, [(0, gathers), (1, load_dst_rows), (7, ends)])

            @block.gpsimd
            def _(pool):
                def gather(b):
                    pool.wait_ge(*this(s_idx["src"], b, 16))
                    wait_freed(pool, *before(norm_s.s_h, b, RING))
                    pool.sem_inc(s_turn, 1)
                    indexed_gather(pool, raw_s[b], t["X1"], idx["src"][b], s_raw[b], NT)

                def scatter(b):
                    pool.wait_ge(*this(s_idx["end"], b, 16))
                    pool.wait_ge(*this(s_rows, b))
                    pool.sem_inc(s_turn, 1)
                    indexed_add(pool, t["H2"], idx["end"][b], rows[b], s_add[b])

                pipeline(pool, EB, [(0, gather), (8, scatter)])
                wait_all(pool, s_add, EB, 64)

            @block.tensor
            def _(pe):
                pe.wait_ge(s_w, 96)
                pe.wait_ge(bn.s_done, 3)
                for n in range(3):
                    last = pe.matmul(p_k[:, n:n + 1], lhsT=w[:, n, :], rhs=bn.shift[:, :], start=True, stop=True)
                last.then_inc(s_pb, 1)
                pe.wait_ge(s_bias, 1)
                pe.wait_ge(s_wn, 1)

                def rows_T(b):
                    for norm, p_h, s_t, s_c in ((norm_s, p_hs, s_hsT, s_hsc), (norm_d, p_hd, s_hdT, s_hdc)):
                        pe.wait_ge(*this(norm.s_h, b))
                        wait_freed(pe, *before(s_c, b, 1))
                        transpose_rows(pe, p_h, norm.h[b], ident, True).then_inc(s_t, 1)

                def project(b):
                    pe.wait_ge(*this(s_hsc, b))
                    pe.wait_ge(*this(s_hdc, b))
                    wait_freed(pe, *before(s_prod, b, 1))
                    pe.matmul(p_k[:, :], lhsT=wn[:, 1, :], rhs=hsT[b][:, :], start=True, stop=True)
                    pe.matmul(p_q[:, :], lhsT=wn[:, 0, :], rhs=hdT[b][:, :], start=True, stop=True).then_inc(s_kq, 1)

                def project_values(b):
                    wait_freed(pe, *before(s_val, b, 1))
                    pe.matmul(p_v[:, :], lhsT=wn[:, 2, :], rhs=hsT[b][:, :], start=True, stop=True).then_inc(s_v, 1)

                def head_sums(b):
                    pe.wait_ge(*this(s_prod, b))
                    wait_freed(pe, *before(s_score, b, 1))
                    pe.matmul(p_s[:, :], lhsT=k["blocks16"], rhs=prod[b][:, :], start=True, stop=True).then_inc(s_s, 1)

                def out(b):
                    pe.wait_ge(*this(s_mix, b))
                    wait_freed(pe, *before(s_delta, b, 1))
                    pe.matmul(p_o[:, :], lhsT=w[:, 3, :], rhs=mix[:, :], start=True, stop=True).then_inc(s_o, 1)

                def back(b):
                    pe.wait_ge(*this(s_delta, b))
                    wait_freed(pe, *before(s_rows, b, 1))
                    transpose_back(pe, p_back, delta[b], ident).then_inc(s_back, 1)

                pipeline(pe, EB, [(4, head_sums), (3, project), (4, project_values), (5, out), (6, back),
                                  (2, rows_T)])

            @block.scalar
            def _(act):
                act.preload_act_table_set(LN_EXP)
                bn.scalar(act, k["node_mv"][:, 1:2], k["eps"][:, :])

                def evac_h(b):
                    wait_freed(act, *before(s_v, b, RING))
                    wait_freed(act, *before(s_moved, b, RING))
                    act.wait_ge(*this(s_hsT, b))
                    act.copy(hsT[b][:, :], p_hs[:, :]).then_inc(s_hsc, 1)
                    act.wait_ge(*this(s_hdT, b))
                    act.copy(hdT[b][:, :], p_hd[:, :]).then_inc(s_hdc, 1)

                def exps(b):
                    act.wait_ge(*this(s_score, b))
                    wait_freed(act, *before(s_sums, b, 2))
                    act.activation(weight[b][:, :], score[b][:, :], ACT.Exp).then_inc(s_exp, 1)

                def inverse(b):
                    act.wait_ge(*this(s_wsum, b))
                    wait_freed(act, *before(s_inv, b, 1))
                    act.activation(lsum[:, :], wsum[b][:, :], ACT.Ln).then_inc(s_lsum, 1)
                    act.wait_ge(*this(s_lsum, b))
                    wait_freed(act, *before(s_mix, b, 1))
                    act.activation(inv[:, :], lsum[:, :], ACT.Exp, scale=-1.0).then_inc(s_inv, 1)

                def evac_out(b):
                    act.wait_ge(*this(s_o, b))
                    wait_freed(act, *before(s_back, b, RING))
                    wait_freed(act, *before(s_moved, b, RING))
                    act.copy(delta[b][:, :], p_o[:, :]).then_inc(s_delta, 1)

                def evac_rows(b):
                    act.wait_ge(*this(s_back, b))
                    wait_freed(act, *before(s_add, b, RING, 64))
                    act.copy(rows[b][:, :, :], grouped(p_back[:, :])).then_inc(s_rows, 1)

                pipeline(act, EB, [(5, inverse), (4, exps), (1, partial(norm_s.scalar_relu, act)),
                                   (1, partial(norm_d.scalar_relu, act)), (5, evac_out), (6, evac_rows), (2, evac_h),
                                   (0, partial(norm_s.scalar_log, act)), (0, partial(norm_d.scalar_log, act)),
                                   (0, partial(norm_s.scalar_rstd, act)), (0, partial(norm_d.scalar_rstd, act))])

            @block.vector
            def _(dve):
                dve.memset(wsum[RING - 1][:, :], 0.0)
                dve.memset(vsum[RING - 1][:, :], 0.0)
                dve.wait_ge(s_w, 96)
                bn.vector(dve, k["node_mv"][:, 0:1])
                dve.tensor_scalar(wn[:, :, :], w[:, 0:3, :], bn.scale[:, :], None, ALU.mult).then_inc(s_wn, 1)
                dve.wait_ge(s_pb, 1)
                dve.tensor_copy(bias[:, :], p_k[:, 0:3]).then_inc(s_bias, 1)
                dve.wait_ge(s_bias, 1)

                def scores(b):
                    dve.wait_ge(*this(s_kq, b))
                    wait_freed(dve, *before(s_prod, b, 1))
                    dve.tensor_scalar(key[:, :], p_k[:, :], bias[:, 1:2], None, ALU.add).then_inc(s_key, 1)
                    dve.wait_ge(*this(s_key, b))
                    wait_freed(dve, *before(s_s, b, 2))
                    dve.scalar_tensor_tensor(prod[b][:, :], p_q[:, :], bias[:, 0:1], key[:, :], ALU.add, ALU.mult
                                             ).then_inc(s_prod, 1)

                def clip(b):
                    dve.wait_ge(*this(s_s, b))
                    wait_freed(dve, *before(s_exp, b, 2))
                    dve.tensor_scalar(score[b][:, :], p_s[:, :], 5.0, -5.0, ALU.min, ALU.max).then_inc(s_score, 1)

                def sums(b):
                    dve.wait_ge(*this(s_v, b))
                    dve.wait_ge(*this(s_exp, b))
                    wait_freed(dve, *before(s_sums, b, 1))
                    dve.scalar_tensor_tensor(value[:, :], p_v[:, :], bias[:, 2:3], weight[b][:, :], ALU.add, ALU.mult
                                             ).then_inc(s_val, 1)
                    dve.tensor_tensor_scan(wsum[b][:, :], edge_cols(same, b), weight[b][:, :], wsum[b.back(1)][:, BLK - 1:BLK],
                                           ALU.mult, ALU.add).then_inc(s_wsum, 1)
                    dve.wait_ge(*this(s_val, b))
                    dve.tensor_tensor_scan(vsum[b][:, :], edge_cols(same, b), value[:, :], vsum[b.back(1)][:, BLK - 1:BLK],
                                           ALU.mult, ALU.add).then_inc(s_sums, 1)

                def average(b):
                    dve.wait_ge(*this(s_inv, b))
                    dve.wait_ge(*this(s_sums, b))
                    wait_freed(dve, *before(s_o, b, 1))
                    dve.tensor_tensor(mix[:, :], vsum[b][:, :], inv[:, :], ALU.mult).then_inc(s_mix, 1)

                def moved(b):
                    dve.wait_ge(*this(s_delta, b))
                    wait_freed(dve, *before(s_moved, b, 1))
                    at = bass.ds(b.num, 1)
                    dve.scalar_tensor_tensor(gone[:, :], same[:, bass.ds(b.num * BLK + 1, BLK)], 1.0, delta[b][:, :],
                                             ALU.subtract, ALU.mult, accum_out=k["moved"][:, 0, at])
                    dve.scalar_tensor_tensor(twice[:, :], hdT[b][:, :], 2.0, delta[b][:, :], ALU.mult, ALU.add
                                             ).then_inc(s_gone, 1)
                    dve.wait_ge(*this(s_gone, b))
                    dve.scalar_tensor_tensor(junk[:, :], gone[:, :], 1.0, twice[:, :], ALU.mult, ALU.mult,
                                             accum_out=k["moved"][:, 1, at]).then_inc(s_moved, 1)

                pipeline(dve, EB, [(4, clip), (1, partial(norm_s.vector_shift, dve)),
                                   (1, partial(norm_d.vector_shift, dve)), (5, average),
                                   (0, partial(norm_s.vector_stats, dve)), (0, partial(norm_d.vector_stats, dve)),
                                   (0, partial(norm_s.vector_aggregate, dve)),
                                   (0, partial(norm_d.vector_aggregate, dve)), (6, moved), (3, scores), (4, sums)])


def edge_indices(sp, t, idx, s_idx, used, s_scattered):
    cols = {"src": 0, "dst": G, "end": 2 * G}

    def gathers(b):
        for n in used:
            wait_freed(sp, *before(used[n], b, RING, 64))
            sp.dma_start(idx[n][b][:, :], block_index(t, b)[:, cols[n]:cols[n] + G]).then_inc(s_idx[n][b], 16)

    def ends(b):
        wait_freed(sp, *before(s_scattered, b, RING, 64))
        sp.dma_start(idx["end"][b][:, :], block_index(t, b)[:, cols["end"]:]).then_inc(s_idx["end"][b], 16)

    return gathers, ends


def nodes(nc, t, k):
    ident = k["ident"]
    F = 2 * D
    with Phase(nc, "nodes") as ph:
        bn = Affine(ph, "bn")
        bo, bf1 = ph.sb("bo", [P, 1]), ph.sb("bf1", [P, 2])
        w1, w1n, w2, wg = ph.sb("w1", [D, F]), ph.sb("w1n", [D, F]), ph.sb("w2", [P, 2, D]), ph.sb("wg", [D, D])
        add_rows, bias_rows = ph.sb("add_rows", [P, 2, D]), ph.sb("bias_rows", [P, D])
        add_row = ph.sb("add_row", [P, D])
        dsum, dsq, e1, e2, e3, e4 = (ph.sb(n, [P, 1]) for n in ("dsum", "dsq", "e1", "e2", "e3", "e4"))
        mean, var, meanb, hbias = (ph.sb(n, [P, 1]) for n in ("mean", "var", "meanb", "hbias"))
        b1n = ph.sb("b1n", [P, 2])
        x1 = ph.ring("x1", [P, G, D])
        h2 = ph.ring("h2", [P, G, D])
        both, base = ph.sb("both", [P, G, D]), ph.ring("base", [P, G, D])
        hT = ph.ring("hT", [P, BLK])
        z = ph.ring("z", [P, 2, BLK])
        x2 = ph.ring("x2", [P, G, D])
        h3T = ph.ring("h3T", [P, BLK])
        pre, low, ex = (ph.ring(n, [P, G, D], depth=2) for n in ("pre", "low", "ex"))
        part = ph.sb("part", [P, G, D])
        res = ph.ring("res", [P, G, D])
        p_z0, p_z1, p_h3, p_g = (ph.ps(n) for n in ("p_z0", "p_z1", "p_h3", "p_g"))
        p_h, p_y = ph.ps_ring("p_h"), ph.ps_ring("p_y")
        p_z = [p_z0, p_z1]

        s_w, s_v, s_b1, s_b1n = ph.sem("weights_loaded"), ph.sem("preparation_steps"), ph.sem("bias_multiplied"), ph.sem("prepared")
        s_var, s_rows = ph.sem("var_ready"), ph.sem("rows_added_up")
        s_in, s_base, s_both = ph.dma("rows_loaded"), ph.sem("base_ready"), ph.sem("both_ready")
        s_hT, s_hTc, s_z, s_zc, s_y, s_x2 = (ph.sem(n) for n in (
            "h_transposed", "hT_ready", "hidden_done", "relu_done", "ffn_done", "x2_ready"))
        s_h3, s_h3c, s_g, s_pre, s_low, s_ex, s_part, s_res = (ph.sem(n) for n in (
            "h3_transposed", "h3T_ready", "gat_done", "pre_ready", "low_ready", "exp_ready", "part_ready", "out_ready"))
        s_st2, s_sto = ph.dma("x2_stored"), ph.dma("out_stored")
        norm = Norm(ph, k, "norm", x2, None, 0, k["eps"][:, :], s_h3)

        with ph.block() as block:
            @block.sync
            def _(sp):
                with nc.allow_non_contiguous_dma(reason="columns of vectors"):
                    for dst, src in ((bn.g[:, :], column(t["g2"])), (bn.b[:, :], column(t["b2"])), (bo[:, :], column(t["bo"])),
                                     (bf1[:, :], t["bf1"].rearrange("(c p) -> p c", p=P)), (w1[:, :], t["W1"]),
                                     (w2[:, :, :], t["W2"].rearrange("(c p) n -> p c n", p=P)), (wg[:, :], t["WgT"]),
                                     (add_rows[:, 0, :], t["bo"].partition_broadcast(P)),
                                     (add_rows[:, 1, :], t["bf2"].partition_broadcast(P)),
                                     (bias_rows[:, :], t["bias"].partition_broadcast(P))):
                        sp.dma_start(dst, src).then_inc(s_w, 16)

                def load(b):
                    wait_freed(sp, *before(s_hT, b, RING))
                    wait_freed(sp, *before(s_both, b, RING))
                    sp.dma_start(x1[b][:, :, :], node_rows(t["X1"], b)).then_inc(s_in[b], 16)
                    sp.dma_start(h2[b][:, :, :], node_rows(t["H2"], b)).then_inc(s_in[b], 16)

                def store_x2(b):
                    if is_last_node_block(b):
                        wait_freed(sp, *before(s_st2, b, 1, 32))
                    sp.wait_ge(*this(s_x2, b))
                    sp.dma_start(node_rows(t["X2"], b), x2[b][:, :, :]).then_inc(s_st2[b], 16)
                    sp.dma_start(node_rows(t["X3"], b), x2[b][:, :, :]).then_inc(s_st2[b], 16)

                def store_out(b):
                    if is_last_node_block(b):
                        wait_freed(sp, *before(s_sto, b, 1, 16))
                    sp.wait_ge(*this(s_res, b))
                    sp.dma_start(node_rows(t["out"], b), res[b][:, :, :]).then_inc(s_sto[b], 16)

                pipeline(sp, NB, [(0, load), (6, store_x2), (9, store_out)])
                wait_all(sp, s_st2, NB, 32)
                wait_all(sp, s_sto, NB, 16)

            @block.gpsimd
            def _(pool):
                pool.wait_ge(s_w, 160)
                pool.tensor_tensor(add_row[:, :], add_rows[:, 0, :], add_rows[:, 1, :], ALU.add).then_inc(s_rows, 1)
                pool.wait_ge(s_rows, 1)

                def add(b):
                    pool.wait_ge(*this(s_in, b, 32))
                    wait_freed(pool, *before(s_base, b, 1))
                    pool.tensor_tensor(both[:, :, :], x1[b][:, :, :], h2[b][:, :, :], ALU.add).then_inc(s_both, 1)
                    pool.wait_ge(*this(s_both, b))
                    wait_freed(pool, *before(s_x2, b, RING))
                    pool.tensor_tensor(base[b][:, :, :], both[:, :, :], bc(add_row[:, :], 1, G), ALU.add).then_inc(s_base, 1)

                pipeline(pool, NB, [(0, add)])

            @block.tensor
            def _(pe):
                pe.wait_ge(s_w, 160)
                pe.wait_ge(s_v, 10)
                for c in range(2):
                    last = pe.matmul(p_g[:, c:c + 1], lhsT=w1[:, c * P:(c + 1) * P], rhs=hbias[:, :], start=True, stop=True)
                last.then_inc(s_b1, 1)
                pe.wait_ge(s_b1n, 2)

                def rows_T(b):
                    pe.wait_ge(*this(s_in, b, 32))
                    wait_freed(pe, *before(s_hTc, b, 2))
                    transpose_rows(pe, p_h[b], h2[b], ident, False).then_inc(s_hT, 1)

                def hidden(b):
                    pe.wait_ge(*this(s_hTc, b))
                    wait_freed(pe, *before(s_zc, b, 1))
                    for c in range(2):
                        last = pe.matmul(p_z[c][:, :], lhsT=w1n[:, c * P:(c + 1) * P], rhs=hT[b][:, :], start=True, stop=True)
                    last.then_inc(s_z, 1)

                def ffn(b):
                    pe.wait_ge(*this(s_zc, b))
                    wait_freed(pe, *before(s_x2, b, 2))
                    for g in range(G):
                        for c in range(2):
                            last = pe.matmul(p_y[b][:, g * P:(g + 1) * P], lhsT=z[b][:, c, g * P:(g + 1) * P], rhs=w2[:, c, :],
                                             start=(c == 0), stop=(c == 1))
                    last.then_inc(s_y, 1)

                def rows3_T(b):
                    pe.wait_ge(*this(norm.s_h, b))
                    wait_freed(pe, *before(s_h3c, b, 1))
                    transpose_rows(pe, p_h3, norm.h[b], ident, False).then_inc(s_h3, 1)

                def gat(b):
                    pe.wait_ge(*this(s_h3c, b))
                    wait_freed(pe, *before(s_pre, b, 1))
                    for g in range(G):
                        last = pe.matmul(p_g[:, g * P:(g + 1) * P], lhsT=h3T[b][:, g * P:(g + 1) * P], rhs=wg[:, :],
                                         start=True, stop=True)
                    last.then_inc(s_g, 1)

                pipeline(pe, NB, [(5, gat), (2, ffn), (1, hidden), (3, rows3_T), (0, rows_T)])

            @block.scalar
            def _(act):
                act.preload_act_table_set(LN_EXP)
                act.wait_ge(s_var, 1)
                bn.scalar(act, var[:, :], k["eps"][:, :])
                act.wait_ge(s_b1n, 2)

                def relu_hidden(b):
                    act.wait_ge(*this(s_z, b))
                    wait_freed(act, *before(s_y, b, RING))
                    for c in range(2):
                        last = act.activation(z[b][:, c, :], p_z[c][:, :], ACT.Relu, bias=b1n[:, c:c + 1])
                    last.then_inc(s_zc, 1)

                def exps(b):
                    act.wait_ge(*this(s_pre, b))
                    wait_freed(act, *before(s_ex, b, 2))
                    act.activation(low[b][:, :, :], pre[b][:, :, :], ACT.Relu, scale=-1.0).then_inc(s_low, 1)
                    act.wait_ge(*this(s_low, b))
                    wait_freed(act, *before(s_part, b, 2))
                    act.activation(ex[b][:, :, :], low[b][:, :, :], ACT.Exp, scale=-1.0).then_inc(s_ex, 1)

                pipeline(act, NB, [(3, partial(norm.scalar_log, act)), (3, partial(norm.scalar_rstd, act)),
                                   (3, partial(norm.scalar_relu, act)), (1, relu_hidden), (5, exps)])

            @block.vector
            def _(dve):
                steps = [0]

                def link(ins):
                    steps[0] += 1
                    ins.then_inc(s_v, 1)
                    dve.wait_ge(s_v, steps[0])

                old_mean, old_var = k["node_mv"][:, 0:1], k["node_mv"][:, 1:2]
                dve.wait_ge(s_w, 160)
                link(dve.reduce_sum(dsum[:, :], k["moved"][:, 0, :], mybir.AxisListType.X))
                link(dve.reduce_sum(dsq[:, :], k["moved"][:, 1, :], mybir.AxisListType.X))
                link(dve.tensor_scalar(e1[:, :], dsum[:, :], -1.0 / N, None, ALU.mult))
                link(dve.tensor_tensor(mean[:, :], old_mean, e1[:, :], ALU.add))
                link(dve.scalar_tensor_tensor(e2[:, :], dsum[:, :], 2.0, old_mean, ALU.mult, ALU.mult))
                link(dve.tensor_tensor(e3[:, :], e2[:, :], dsq[:, :], ALU.subtract))
                link(dve.scalar_tensor_tensor(e4[:, :], e3[:, :], 1.0 / N, old_var, ALU.mult, ALU.add))
                link(dve.tensor_tensor(e2[:, :], e1[:, :], e1[:, :], ALU.mult))
                dve.tensor_tensor(var[:, :], e4[:, :], e2[:, :], ALU.subtract).then_inc(s_var, 1)
                bn.vector(dve, mean[:, :])
                link(dve.tensor_scalar(w1n[:, :], w1[:, :], bn.scale[:, :], None, ALU.mult))
                link(dve.tensor_copy(hbias[:, :], bn.shift[:, :]))
                dve.wait_ge(s_b1, 1)
                dve.tensor_tensor(b1n[:, :], p_g[:, 0:2], bf1[:, :], ALU.add).then_inc(s_b1n, 2)
                dve.wait_ge(s_b1n, 2)

                def evac_h(b):
                    dve.wait_ge(*this(s_hT, b))
                    wait_freed(dve, *before(s_z, b, RING))
                    dve.tensor_copy(hT[b][:, :], p_h[b][:, :]).then_inc(s_hTc, 1)

                def residual(b):
                    dve.wait_ge(*this(s_y, b))
                    dve.wait_ge(*this(s_base, b))
                    wait_freed(dve, *before(s_st2, b, RING, 32))
                    wait_freed(dve, *before(s_res, b, RING))
                    wait_freed(dve, *before(norm.s_h, b, RING))
                    dve.tensor_tensor(x2[b][:, :, :], grouped(p_y[b][:, :]), base[b][:, :, :], ALU.add).then_inc(s_x2, 1)

                def row_stats(b):
                    dve.wait_ge(*this(s_x2, b))
                    norm.vector_stats(dve, b)

                def evac_h3(b):
                    dve.wait_ge(*this(s_h3, b))
                    wait_freed(dve, *before(s_g, b, RING))
                    dve.tensor_copy(h3T[b][:, :], p_h3[:, :]).then_inc(s_h3c, 1)

                def before_elu(b):
                    dve.wait_ge(*this(s_g, b))
                    wait_freed(dve, *before(s_low, b, 2))
                    wait_freed(dve, *before(s_part, b, 2))
                    dve.tensor_tensor(pre[b][:, :, :], grouped(p_g[:, :]), bc(bias_rows[:, :], 1, G), ALU.add).then_inc(s_pre, 1)

                def elu_part(b):
                    dve.wait_ge(*this(s_ex, b))
                    wait_freed(dve, *before(s_res, b, 1))
                    dve.scalar_tensor_tensor(part[:, :, :], pre[b][:, :, :], 0.0, ex[b][:, :, :], ALU.max, ALU.add
                                             ).then_inc(s_part, 1)

                def elu(b):
                    dve.wait_ge(*this(s_part, b))
                    wait_freed(dve, *before(s_sto, b, RING, 16))
                    dve.scalar_tensor_tensor(res[b][:, :, :], part[:, :, :], -1.0, x2[b][:, :, :], ALU.add, ALU.add
                                             ).then_inc(s_res, 1)

                pipeline(dve, NB, [(1, evac_h), (4, evac_h3), (3, partial(norm.vector_shift, dve)), (6, elu_part),
                                   (5, before_elu), (6, elu), (2, residual), (2, row_stats),
                                   (2, partial(norm.vector_aggregate, dve))])


def layer2(nc, t, k):
    ident, same = k["ident"], k["same"]
    NF = 11
    CHUNKS = [(0, 4), (4, 8), (8, NF)]
    WEIGHT = {0: ("w0", None), 1: ("w3", None)}
    for c in range(3):
        for n, name in enumerate(("w1", "w2", "w4")):
            WEIGHT[2 + 3 * c + n] = (name, c)
    with Phase(nc, "layer2") as ph:
        w = ph.sb("w", [P, 3, D])
        idx = {n: ph.ring(n, [P, G], I32) for n in ("src", "end")}
        attrT = ph.ring("attrT", [9, BLK])
        raw = ph.ring("raw", [P, G, D])
        coef = ph.ring("coef", [P, G, COEF])
        vy = ph.sb("vy", [P, G, MUL, 3])
        m0, m1, m2, m01 = (ph.sb(n, [P, G, 3, MUL]) for n in ("m0", "m1", "m2", "m01"))
        feat = ph.ring("feat", [P, G, NF, MUL])
        featT = ph.ring("featT", [P, 3, BLK])
        total = ph.ring("total", [P, BLK])
        rows = ph.ring("rows", [P, G, D])
        p_f0, p_f1, p_f2, p_back = (ph.ps(n) for n in ("p_f0", "p_f1", "p_f2", "p_back"))
        p_c, p_out = ph.ps_ring("p_c"), ph.ps_ring("p_out")
        p_f = [p_f0, p_f1, p_f2]

        s_w0, s_w = ph.sem("weights_cleared"), ph.sem("weights_loaded")
        s_idx = {n: ph.dma(f"{n}_loaded") for n in ("src", "end")}
        s_attr, s_c, s_cc = ph.dma("attributes_loaded"), ph.sem("coefficients_done"), ph.sem("coefficients_ready")
        s_raw, s_add, s_turn = ph.dma("x2_gathered"), ph.dma("rows_added"), ph.sem("pool_goes_on")
        s_first, s_mid, s_feat, s_fT, s_fTc = (ph.sem(n) for n in (
            "products_done", "half_summed", "features_done", "features_transposed", "featT_ready"))
        s_out, s_total, s_back, s_rows = (ph.sem(n) for n in ("out_done", "totals_done", "totals_transposed", "rows_ready"))
        norm = Norm(ph, k, "norm", raw, s_raw, 64, k["eps"][:, :], s_feat)

        with ph.block() as block:
            @block.sync
            def _(sp):
                sp.wait_ge(s_w0, 1)
                with nc.allow_non_contiguous_dma(reason="weights laid out by component"):
                    for n, (lo, hi) in enumerate(CHUNKS):
                        for f in range(lo, hi):
                            name, c = WEIGHT[f]
                            cols = slice(0, MUL) if c is None else slice(MUL + c, D, 3)
                            sp.dma_start(w[(f - lo) * MUL:(f - lo + 1) * MUL, n, cols],
                                         t[name].rearrange("u a v -> u (a v)")).then_inc(s_w, 16)

                cols = {"src": 0, "end": 2 * G}

                def gathers(b):
                    wait_freed(sp, *before(s_raw, b, RING, 64))
                    sp.dma_start(idx["src"][b][:, :], block_index(t, b)[:, 0:G]).then_inc(s_idx["src"][b], 16)
                    wait_freed(sp, *before(s_c, b, RING))
                    sp.dma_start(attrT[b][:, :], t["edge9T"][:, bass.ds(b.num * BLK, BLK)]).then_inc(s_attr[b], 16)

                def ends(b):
                    wait_freed(sp, *before(s_add, b, RING, 64))
                    sp.dma_start(idx["end"][b][:, :], block_index(t, b)[:, cols["end"]:]).then_inc(s_idx["end"][b], 16)

                pipeline(sp, EB, [(0, gathers), (6, ends)])

            @block.gpsimd
            def _(pool):
                def gather(b):
                    pool.wait_ge(*this(s_idx["src"], b, 16))
                    wait_freed(pool, *before(norm.s_h, b, RING))
                    pool.sem_inc(s_turn, 1)
                    indexed_gather(pool, raw[b], t["X2"], idx["src"][b], s_raw[b], N)

                def scatter(b):
                    pool.wait_ge(*this(s_idx["end"], b, 16))
                    pool.wait_ge(*this(s_rows, b))
                    pool.sem_inc(s_turn, 1)
                    indexed_add(pool, t["X3"], idx["end"][b], rows[b], s_add[b])

                pipeline(pool, EB, [(0, gather), (7, scatter)])
                wait_all(pool, s_add, EB, 64)

            @block.tensor
            def _(pe):
                pe.wait_ge(s_w, NF * 16)

                def coefficients(b):
                    pe.wait_ge(*this(s_attr, b, 16))
                    wait_freed(pe, *before(s_cc, b, 2))
                    for g in range(G):
                        last = pe.matmul(p_c[b][:, g * COEF:(g + 1) * COEF], lhsT=attrT[b][:, g:BLK:G], rhs=k["coef"][:, :],
                                         start=True, stop=True)
                    last.then_inc(s_c, 1)

                def features(b):
                    pe.wait_ge(*this(s_feat, b))
                    wait_freed(pe, *before(s_fTc, b, 1))
                    for n, (lo, hi) in enumerate(CHUNKS):
                        rows_f = (hi - lo) * MUL
                        for g in range(G):
                            last = pe.transpose(p_f[n][0:rows_f, g:BLK:G],
                                                feat[b][:, g, lo:hi, :].rearrange("p a b -> p (a b)"), ident)
                    last.then_inc(s_fT, 1)

                def out(b):
                    pe.wait_ge(*this(s_fTc, b))
                    wait_freed(pe, *before(s_total, b, 2))
                    for n, (lo, hi) in enumerate(CHUNKS):
                        r = (hi - lo) * MUL
                        last = pe.matmul(p_out[b][:, :], lhsT=w[0:r, n, :], rhs=featT[b][0:r, n, :], start=(n == 0), stop=(n == 2))
                    last.then_inc(s_out, 1)

                def back(b):
                    pe.wait_ge(*this(s_total, b))
                    wait_freed(pe, *before(s_rows, b, 1))
                    transpose_back(pe, p_back, total[b], ident).then_inc(s_back, 1)

                pipeline(pe, EB, [(4, out), (5, back), (3, features), (1, coefficients)])

            @block.scalar
            def _(act):
                act.preload_act_table_set(LN_EXP)

                def evac_coefficients(b):
                    act.wait_ge(*this(s_c, b))
                    wait_freed(act, *before(s_feat, b, RING))
                    act.copy(coef[b][:, :, :], p_c[b][:, 0:G * COEF].rearrange("p (g c) -> p g c", g=G)).then_inc(s_cc, 1)

                def evac_features(b):
                    act.wait_ge(*this(s_fT, b))
                    wait_freed(act, *before(s_out, b, RING))
                    for n, (lo, hi) in enumerate(CHUNKS):
                        r = (hi - lo) * MUL
                        last = act.copy(featT[b][0:r, n, :], p_f[n][0:r, :])
                    last.then_inc(s_fTc, 1)

                def evac_rows(b):
                    act.wait_ge(*this(s_back, b))
                    wait_freed(act, *before(s_add, b, RING, 64))
                    act.copy(rows[b][:, :, :], grouped(p_back[:, :])).then_inc(s_rows, 1)

                pipeline(act, EB, [(0, partial(norm.scalar_log, act)), (1, partial(norm.scalar_relu, act)),
                                   (0, partial(norm.scalar_rstd, act)), (5, evac_rows), (3, evac_features),
                                   (1, evac_coefficients)])

            @block.vector
            def _(dve):
                dve.memset(total[RING - 1][:, :], 0.0)
                dve.memset(w[:, :, :], 0.0).then_inc(s_w0, 1)

                def products(b):
                    dve.wait_ge(*this(norm.s_h, b))
                    dve.wait_ge(*this(s_cc, b))
                    wait_freed(dve, *before(s_feat, b, 1))
                    wait_freed(dve, *before(s_fT, b, RING))
                    h, c, f = norm.h[b], coef[b], feat[b]
                    hs = h[:, :, 0:MUL]
                    hv = h[:, :, MUL:D].rearrange("p g (c i) -> p g c i", i=3)
                    hvk = h[:, :, MUL:D].rearrange("p g (c i) -> p g i c", i=3)
                    dve.tensor_tensor(vy[:, :, :, :], hv, bc(c[:, :, 1:4], 2, MUL), ALU.mult)
                    for n, m in enumerate((m0, m1, m2)):
                        last = dve.tensor_tensor(m[:, :, :, :], bc(hvk[:, :, n, :], 2, 3),
                                                 bc(c[:, :, 8 + 3 * n:11 + 3 * n], 3, MUL), ALU.mult)
                    last.then_inc(s_first, 1)
                    dve.tensor_tensor(f[:, :, 0, :], hs, c[:, :, 0:1].to_broadcast([P, G, MUL]), ALU.mult)
                    dve.tensor_tensor(f[:, :, 2:NF:3, :], bc(hs, 2, 3), bc(c[:, :, 4:7], 3, MUL), ALU.mult)
                    dve.tensor_tensor(f[:, :, 3:NF:3, :], hvk, bc(c[:, :, 7:8].to_broadcast([P, G, 3]), 3, MUL), ALU.mult)
                    dve.wait_ge(*this(s_first, b))
                    dve.tensor_tensor(m01[:, :, :, :], m0[:, :, :, :], m1[:, :, :, :], ALU.add).then_inc(s_mid, 1)
                    dve.tensor_reduce(f[:, :, 1, :], vy[:, :, :, :], mybir.AxisListType.X, ALU.add)
                    dve.wait_ge(*this(s_mid, b))
                    dve.tensor_tensor(f[:, :, 4:NF:3, :], m01[:, :, :, :], m2[:, :, :, :], ALU.add).then_inc(s_feat, 1)

                def sums(b):
                    dve.wait_ge(*this(s_out, b))
                    wait_freed(dve, *before(s_total, b, 1))
                    wait_freed(dve, *before(s_back, b, RING))
                    dve.tensor_tensor_scan(total[b][:, :], edge_cols(same, b), p_out[b][:, :], total[b.back(1)][:, BLK - 1:BLK],
                                           ALU.mult, ALU.add).then_inc(s_total, 1)

                pipeline(dve, EB, [(0, partial(norm.vector_stats, dve)), (1, partial(norm.vector_shift, dve)),
                                   (0, partial(norm.vector_aggregate, dve)), (2, products), (4, sums)])


def layer3(nc, t, k):
    ident, same = k["ident"], k["same"]
    with Phase(nc, "layer3") as ph:
        wg, wgT = ph.sb("wg", [D, D]), ph.sb("wgT", [D, D])
        att = ph.sb("att", [P, 2])
        spread = ph.sb("spread", [P, 2, D])
        wa, wa_sum = ph.sb("wa", [D, 2, D]), ph.sb("wa_sum", [D, D])
        bias, nbias = ph.sb("bias", [P, 1]), ph.sb("nbias", [P, 1])
        idx = {n: ph.ring(n, [P, G], I32) for n in ("src", "dst", "end")}
        raw_s = ph.ring("raw_s", [P, G, D])
        raw_d = ph.ring("raw_d", [P, G, D])
        hsT = ph.ring("hsT", [P, BLK])
        hdT = ph.ring("hdT", [P, BLK])
        lin, log = ph.ring("lin", [P, 2, BLK], depth=2), ph.sb("log", [P, 2, BLK])
        drop, weight = (ph.ring(n, [P, 2, BLK], depth=2) for n in ("drop", "weight"))
        both = ph.sb("both", [P, BLK])
        top = ph.ring("top", [P, BLK + 1], depth=2)
        neg, fall, keep, wsum, vsum, num, den, mix, ex, part = (ph.ring(n, [P, BLK], depth=2) for n in (
            "neg", "fall", "keep", "wsum", "vsum", "num", "den", "mix", "ex", "part"))
        value, own, lden, inv, low, elu_T = (ph.sb(n, [P, BLK]) for n in (
            "value", "own", "lden", "inv", "low", "elu_T"))
        kept_d = ph.ring("kept_d", [P, G, D])
        rows = ph.ring("rows", [P, G, D])
        p_hs, p_hd, p_xs, p_xd, p_e, p_l, p_back = (ph.ps(n) for n in ("p_hs", "p_hd", "p_xs", "p_xd", "p_e", "p_l", "p_back"))

        s_w, s_spread, s_wa, s_wac = ph.sem("weights_loaded"), ph.sem("attention_spread"), ph.sem("wa_done"), ph.sem("wa_ready")
        s_idx = {n: ph.dma(f"{n}_loaded") for n in ("src", "dst", "end")}
        s_aside, s_kept, s_sp_turn = ph.dma("dst_rows_set_aside"), ph.dma("dst_rows_back"), ph.sem("sync_goes_on")
        s_raw, s_rawd, s_put, s_turn = ph.dma("src_gathered"), ph.dma("dst_gathered"), ph.dma("rows_written"), ph.sem("pool_goes_on")
        s_hsT, s_hdT, s_hsc, s_hdc = (ph.sem(n) for n in ("hs_transposed", "hd_transposed", "hsT_ready", "hdT_ready"))
        s_logp, s_xp, s_lin, s_neg, s_log, s_both, s_top = (ph.sem(n) for n in (
            "logits_projected", "values_projected", "logits_evacuated", "resets_ready", "logits_ready", "logits_joined", "maximum_done"))
        s_diff, s_fall, s_exp, s_val, s_sums, s_num, s_den = (ph.sem(n) for n in (
            "logits_lowered", "fall_ready", "exps_done", "values_weighted", "sums_done", "numerator_ready", "denominator_ready"))
        s_own, s_lden, s_inv, s_mix, s_low, s_ex, s_part, s_elu = (ph.sem(n) for n in (
            "own_ready", "log_denominator", "reciprocal_ready", "mix_ready", "low_ready", "ex_ready", "part_ready", "elu_ready"))
        s_back, s_rows = ph.sem("elu_transposed"), ph.sem("rows_ready")
        norm_s = Norm(ph, k, "src", raw_s, s_raw, 64, k["eps"][:, :], s_hsT, 2)
        norm_d = Norm(ph, k, "dst", raw_d, s_rawd, 64, k["eps"][:, :], s_hdT, 2)

        with ph.block() as block:
            @block.sync
            def _(sp):
                for dst, src in ((wg[:, :], t["Wg"]), (wgT[:, :], t["WgT"]),
                                 (att[:, 0:1], t["att_src"].rearrange("a h c -> (h c) a")),
                                 (att[:, 1:2], t["att_dst"].rearrange("a h c -> (h c) a")), (bias[:, :], column(t["bias"]))):
                    sp.dma_start(dst, src).then_inc(s_w, 16)
                gathers, ends = edge_indices(sp, t, idx, s_idx, {"src": s_raw, "dst": s_rawd}, s_put)

                def set_aside(b):
                    sp.wait_ge(*this(s_rawd, b, 64))
                    sp.sem_inc(s_sp_turn, 1)
                    sp.dma_start(edge_rows(t["KEPT"], b), raw_d[b][:, :, :]).then_inc(s_aside[b], 16)

                def bring_back(b):
                    sp.wait_ge(*this(s_aside, b, 16))
                    sp.sem_inc(s_sp_turn, 1)
                    wait_freed(sp, *before(s_back, b, RING))
                    sp.sem_inc(s_sp_turn, 1)
                    sp.dma_start(kept_d[b][:, :, :], edge_rows(t["KEPT"], b)).then_inc(s_kept[b], 16)

                pipeline(sp, EB, [(0, gathers), (3, set_aside), (10, bring_back), (10, ends)])

            @block.gpsimd
            def _(pool):
                def gather_src(b):
                    pool.wait_ge(*this(s_idx["src"], b, 16))
                    wait_freed(pool, *before(norm_s.s_h, b, RING))
                    pool.sem_inc(s_turn, 1)
                    indexed_gather(pool, raw_s[b], t["X3"], idx["src"][b], s_raw[b], NT)

                def gather_dst(b):
                    pool.wait_ge(*this(s_idx["dst"], b, 16))
                    wait_freed(pool, *before(norm_d.s_h, b, RING))
                    wait_freed(pool, *before(s_aside, b, RING, 16))
                    pool.sem_inc(s_turn, 1)
                    indexed_gather(pool, raw_d[b], t["X3"], idx["dst"][b], s_rawd[b], NT)

                def scatter(b):
                    pool.wait_ge(*this(s_idx["end"], b, 16))
                    pool.wait_ge(*this(s_rows, b))
                    pool.sem_inc(s_turn, 1)
                    indexed_write(pool, t["out"], idx["end"][b], rows[b], s_put[b], N - 1)

                pipeline(pool, EB, [(0, gather_src), (11, scatter), (0, gather_dst)])
                wait_all(pool, s_put, EB, 64)

            @block.tensor
            def _(pe):
                pe.wait_ge(s_w, 80)
                pe.wait_ge(s_spread, 2)
                for n in range(2):
                    last = pe.matmul(p_e[:, n * D:(n + 1) * D], lhsT=wg[:, :], rhs=spread[:, n, :], start=True, stop=True)
                last.then_inc(s_wa, 1)
                pe.wait_ge(s_wac, 2)

                def rows_T(b):
                    for norm, p_h, s_t, s_c in ((norm_s, p_hs, s_hsT, s_hsc), (norm_d, p_hd, s_hdT, s_hdc)):
                        pe.wait_ge(*this(norm.s_h, b))
                        wait_freed(pe, *before(s_c, b, 1))
                        transpose_rows(pe, p_h, norm.h[b], ident, True).then_inc(s_t, 1)

                def project(b):
                    pe.wait_ge(*this(s_hsc, b))
                    pe.wait_ge(*this(s_hdc, b))
                    wait_freed(pe, *before(s_lin, b, 1))
                    pe.matmul(p_e[:, :], lhsT=wa[:, 0, :], rhs=hsT[b][:, :], start=True, stop=False)
                    pe.matmul(p_e[:, :], lhsT=wa[:, 1, :], rhs=hdT[b][:, :], start=False, stop=True)
                    pe.matmul(p_l[:, :], lhsT=wa_sum[:, :], rhs=hdT[b][:, :], start=True, stop=True).then_inc(s_logp, 1)

                def project_values(b):
                    wait_freed(pe, *before(s_own, b, 1))
                    pe.matmul(p_xs[:, :], lhsT=wgT[:, :], rhs=hsT[b][:, :], start=True, stop=True)
                    pe.matmul(p_xd[:, :], lhsT=wgT[:, :], rhs=hdT[b][:, :], start=True, stop=True).then_inc(s_xp, 1)

                def back(b):
                    pe.wait_ge(*this(s_elu, b))
                    wait_freed(pe, *before(s_rows, b, 1))
                    pe.wait_ge(*this(s_kept, b, 16))
                    for g in range(G):
                        o = p_back[:, g * P:(g + 1) * P]
                        pe.matmul(o, lhsT=elu_T[:, g:BLK:G], rhs=ident, start=True, stop=False)
                        last = pe.matmul(o, lhsT=ident, rhs=kept_d[b][:, g, :], start=False, stop=True)
                    last.then_inc(s_back, 1)

                pipeline(pe, EB, [(3, project), (2, rows_T), (8, back), (4, project_values)])

            @block.scalar
            def _(act):
                act.preload_act_table_set(LN_EXP)

                def rstd(b):
                    norm_s.scalar_log(act, b)
                    norm_d.scalar_log(act, b)
                    norm_s.scalar_rstd(act, b)
                    norm_d.scalar_rstd(act, b)

                def relu(b):
                    norm_s.scalar_relu(act, b)
                    norm_d.scalar_relu(act, b)

                def evac_h(b):
                    wait_freed(act, *before(s_xp, b, RING))
                    act.wait_ge(*this(s_hsT, b))
                    act.copy(hsT[b][:, :], p_hs[:, :]).then_inc(s_hsc, 1)
                    act.wait_ge(*this(s_hdT, b))
                    act.copy(hdT[b][:, :], p_hd[:, :]).then_inc(s_hdc, 1)

                def resets(b):
                    wait_freed(act, *before(s_fall, b, 2))
                    act.activation(neg[b][:, :], edge_cols(same, b), ACT.Copy, bias=-NEG, scale=NEG).then_inc(s_neg, 1)

                def evac_logits(b):
                    act.wait_ge(*this(s_logp, b))
                    wait_freed(act, *before(s_log, b, 2))
                    act.copy(lin[b][:, 0, :], p_e[:, :])
                    act.copy(lin[b][:, 1, :], p_l[:, :]).then_inc(s_lin, 1)

                def evac_rows(b):
                    act.wait_ge(*this(s_back, b))
                    wait_freed(act, *before(s_put, b, RING, 64))
                    act.copy(rows[b][:, :, :], grouped(p_back[:, :])).then_inc(s_rows, 1)

                def exps(b):
                    act.wait_ge(*this(s_diff, b))
                    wait_freed(act, *before(s_num, b, 2))
                    act.activation(weight[b][:, :, :], drop[b][:, :, :], ACT.Exp).then_inc(s_exp, 1)
                    act.wait_ge(*this(s_fall, b))
                    act.activation(keep[b][:, :], fall[b][:, :], ACT.Exp).then_inc(s_exp, 1)

                def inverse(b):
                    act.wait_ge(*this(s_den, b))
                    wait_freed(act, *before(s_inv, b, 1))
                    act.activation(lden[:, :], den[b][:, :], ACT.Ln).then_inc(s_lden, 1)
                    act.wait_ge(*this(s_lden, b))
                    wait_freed(act, *before(s_mix, b, 1))
                    act.activation(inv[:, :], lden[:, :], ACT.Exp, scale=-1.0).then_inc(s_inv, 1)

                def low_exp(b):
                    act.wait_ge(*this(s_mix, b))
                    wait_freed(act, *before(s_ex, b, 1))
                    act.activation(low[:, :], mix[b][:, :], ACT.Relu, bias=nbias[:, :], scale=-1.0).then_inc(s_low, 1)
                    wait_freed(act, *before(s_elu, b, 2))
                    act.activation(part[b][:, :], mix[b][:, :], ACT.Relu, bias=bias[:, :]).then_inc(s_part, 1)
                    act.wait_ge(*this(s_low, b))
                    act.activation(ex[b][:, :], low[:, :], ACT.Exp, scale=-1.0).then_inc(s_ex, 1)

                act.wait_ge(s_spread, 3)
                pipeline(act, EB, [(4, exps), (9, evac_rows), (6, inverse), (3, evac_logits), (7, low_exp),
                                   (1, relu), (2, evac_h), (2, resets), (0, rstd)])

            @block.vector
            def _(dve):
                for x in (wsum[1], vsum[1], top[0], top[1]):
                    dve.memset(x[:, :], 0.0)
                dve.wait_ge(s_w, 80)
                for n in range(2):
                    dve.tensor_scalar(spread[:, n, :], k["blocks32"], att[:, n:n + 1], None, ALU.mult).then_inc(s_spread, 1)
                dve.tensor_scalar(nbias[:, :], bias[:, :], -1.0, None, ALU.mult).then_inc(s_spread, 1)
                dve.wait_ge(s_wa, 1)
                dve.tensor_copy(wa[:, :, :], p_e[:, 0:2 * D].rearrange("p (n c) -> p n c", n=2)).then_inc(s_wac, 1)
                dve.wait_ge(s_wac, 1)
                dve.tensor_tensor(wa_sum[:, :], wa[:, 0, :], wa[:, 1, :], ALU.add).then_inc(s_wac, 1)
                dve.wait_ge(s_spread, 3)

                def row_stats(b):
                    norm_s.vector_stats(dve, b)
                    norm_d.vector_stats(dve, b)
                    norm_s.vector_aggregate(dve, b)
                    norm_d.vector_aggregate(dve, b)

                def shift(b):
                    norm_s.vector_shift(dve, b)
                    norm_d.vector_shift(dve, b)

                def logits(b):
                    dve.wait_ge(*this(s_lin, b))
                    wait_freed(dve, *before(s_diff, b, 1))
                    dve.scalar_tensor_tensor(log[:, :, :], lin[b][:, :, :], 0.2, lin[b][:, :, :], ALU.mult, ALU.max).then_inc(s_log, 1)
                    dve.wait_ge(*this(s_log, b))
                    wait_freed(dve, *before(s_top, b, 1))
                    dve.tensor_tensor(both[:, :], log[:, 0, :], log[:, 1, :], ALU.max).then_inc(s_both, 1)
                    dve.wait_ge(*this(s_both, b))
                    dve.wait_ge(*this(s_neg, b))
                    dve.tensor_tensor_scan(top[b][:, 1:BLK + 1], neg[b][:, :], both[:, :], top[b.back(1)][:, BLK:BLK + 1],
                                           ALU.add, ALU.max)
                    dve.tensor_copy(top[b][:, 0:1], top[b.back(1)][:, BLK:BLK + 1]).then_inc(s_top, 1)
                    dve.wait_ge(*this(s_top, b))
                    wait_freed(dve, *before(s_exp, b, 2, 2))
                    dve.tensor_tensor(drop[b][:, :, :], log[:, :, :], bc(top[b][:, 1:BLK + 1], 1, 2), ALU.subtract)
                    dve.tensor_tensor(fall[b][:, :], top[b][:, 0:BLK], top[b][:, 1:BLK + 1], ALU.subtract).then_inc(s_diff, 1)
                    dve.wait_ge(*this(s_diff, b))
                    dve.tensor_tensor(fall[b][:, :], fall[b][:, :], neg[b][:, :], ALU.add).then_inc(s_fall, 1)

                def sums(b):
                    dve.wait_ge(*this(s_xp, b))
                    dve.wait_ge(*this(s_exp, b, 2))
                    wait_freed(dve, *before(s_num, b, 1))
                    dve.tensor_tensor(value[:, :], p_xs[:, :], weight[b][:, 0, :], ALU.mult).then_inc(s_val, 1)
                    dve.tensor_tensor_scan(wsum[b][:, :], keep[b][:, :], weight[b][:, 0, :], wsum[b.back(1)][:, BLK - 1:BLK], ALU.mult, ALU.add)
                    dve.tensor_tensor(own[:, :], p_xd[:, :], weight[b][:, 1, :], ALU.mult).then_inc(s_own, 1)
                    dve.wait_ge(*this(s_val, b))
                    dve.tensor_tensor_scan(vsum[b][:, :], keep[b][:, :], value[:, :], vsum[b.back(1)][:, BLK - 1:BLK],
                                           ALU.mult, ALU.add).then_inc(s_sums, 1)
                    dve.wait_ge(*this(s_sums, b))
                    wait_freed(dve, *before(s_lden, b, 2))
                    dve.scalar_tensor_tensor(den[b][:, :], wsum[b][:, :], 1e-16, weight[b][:, 1, :], ALU.add, ALU.add).then_inc(s_den, 1)
                    wait_freed(dve, *before(s_mix, b, 2))
                    dve.tensor_tensor(num[b][:, :], vsum[b][:, :], own[:, :], ALU.add).then_inc(s_num, 1)

                def output(b):
                    dve.wait_ge(*this(s_inv, b))
                    dve.wait_ge(*this(s_num, b))
                    wait_freed(dve, *before(s_ex, b, 2))
                    dve.tensor_tensor(mix[b][:, :], num[b][:, :], inv[:, :], ALU.mult).then_inc(s_mix, 1)

                def elu(b):
                    dve.wait_ge(*this(s_part, b))
                    dve.wait_ge(*this(s_ex, b))
                    wait_freed(dve, *before(s_back, b, 1))
                    dve.scalar_tensor_tensor(elu_T[:, :], ex[b][:, :], -1.0, part[b][:, :], ALU.add, ALU.add).then_inc(s_elu, 1)

                pipeline(dve, EB, [(8, elu), (5, sums), (1, shift), (3, logits), (0, row_stats), (6, output)])


INPUTS = {
    "x": ("x", (N, D)), "A1": ("L0_gnn_A1", (8, 64)), "b1_0": ("L0_gnn_b1", (64,)), "A2": ("L0_gnn_A2", (64, 64)),
    "b2_0": ("L0_gnn_b2", (64,)), "A3": ("L0_gnn_A3", (64, D)), "W_up_s": ("L0_gnn_W_up_s", (MUL, MUL)),
    "W_up_v": ("L0_gnn_W_up_v", (MUL, MUL)), "W_out_s": ("L0_gnn_W_out_s", (2 * MUL, MUL)),
    "W_out_v": ("L0_gnn_W_out_v", (2 * MUL, MUL)), "Wq": ("L1_gnn_Wq", (D, D)), "Wk": ("L1_gnn_Wk", (D, D)),
    "Wv": ("L1_gnn_Wv", (D, D)), "Wo": ("L1_gnn_Wo", (D, D)), "bo": ("L1_gnn_bo", (D,)), "g1": ("L1_gnn_bn1_g", (D,)),
    "b1": ("L1_gnn_bn1_b", (D,)), "g2": ("L1_gnn_bn2_g", (D,)), "b2": ("L1_gnn_bn2_b", (D,)), "W1": ("L1_gnn_W1", (D, 2 * D)),
    "bf1": ("L1_gnn_b1", (2 * D,)), "W2": ("L1_gnn_W2", (2 * D, D)), "bf2": ("L1_gnn_b2", (D,)),
    "w0": ("L2_gnn_w0", (MUL, 1, MUL)), "w1": ("L2_gnn_w1", (MUL, 1, MUL)), "w2": ("L2_gnn_w2", (MUL, 1, MUL)),
    "w3": ("L2_gnn_w3", (MUL, 1, MUL)), "w4": ("L2_gnn_w4", (MUL, 1, MUL)), "Wg": ("L3_gnn_W", (D, D)),
    "att_src": ("L3_gnn_att_src", (1, HEADS3, D // HEADS3)), "att_dst": ("L3_gnn_att_dst", (1, HEADS3, D // HEADS3)),
    "bias": ("L3_gnn_bias", (D,)),
}


def build(nc, t, phases=None):
    with ExitStack() as ctx:
        def sb(name, shape, dt=F32):
            return ctx.enter_context(nc.sbuf_tensor(name, shape, dt))

        const, coef, eps = sb("const", [P, 3 * P]), sb("coef", [9, COEF]), sb("eps", [P, 1])
        k = {"const": const, "coef": coef, "eps": eps, "same": sb("same", [P, EP + 4], U8),
             "ident": const[:, 0:P], "blocks16": const[:, P:2 * P], "blocks32": const[:, 2 * P:3 * P],
             "node_stats": sb("node_stats", [P, NB, 6]), "node_mv": sb("node_mv", [P, 2]),
             "moved": sb("moved", [P, 2, EB])}
        for phase in (setup, layer0, stats, layer1, nodes, layer2, layer3)[:phases]:
            phase(nc, t, k)


def laid_out(inputs):
    arrays = {name: np.ascontiguousarray(inputs[key]) for name, (key, _) in INPUTS.items()}
    src, dst = np.asarray(inputs["src"]), np.asarray(inputs["dst"])
    tail = EP - E

    def by_partition(a):
        return np.ascontiguousarray(a.reshape(EB, P, G).transpose(1, 0, 2).reshape(P, EB * G))

    ext = np.concatenate([np.full(1, -1, dst.dtype), dst, np.full(tail, N, dst.dtype), np.full(1, N + 1, dst.dtype)])
    arrays["dst_ext"] = ext
    arrays["src_rows"] = by_partition(np.concatenate([src, np.zeros(tail, src.dtype)]))
    arrays["dst_rows"] = by_partition(ext[1:EP + 1])
    arrays["next_rows"] = by_partition(ext[2:EP + 2])

    def padded(a):
        a = np.asarray(a)
        return np.concatenate([a, np.zeros((tail, a.shape[1]), a.dtype)])

    arrays["edge4"] = padded(inputs["edge_attr_4"])
    arrays["edge8T"] = np.ascontiguousarray(
        padded(inputs["edge_attr_8"]).reshape(EB // 2, 2, BLK, 8).transpose(1, 3, 0, 2).reshape(16, EP // 2))
    arrays["edge9T"] = np.ascontiguousarray(padded(inputs["edge_attr_9"]).T)
    arrays["WgT"] = np.ascontiguousarray(np.asarray(inputs["L3_gnn_W"]).T)
    arrays["shape_constants"] = shape_constants()
    arrays["trash_rows"] = trash_rows()
    arrays["coefficients"] = coefficient_matrix()
    return arrays


def make(nc, arrays, phases=None, debug=False):
    t = {name: nc.dram_tensor(f"in_{name}", a.shape, mybir.dt.from_np(a.dtype), kind="ExternalInput").ap()
         for name, a in arrays.items()}
    kind = "ExternalOutput" if debug else "Internal"
    for name, rows, cols, dt in (("X1", NT, D, F32), ("H2", NT, D, F32), ("X2", N, D, F32), ("X3", NT, D, F32),
                                 ("TPW", EP, D, F32), ("KEPT", EP, D, F32), ("XS", EP, D, F32), ("XD", EP, D, F32),
                                 ("INDEX", EB * P, 3 * G, I32)):
        t[name] = nc.dram_tensor(name, (rows, cols), dt, kind=kind).ap()
    t["out"] = nc.dram_tensor("out_0", (N, D), F32, kind="ExternalOutput").ap()
    build(nc, t, phases)


def kernel(**inputs):
    import concourse.bacc as bacc
    from concourse.bass_utils import run_bass_kernel_spmd

    nc = bacc.Bacc("TRN2", target_bir_lowering=False, num_devices=1)
    arrays = laid_out(inputs)
    make(nc, arrays)
    result = run_bass_kernel_spmd(nc, [{f"in_{name}": a for name, a in arrays.items()}], core_ids=[0])
    return result.results[0]["out_0"]
```
